# Optimizing a Trainium2 kernel written in Bass

```python
import numpy as np
import jax
import jax.numpy as jnp

def _softmax(x, axis=-1):
    return jax.nn.softmax(x, axis=axis)
def _gelu(x):
    return jax.nn.gelu(x, approximate=True)
def _silu(x):
    return jax.nn.silu(x)
def _sigmoid(x):
    return jax.nn.sigmoid(x)
def _layernorm(x, axis=-1, eps=1e-5):
    m = jnp.mean(x, axis=axis, keepdims=True)
    v = jnp.var(x, axis=axis, keepdims=True)
    return (x - m) / jnp.sqrt(v + eps)
def _scatter_add(tgt, idx, src, axis=0):
    return tgt.at[idx].add(src)
def _segment_sum(src, seg, n):
    return jax.ops.segment_sum(src, seg, n)

kernel_name = 'mk_conv_preact_d2_conv_nchw32_24a45d'

def setup_inputs(seed: int = 0):
    np.random.seed(seed)
    _w = jnp.asarray
    def _rec_inputs():
        import jax
        import jax.numpy as jnp
        _gk = jax.random.key(seed)
        x = -0.000125 + 0.9999 * jax.random.normal(jax.random.fold_in(_gk, 1), (16, 32, 256, 256), jnp.float32)
        return x
    x = _rec_inputs()
    def _L0_conv_setup():
        import jax, jax.numpy as jnp
        import numpy as np
        B, CI, CO, H, W, M1, M2 = (16, 32, 32, 256, 256, 32, 32)

        def dht2d(x):
            for ax in (-2, -1):
                F = jnp.fft.fft(x, axis=ax)
                x = F.real - F.imag
            return x

        def flip_periodic(x):
            for ax in (2, 3):
                n = x.shape[ax]
                idx = -jnp.arange(n) % n
                x = jnp.take(x, idx, axis=ax)
            return x
        key = jax.random.key(seed)
        k1, k2 = jax.random.split(key)
        x = jax.random.normal(k1, (B, CI, H, W), dtype=jnp.float32)
        scale = 1.0 / (CI * CO)
        weights1 = scale * jax.random.uniform(k2, (CI, CO, M1, M2), dtype=jnp.float32)
        return {'x': x, 'weights1': weights1}
    _L0_conv_all = _L0_conv_setup()
    _L0_conv_in = {k: v for k, v in _L0_conv_all.items() if k in ('weights1', )}
    del _L0_conv_all

    def _L1_conv_setup():
        import jax, jax.numpy as jnp
        import numpy as np
        B, C, O, H, W, M1, M2, HD = (4, 32, 32, 256, 256, 32, 32, 64)

        def _gelu(x):
            return jax.nn.gelu(x, approximate=False)

        def _cmlp(inp, w0, b0, w1, b1, w2, b2):
            h = _gelu(inp @ w0 + b0)
            h = _gelu(h @ w1 + b1)
            o = h @ w2 + b2
            m = o.shape[-1] // 2
            return jax.lax.complex(o[..., :m], o[..., m:])

        def _forward(x, bw0_w, bw0_b, bw1_w, bw1_b, bw2_w, bw2_b, bh0_w, bh0_b, bh1_w, bh1_b, bh2_w, bh2_b, hi0_w, hi0_b, hi1_w, hi1_b, hi2_w, hi2_b, wi0_w, wi0_b, wi1_w, wi1_b, wi2_w, wi2_b, comp_h_w, comp_h_b, comp_w_w, comp_w_b, wf_real, wf_imag, mixer_w, mixer_b, sc_w, sc_b, ln_g, ln_b):
            b, c, h, w = x.shape
            o = mixer_b.shape[0]
            hc = jnp.linspace(-1.0, 1.0, h)
            wc = jnp.linspace(-1.0, 1.0, w)
            xp = jnp.transpose(x, (0, 2, 3, 1))
            wcoord = jnp.broadcast_to(wc[None, None, :, None], (b, h, w, 1))
            b_w = _cmlp(jnp.concatenate([xp, wcoord], -1), bw0_w, bw0_b, bw1_w, bw1_b, bw2_w, bw2_b)
            x_w = jnp.einsum('bchw,bhwm->bchm', x.astype(b_w.dtype), b_w)
            hcoord = jnp.broadcast_to(hc[None, None, :, None], (b, M2, h, 1))
            mlp_h_in = jnp.concatenate([jnp.transpose(x_w.real, (0, 3, 2, 1)), hcoord], -1)
            b_h = _cmlp(mlp_h_in, bh0_w, bh0_b, bh1_w, bh1_b, bh2_w, bh2_b)
            x_hw = jnp.einsum('bchm,bmhk->bckm', x_w, b_h)
            wf = jax.lax.complex(wf_real, wf_imag)
            xf = jnp.einsum('bikm,oikm->bokm', x_hw, wf)
            xf_ri = jnp.concatenate([xf.real, xf.imag], axis=1)
            ch = jnp.einsum('bokm,k->bom', xf_ri, comp_h_w) + comp_h_b[0]
            cond_h = jnp.broadcast_to(jnp.transpose(ch, (0, 2, 1))[:, :, None, :], (b, M2, h, 2 * o))
            b_h_inv = _cmlp(jnp.concatenate([hcoord, cond_h], -1), hi0_w, hi0_b, hi1_w, hi1_b, hi2_w, hi2_b)
            x_h_rec = jnp.einsum('bokm,bmhk->bohm', xf, jnp.conj(b_h_inv))
            xr_ri = jnp.concatenate([x_h_rec.real, x_h_rec.imag], axis=1)
            cw = jnp.einsum('bohm,m->boh', xr_ri, comp_w_w) + comp_w_b[0]
            cond_w = jnp.broadcast_to(jnp.transpose(cw, (0, 2, 1))[:, :, None, :], (b, h, w, 2 * o))
            b_w_inv = _cmlp(jnp.concatenate([wcoord, cond_w], -1), wi0_w, wi0_b, wi1_w, wi1_b, wi2_w, wi2_b)
            x_rec = jnp.einsum('bohm,bhwm->bohw', x_h_rec, jnp.conj(b_w_inv)).real * (1.0 / (h * w))
            y = jnp.einsum('bihw,oi->bohw', x_rec, mixer_w) + mixer_b[None, :, None, None]
            mu = jnp.mean(y, axis=1, keepdims=True)
            var = jnp.var(y, axis=1, keepdims=True)
            y = (y - mu) / jnp.sqrt(var + 1e-05) * ln_g[None, :, None, None] + ln_b[None, :, None, None]
            y = _gelu(y)
            sc = jnp.einsum('bchw,oc->bohw', x, sc_w) + sc_b[None, :, None, None]
            return _gelu(y + sc)
        keys = iter(jax.random.split(jax.random.key(seed), 80))

        def lin(i, o):
            w = jax.random.normal(next(keys), (i, o), jnp.float32) / np.sqrt(i).astype(np.float32)
            b = jax.random.normal(next(keys), (o,), jnp.float32) * 0.01
            return (w, b)
        d = {}
        d['x'] = jax.random.normal(next(keys), (B, C, H, W), jnp.float32)
        for pfx, i, o in [('bw', C + 1, 2 * M2), ('bh', C + 1, 2 * M1), ('hi', 1 + 2 * O, 2 * M1), ('wi', 1 + 2 * O, 2 * M2)]:
            d[pfx + '0_w'], d[pfx + '0_b'] = lin(i, HD)
            d[pfx + '1_w'], d[pfx + '1_b'] = lin(HD, HD)
            d[pfx + '2_w'], d[pfx + '2_b'] = lin(HD, o)
        d['comp_h_w'] = jax.random.normal(next(keys), (M1,), jnp.float32) / np.sqrt(M1).astype(np.float32)
        d['comp_h_b'] = jax.random.normal(next(keys), (1,), jnp.float32) * 0.01
        d['comp_w_w'] = jax.random.normal(next(keys), (M2,), jnp.float32) / np.sqrt(M2).astype(np.float32)
        d['comp_w_b'] = jax.random.normal(next(keys), (1,), jnp.float32) * 0.01
        d['wf_real'] = jax.random.normal(next(keys), (C, O, M1, M2), jnp.float32) * 0.1
        d['wf_imag'] = jax.random.normal(next(keys), (C, O, M1, M2), jnp.float32) * 0.1
        d['mixer_w'] = jax.random.normal(next(keys), (O, O), jnp.float32) / np.sqrt(O).astype(np.float32)
        d['mixer_b'] = jax.random.normal(next(keys), (O,), jnp.float32) * 0.01
        d['sc_w'] = jax.random.normal(next(keys), (O, C), jnp.float32) / np.sqrt(C).astype(np.float32)
        d['sc_b'] = jax.random.normal(next(keys), (O,), jnp.float32) * 0.01
        d['ln_g'] = jnp.ones((O,), jnp.float32)
        d['ln_b'] = jnp.zeros((O,), jnp.float32)
        return d
    _L1_conv_all = _L1_conv_setup()
    _L1_conv_in = {k: v for k, v in _L1_conv_all.items() if k in ('bw0_w', 'bw0_b', 'bw1_w', 'bw1_b', 'bw2_w', 'bw2_b', 'bh0_w', 'bh0_b', 'bh1_w', 'bh1_b', 'bh2_w', 'bh2_b', 'hi0_w', 'hi0_b', 'hi1_w', 'hi1_b', 'hi2_w', 'hi2_b', 'wi0_w', 'wi0_b', 'wi1_w', 'wi1_b', 'wi2_w', 'wi2_b', 'comp_h_w', 'comp_h_b', 'comp_w_w', 'comp_w_b', 'wf_real', 'wf_imag', 'mixer_w', 'mixer_b', 'sc_w', 'sc_b', 'ln_g', 'ln_b', )}
    del _L1_conv_all

    return {
        "x": x,
        "L0_conv_weights1": _L0_conv_in["weights1"],
        "L1_conv_bw0_w": _L1_conv_in["bw0_w"],
        "L1_conv_bw0_b": _L1_conv_in["bw0_b"],
        "L1_conv_bw1_w": _L1_conv_in["bw1_w"],
        "L1_conv_bw1_b": _L1_conv_in["bw1_b"],
        "L1_conv_bw2_w": _L1_conv_in["bw2_w"],
        "L1_conv_bw2_b": _L1_conv_in["bw2_b"],
        "L1_conv_bh0_w": _L1_conv_in["bh0_w"],
        "L1_conv_bh0_b": _L1_conv_in["bh0_b"],
        "L1_conv_bh1_w": _L1_conv_in["bh1_w"],
        "L1_conv_bh1_b": _L1_conv_in["bh1_b"],
        "L1_conv_bh2_w": _L1_conv_in["bh2_w"],
        "L1_conv_bh2_b": _L1_conv_in["bh2_b"],
        "L1_conv_hi0_w": _L1_conv_in["hi0_w"],
        "L1_conv_hi0_b": _L1_conv_in["hi0_b"],
        "L1_conv_hi1_w": _L1_conv_in["hi1_w"],
        "L1_conv_hi1_b": _L1_conv_in["hi1_b"],
        "L1_conv_hi2_w": _L1_conv_in["hi2_w"],
        "L1_conv_hi2_b": _L1_conv_in["hi2_b"],
        "L1_conv_wi0_w": _L1_conv_in["wi0_w"],
        "L1_conv_wi0_b": _L1_conv_in["wi0_b"],
        "L1_conv_wi1_w": _L1_conv_in["wi1_w"],
        "L1_conv_wi1_b": _L1_conv_in["wi1_b"],
        "L1_conv_wi2_w": _L1_conv_in["wi2_w"],
        "L1_conv_wi2_b": _L1_conv_in["wi2_b"],
        "L1_conv_comp_h_w": _L1_conv_in["comp_h_w"],
        "L1_conv_comp_h_b": _L1_conv_in["comp_h_b"],
        "L1_conv_comp_w_w": _L1_conv_in["comp_w_w"],
        "L1_conv_comp_w_b": _L1_conv_in["comp_w_b"],
        "L1_conv_wf_real": _L1_conv_in["wf_real"],
        "L1_conv_wf_imag": _L1_conv_in["wf_imag"],
        "L1_conv_mixer_w": _L1_conv_in["mixer_w"],
        "L1_conv_mixer_b": _L1_conv_in["mixer_b"],
        "L1_conv_sc_w": _L1_conv_in["sc_w"],
        "L1_conv_sc_b": _L1_conv_in["sc_b"],
        "L1_conv_ln_g": _L1_conv_in["ln_g"],
        "L1_conv_ln_b": _L1_conv_in["ln_b"],
    }

def reference(x, L0_conv_weights1, L1_conv_bw0_w, L1_conv_bw0_b, L1_conv_bw1_w, L1_conv_bw1_b, L1_conv_bw2_w, L1_conv_bw2_b, L1_conv_bh0_w, L1_conv_bh0_b, L1_conv_bh1_w, L1_conv_bh1_b, L1_conv_bh2_w, L1_conv_bh2_b, L1_conv_hi0_w, L1_conv_hi0_b, L1_conv_hi1_w, L1_conv_hi1_b, L1_conv_hi2_w, L1_conv_hi2_b, L1_conv_wi0_w, L1_conv_wi0_b, L1_conv_wi1_w, L1_conv_wi1_b, L1_conv_wi2_w, L1_conv_wi2_b, L1_conv_comp_h_w, L1_conv_comp_h_b, L1_conv_comp_w_w, L1_conv_comp_w_b, L1_conv_wf_real, L1_conv_wf_imag, L1_conv_mixer_w, L1_conv_mixer_b, L1_conv_sc_w, L1_conv_sc_b, L1_conv_ln_g, L1_conv_ln_b):
    import jax
    import jax.numpy as jnp
    def _L0_conv_ref(x, weights1):
        import jax, jax.numpy as jnp
        import numpy as np
        B, CI, CO, H, W, M1, M2 = (16, 32, 32, 256, 256, 32, 32)

        def dht2d(x):
            for ax in (-2, -1):
                F = jnp.fft.fft(x, axis=ax)
                x = F.real - F.imag
            return x

        def flip_periodic(x):
            for ax in (2, 3):
                n = x.shape[ax]
                idx = -jnp.arange(n) % n
                x = jnp.take(x, idx, axis=ax)
            return x
        b, ci, h, w = x.shape
        co, m1, m2 = (weights1.shape[1], weights1.shape[2], weights1.shape[3])
        x_ht = dht2d(x)
        xm = x_ht[:, :, :m1, :m2]
        wflip = flip_periodic(weights1)
        yeven = 0.5 * (weights1 + wflip)
        yodd = 0.5 * (weights1 - wflip)
        xflip = flip_periodic(xm)
        z = jnp.einsum('bixy,ioxy->boxy', xm, yeven) + jnp.einsum('bixy,ioxy->boxy', xflip, yodd)
        out_ht = jnp.zeros((b, co, h, w), dtype=x.dtype).at[:, :, :m1, :m2].set(z)
        return dht2d(out_ht) / (h * w)

    def _L1_conv_ref(x, bw0_w, bw0_b, bw1_w, bw1_b, bw2_w, bw2_b, bh0_w, bh0_b, bh1_w, bh1_b, bh2_w, bh2_b, hi0_w, hi0_b, hi1_w, hi1_b, hi2_w, hi2_b, wi0_w, wi0_b, wi1_w, wi1_b, wi2_w, wi2_b, comp_h_w, comp_h_b, comp_w_w, comp_w_b, wf_real, wf_imag, mixer_w, mixer_b, sc_w, sc_b, ln_g, ln_b):
        import jax, jax.numpy as jnp
        import numpy as np
        B, C, O, H, W, M1, M2, HD = (4, 32, 32, 256, 256, 32, 32, 64)

        def _gelu(x):
            return jax.nn.gelu(x, approximate=False)

        def _cmlp(inp, w0, b0, w1, b1, w2, b2):
            h = _gelu(inp @ w0 + b0)
            h = _gelu(h @ w1 + b1)
            o = h @ w2 + b2
            m = o.shape[-1] // 2
            return jax.lax.complex(o[..., :m], o[..., m:])

        def _forward(x, bw0_w, bw0_b, bw1_w, bw1_b, bw2_w, bw2_b, bh0_w, bh0_b, bh1_w, bh1_b, bh2_w, bh2_b, hi0_w, hi0_b, hi1_w, hi1_b, hi2_w, hi2_b, wi0_w, wi0_b, wi1_w, wi1_b, wi2_w, wi2_b, comp_h_w, comp_h_b, comp_w_w, comp_w_b, wf_real, wf_imag, mixer_w, mixer_b, sc_w, sc_b, ln_g, ln_b):
            b, c, h, w = x.shape
            o = mixer_b.shape[0]
            hc = jnp.linspace(-1.0, 1.0, h)
            wc = jnp.linspace(-1.0, 1.0, w)
            xp = jnp.transpose(x, (0, 2, 3, 1))
            wcoord = jnp.broadcast_to(wc[None, None, :, None], (b, h, w, 1))
            b_w = _cmlp(jnp.concatenate([xp, wcoord], -1), bw0_w, bw0_b, bw1_w, bw1_b, bw2_w, bw2_b)
            x_w = jnp.einsum('bchw,bhwm->bchm', x.astype(b_w.dtype), b_w)
            hcoord = jnp.broadcast_to(hc[None, None, :, None], (b, M2, h, 1))
            mlp_h_in = jnp.concatenate([jnp.transpose(x_w.real, (0, 3, 2, 1)), hcoord], -1)
            b_h = _cmlp(mlp_h_in, bh0_w, bh0_b, bh1_w, bh1_b, bh2_w, bh2_b)
            x_hw = jnp.einsum('bchm,bmhk->bckm', x_w, b_h)
            wf = jax.lax.complex(wf_real, wf_imag)
            xf = jnp.einsum('bikm,oikm->bokm', x_hw, wf)
            xf_ri = jnp.concatenate([xf.real, xf.imag], axis=1)
            ch = jnp.einsum('bokm,k->bom', xf_ri, comp_h_w) + comp_h_b[0]
            cond_h = jnp.broadcast_to(jnp.transpose(ch, (0, 2, 1))[:, :, None, :], (b, M2, h, 2 * o))
            b_h_inv = _cmlp(jnp.concatenate([hcoord, cond_h], -1), hi0_w, hi0_b, hi1_w, hi1_b, hi2_w, hi2_b)
            x_h_rec = jnp.einsum('bokm,bmhk->bohm', xf, jnp.conj(b_h_inv))
            xr_ri = jnp.concatenate([x_h_rec.real, x_h_rec.imag], axis=1)
            cw = jnp.einsum('bohm,m->boh', xr_ri, comp_w_w) + comp_w_b[0]
            cond_w = jnp.broadcast_to(jnp.transpose(cw, (0, 2, 1))[:, :, None, :], (b, h, w, 2 * o))
            b_w_inv = _cmlp(jnp.concatenate([wcoord, cond_w], -1), wi0_w, wi0_b, wi1_w, wi1_b, wi2_w, wi2_b)
            x_rec = jnp.einsum('bohm,bhwm->bohw', x_h_rec, jnp.conj(b_w_inv)).real * (1.0 / (h * w))
            y = jnp.einsum('bihw,oi->bohw', x_rec, mixer_w) + mixer_b[None, :, None, None]
            mu = jnp.mean(y, axis=1, keepdims=True)
            var = jnp.var(y, axis=1, keepdims=True)
            y = (y - mu) / jnp.sqrt(var + 1e-05) * ln_g[None, :, None, None] + ln_b[None, :, None, None]
            y = _gelu(y)
            sc = jnp.einsum('bchw,oc->bohw', x, sc_w) + sc_b[None, :, None, None]
            return _gelu(y + sc)
        return _forward(x, bw0_w, bw0_b, bw1_w, bw1_b, bw2_w, bw2_b, bh0_w, bh0_b, bh1_w, bh1_b, bh2_w, bh2_b, hi0_w, hi0_b, hi1_w, hi1_b, hi2_w, hi2_b, wi0_w, wi0_b, wi1_w, wi1_b, wi2_w, wi2_b, comp_h_w, comp_h_b, comp_w_w, comp_w_b, wf_real, wf_imag, mixer_w, mixer_b, sc_w, sc_b, ln_g, ln_b)

    def _gn(v, G=16, eps=1e-5):
        B_, C_, H_, W_ = v.shape
        g = v.reshape(B_, G, C_ // G, H_, W_)
        m = jnp.mean(g, axis=(2, 3, 4), keepdims=True)
        s = jnp.var(g, axis=(2, 3, 4), keepdims=True)
        return ((g - m) / jnp.sqrt(s + eps)).reshape(v.shape)

    def _ln_c(v, eps=1e-6):
        m = jnp.mean(v, axis=1, keepdims=True)
        s = jnp.var(v, axis=1, keepdims=True)
        return (v - m) / jnp.sqrt(s + eps)

    def _ln_t(v, eps=1e-5):
        m = jnp.mean(v, axis=-1, keepdims=True)
        s = jnp.var(v, axis=-1, keepdims=True)
        return (v - m) / jnp.sqrt(s + eps)

    def _to_tokens(v):
        B_, C_, H_, W_ = v.shape
        return v.reshape(B_, C_, H_ * W_).transpose(0, 2, 1)
    def _from_tokens(t, like):
        B_, C_, H_, W_ = like.shape
        return t.transpose(0, 2, 1).reshape(B_, C_, H_, W_)

    x = x + _L0_conv_ref(_gn(x), L0_conv_weights1)
    x = x + _L1_conv_ref(_gn(x), L1_conv_bw0_w, L1_conv_bw0_b, L1_conv_bw1_w, L1_conv_bw1_b, L1_conv_bw2_w, L1_conv_bw2_b, L1_conv_bh0_w, L1_conv_bh0_b, L1_conv_bh1_w, L1_conv_bh1_b, L1_conv_bh2_w, L1_conv_bh2_b, L1_conv_hi0_w, L1_conv_hi0_b, L1_conv_hi1_w, L1_conv_hi1_b, L1_conv_hi2_w, L1_conv_hi2_b, L1_conv_wi0_w, L1_conv_wi0_b, L1_conv_wi1_w, L1_conv_wi1_b, L1_conv_wi2_w, L1_conv_wi2_b, L1_conv_comp_h_w, L1_conv_comp_h_b, L1_conv_comp_w_w, L1_conv_comp_w_b, L1_conv_wf_real, L1_conv_wf_imag, L1_conv_mixer_w, L1_conv_mixer_b, L1_conv_sc_w, L1_conv_sc_b, L1_conv_ln_g, L1_conv_ln_b)
    return x


_drawn_inputs = setup_inputs


def setup_inputs(seed=0):
    import zlib

    import numpy as np

    out = dict(_drawn_inputs(seed))
    spreads = {'L1_conv_ln_g': (1.0, 0.2), 'L1_conv_ln_b': (0.0, 0.1)}
    factors = {'L0_conv_weights1': 200.0,
     'L1_conv_bw0_b': 7.457,
     'L1_conv_bw1_b': 4.833,
     'L1_conv_bw2_b': 45.527,
     'L1_conv_bh0_b': 64.0,
     'L1_conv_bh1_b': 64.0,
     'L1_conv_bh2_b': 51.24,
     'L1_conv_hi0_b': 200.0,
     'L1_conv_hi1_b': 200.0,
     'L1_conv_hi2_b': 200.0,
     'L1_conv_sc_b': 8.0}
    for name, (base, spread) in spreads.items():
        noise = np.random.default_rng([zlib.crc32(name.encode()), seed]).standard_normal(out[name].shape)
        drawn = base * np.exp(spread * noise) if base else spread * noise
        out[name] = jnp.asarray(drawn.astype(out[name].dtype))
    for name, factor in factors.items():
        out[name] = (out[name] * factor).astype(out[name].dtype)
    return out
```

```python
import numpy as np
import concourse.bass as bass
from concourse import mybir
from contextlib import ExitStack

F32 = mybir.dt.float32
BF16 = mybir.dt.bfloat16
I32 = mybir.dt.int32
ACT = mybir.ActivationFunctionType
ALU = mybir.AluOpType
AX = mybir.AxisListType

C, H, W, M, HID = 32, 256, 256, 32, 64
P = 128
NPX = H * W
HP = 64
ROWS = 2
CHUNK = 4
STEPS = 4
ITERS = HP // (ROWS * STEPS)
PRIME = 12
MAGIC = 1597463007.0


def done(step):
    return step + 1 + PRIME


class Kit:

    def __init__(self, nc, ctx, a, out):
        self.nc, self.ctx, self.a, self.out = nc, ctx, a, out
        self.B = a["x"].shape[0]
        self.t = {}

    def sb(self, name, shape, dt=F32, ctx=None):
        t = (ctx or self.ctx).enter_context(self.nc.sbuf_tensor(name, shape, dt))
        self.t[name] = t
        return t

    def ps(self, name, ctx, shape=(P, 512)):
        return ctx.enter_context(self.nc.psum_tensor(name, list(shape), F32))

    def sem(self, name):
        return self.ctx.enter_context(self.nc.semaphore(name))


def prime(eng, *sems):
    for s in sems:
        eng.sem_inc(s, PRIME)


class Chain:

    def __init__(self, eng, sem):
        self.eng, self.sem, self.n = eng, sem, 0

    def __call__(self, ins):
        ins.then_inc(self.sem, 1)
        self.n += 1
        self.eng.wait_ge(self.sem, self.n)


def rsqrt_chain(v, link, y, x, t):
    link(v.tensor_scalar(y.bitcast(I32), x.bitcast(I32), -0.5, MAGIC, ALU.mult, ALU.add))
    for _ in range(3):
        link(v.tensor_tensor(t, y, y, ALU.mult))
        link(v.tensor_tensor(t, t, x, ALU.mult))
        link(v.tensor_scalar(t, t, -0.5, 1.5, ALU.mult, ALU.add))
        link(v.tensor_tensor(y, y, t, ALU.mult))


TABLES = {
    "cas_n": (P, 2, 3 * M), "cas_k": (M, W), "cas_bd": (P, 4 * H), "ident": (P, P),
    "chan_mask": (P, 16), "group_avg": (P, P), "ones_avg": (P, P),
    "bw0": (P, 2, P), "bh0": (P, 2, P), "bw1": (P, P), "bh1": (P, P), "hi1": (P, P), "wi1": (P, P),
    "bw0_b": (P, 1), "bh0_b": (P, 1), "hi1_b": (P, 1), "wi1_b": (P, 1), "hi0_b": (P, 1), "wi0_b": (P, 1),
    "bw2": (P, HID), "bw2_b": (P, HID), "bh2": (HID + 1, 2, 2 * M),
    "cond_h": (2 * M, 4), "comp_h_b": (C, 1), "hi0": (C, 2, HID), "hi0_c": (P, 1), "hc_row": (P, H),
    "hi2": (2 * M, 2, HID), "wi0": (P, HID), "wi0_c": (P, 1), "wc_row": (P, W), "comp_w": (P, 16),
    "wi0_sum": (2 * C, P), "comp_w_b": (2 * C, 1), "mixer": (P, C), "mixer_b": (P, C), "mixer_own": (P, 1),
    "wi2_b": (P, 16), "wi2": (P, P), "lane_avg": (P, 4), "sc": (P, P), "sc_b": (P, 1), "ln_g": (P, 1), "ln_b": (P, 1),
}


def split_rows(v, link, parts, src, tmp):
    link(v.tensor_copy(parts[0], src))
    link(v.tensor_tensor(tmp, src, parts[0], ALU.subtract))
    link(v.tensor_copy(parts[1], tmp))
    link(v.tensor_tensor(tmp, tmp, parts[1], ALU.subtract))
    link(v.tensor_copy(parts[2], tmp))


def setup(k):
    nc, a = k.nc, k.a
    loaded, chain, placed = k.sem("tables_loaded"), k.sem("setup_chain"), k.sem("rows_placed")
    for name, shape in TABLES.items():
        k.sb(name, list(shape))
    t = k.t
    mix_c = k.sb("mix_c", [P, C])
    mix_bd = k.sb("mix_bd", [P, P])
    cond_y_w = k.sb("cond_y_w", [P, 16, HID + C])
    wi0_const = k.sb("wi0_const", [P, 1])
    y_const = k.sb("y_const", [P, 1])
    coord_w = k.sb("coord_w", [9, P], BF16)
    coord_wc = k.sb("coord_wc", [9, ROWS * W], BF16)
    coord_h = k.sb("coord_h", [18, P], BF16)
    coord_hc = k.sb("coord_hc", [18, 2, HP], BF16)
    bias_bw1 = k.sb("bias_bw1", [3, 4, P], BF16)
    bias_bh1 = k.sb("bias_bh1", [3, 4, P], BF16)
    ones3 = k.sb("ones3", [3, P], BF16)
    with ExitStack() as ctx:
        raw = {n: k.sb(n + "_raw", [9, w], F32, ctx) for n, w in
               (("coord_w", P), ("coord_wc", ROWS * W), ("coord_h", P), ("coord_hc", 4 * HP),
                ("bias_bw1", 4 * P), ("bias_bh1", 4 * P))}
        cut = {n: [k.sb(f"{n}_cut{i}", [9, r.shape[1]], BF16, ctx) for i in range(3)] for n, r in raw.items()}
        tmp = k.sb("setup_tmp", [P, 512], F32, ctx)
        mean = k.sb("setup_mean", [P, 4], F32, ctx)
        ps = k.ps("setup_ps", ctx)
        n_loads = len(TABLES) + len(raw)
        mm = k.sem("setup_mm")
        block = ctx.enter_context(nc.Block())

        @block.sync
        def _(sp):
            for name in TABLES:
                sp.dma_start(t[name][tuple(slice(None) for _ in TABLES[name])], a[name]).then_inc(loaded, 16)
            for name, r in raw.items():
                sp.dma_start(r[:, :], a[name]).then_inc(loaded, 16)
            sp.wait_ge(chain, 1 + 5 * len(raw) + 6)
            n = 0
            for i in range(3):
                for name, dst in (("coord_w", coord_w),):
                    sp.dma_start(dst[3 * i:3 * i + 3, :], cut[name][i][0:3, :]).then_inc(placed, 16)
                    n += 1
                for j in range(3):
                    sp.dma_start(coord_wc[3 * j + i:3 * j + i + 1, :], cut["coord_wc"][i][0:1, :]).then_inc(placed, 16)
                    n += 1
                    for hj in range(2):
                        sp.dma_start(coord_hc[9 * hj + 3 * j + i:9 * hj + 3 * j + i + 1, :, :],
                                     cut["coord_hc"][i][0:1, hj * P:hj * P + P]
                                     .rearrange("a (p h) -> a p h", p=2)).then_inc(placed, 16)
                        n += 1
                for hj in range(2):
                    sp.dma_start(coord_h[9 * hj + 3 * i:9 * hj + 3 * i + 3, hj * HID:hj * HID + HID],
                                 cut["coord_h"][i][0:3, 0:HID]).then_inc(placed, 16)
                    n += 1
                for name, dst in (("bias_bw1", bias_bw1), ("bias_bh1", bias_bh1)):
                    sp.dma_start(dst[i:i + 1, :, :], cut[name][i][0:1, :].rearrange("a (g n) -> a g n", g=4)).then_inc(placed, 16)
                    n += 1
            sp.wait_ge(placed, 16 * n)

        @block.vector
        def _(v):
            link = Chain(v, chain)
            v.wait_ge(loaded, 16 * n_loads)
            link(v.memset(ones3[:, :], 1.0))
            for name, r in raw.items():
                w = r.shape[1]
                split_rows(v, link, [c[:, :] for c in cut[name]], r[:, :], tmp[0:9, 0:w])
            link(v.memset(coord_h[:, :], 0.0))
            link(v.memset(mix_bd[:, :], 0.0))
            link(v.tensor_scalar(t["bh2"][:, 1, 0:M], t["bh2"][:, 1, 0:M], -1.0, None, ALU.mult))
            link(v.tensor_scalar(t["cond_h"][0:M, 3:4], t["cond_h"][0:M, 3:4], -1.0, None, ALU.mult))
            link(v.tensor_scalar(t["hi2"][0:M, 1, :], t["hi2"][0:M, 1, :], -1.0, None, ALU.mult))
            link(v.reduce_sum(mean[:, 0:1], t["mixer"][:, :], axis=AX.X))
            link(v.tensor_scalar(mean[:, 1:2], mean[:, 0:1], 1.0 / C, None, ALU.mult))
            link(v.tensor_scalar(mix_c[:, :], t["mixer"][:, :], mean[:, 1:2], 1.0 / NPX, ALU.subtract, ALU.mult))
            for q in range(4):
                r = slice(32 * q, 32 * q + 32)
                link(v.tensor_copy(mix_bd[r, r], mix_c[r, :]))
            link(v.reduce_sum(mean[:, 2:3], t["mixer_b"][:, :], axis=AX.X))
            link(v.tensor_scalar(mean[:, 3:4], mean[:, 2:3], 1.0 / C, None, ALU.mult))
            link(v.tensor_tensor(y_const[:, :], t["mixer_own"][:, :], mean[:, 3:4], ALU.subtract))
            for mp in range(16):
                v.tensor_scalar(cond_y_w[:, mp, HID:HID + C], mix_c[:, :], t["wi2_b"][:, mp:mp + 1], None, ALU.mult)
                last = v.tensor_scalar(cond_y_w[:, mp, 0:HID], t["wi0"][:, :], t["comp_w"][:, mp:mp + 1], None, ALU.mult)
            link(last)
            v.wait_ge(mm, 1)
            link(v.tensor_tensor(wi0_const[:, :], ps[:, 0:1], t["wi0_b"][:, :], ALU.add))

        @block.tensor
        def _(pe):
            pe.wait_ge(loaded, 16 * n_loads)
            pe.matmul(ps[:, 0:1], t["wi0_sum"][:, :], t["comp_w_b"][:, :], start=True, stop=True).then_inc(mm, 1)


def dht(k):
    nc, t, x, B = k.nc, k.t, k.a["x"], k.B
    CH = 4
    KEEP = t["cas_n"].shape[2]
    NJ = C // CH
    loaded = [k.sem(f"dht_x_loaded{i}") for i in range(4)]
    cols_done, a1_done, stats_done = k.sem("dht_cols_done"), k.sem("dht_a1_done"), k.sem("dht_stats_done")
    modes_done, xm_done, rows_agg, rows_kept = (k.sem(n) for n in ("dht_modes_done", "dht_xm_done", "dht_rows_agg", "dht_rows_kept"))
    XM, MV = t["XM"], t["MV"]
    with ExitStack() as ctx:
        xa = [k.sb(f"dht_x{i}", [P, CH, 2, W], F32, ctx) for i in range(4)]
        A1 = k.sb("dht_a1", [P, 2, 2 * M, C], F32, ctx)
        ST = k.sb("dht_stats", [P, C, 6], F32, ctx)
        AG = k.sb("dht_agg", [P, 16, 2], F32, ctx)
        pad = k.sb("dht_pad", [P, 1], F32, ctx)
        psA = [ctx.enter_context(nc.psum_tensor(f"dht_psA{i}", [P, 2, 512], F32)) for i in range(2)]
        psX = k.ps("dht_psX", ctx)
        block = ctx.enter_context(nc.Block())

        @block.sync
        def _(sp):
            prime(sp, cols_done, a1_done, stats_done, modes_done, xm_done, rows_agg, rows_kept)
            with sp.Fori(0, B) as b:
                for j in range(NJ):
                    sp.wait_ge(cols_done, done(b * NJ + j - 4))
                    sp.wait_ge(stats_done, done(b * NJ + j - 4))
                    sp.dma_start(xa[j % 4][:, :, :, :],
                                 x[bass.ds(b, 1), CH * j:CH * j + CH].rearrange("a c (g p) w -> p (a c) g w", p=P))\
                      .then_inc(loaded[j % 4], 16)

        @block.tensor
        def _(pe):
            with pe.Fori(0, B) as b:
                for j in range(NJ):
                    pe.wait_ge(loaded[j % 4], (b * 2 + j // 4 + 1) * 16)
                    pe.wait_ge(a1_done, done(b * NJ + j - 2))
                    ps = psA[j % 2][:, :, 0:4 * KEEP].rearrange("p k (c g n) -> p k c g n", c=2, g=2)
                    for c in range(CH):
                        for g in range(2):
                            for hh in range(2):
                                last = pe.matmul(ps[:, c // 2, c % 2, g, :], xa[j % 4][:, c, hh, g * P:g * P + P],
                                                 t["cas_n"][:, hh, :], start=hh == 0, stop=hh == 1)
                    last.then_inc(cols_done, 1)
                pe.wait_ge(a1_done, done(b * NJ + NJ - 1))
                pe.wait_ge(xm_done, done(b - 1))
                for f in range(2):
                    for kg in range(8):
                        for g in range(2):
                            last = pe.matmul(psX[:, (f * 8 + kg) * M:(f * 8 + kg + 1) * M],
                                             A1[:, g, f * M + 4 * kg:f * M + 4 * kg + 4, :],
                                             t["cas_n"][:, g, f * M:f * M + M], start=g == 0, stop=g == 1)
                last.then_inc(modes_done, 1)

        @block.scalar
        def _(act):
            with act.Fori(0, B) as b:
                for j in range(NJ):
                    act.wait_ge(cols_done, done(b * NJ + j))
                    if j == 0:
                        act.wait_ge(modes_done, done(b - 1))
                    for bank in range(2):
                        last = act.copy(A1[:, :, :, CH * j + 2 * bank:CH * j + 2 * bank + 2].rearrange("p g n c -> p c g n"),
                                        psA[j % 2][:, bank, 0:4 * KEEP].rearrange("p (c g n) -> p c g n", c=2, g=2)[:, :, :, 0:2 * M])
                    last.then_inc(a1_done, 1)
                act.wait_ge(modes_done, done(b))
                act.copy(XM[:, :, bass.ds(b, 1)], psX[:, :].rearrange("p (n a) -> p n a", a=1)).then_inc(xm_done, 1)

        @block.vector
        def _(v):
            with v.Fori(0, B) as b:
                for j in range(NJ):
                    v.wait_ge(loaded[j % 4], (b * 2 + j // 4 + 1) * 16)
                    if j == 0:
                        v.wait_ge(rows_agg, done(b - 1))
                    for c in range(CH):
                        last = v.bn_stats(ST[:, CH * j + c, :], xa[j % 4][:, c, :, :].rearrange("p g w -> p (g w)"))
                    last.then_inc(stats_done, 1)
                v.wait_ge(stats_done, done(b * NJ + NJ - 1))
                v.wait_ge(rows_kept, done(b - 1))
                v.memset(pad[:, :], 0.0)
                for g in range(16):
                    last = v.bn_aggr(AG[:, g, :], ST[:, 2 * g:2 * g + 2, :].rearrange("p a s -> p (a s)"))
                last.then_inc(rows_agg, 1)
                v.wait_ge(rows_agg, done(b))
                v.tensor_copy(MV[:, bass.ds(b, 1), :, :], AG[:, :, :].rearrange("p (a g) s -> p a g s", a=1)).then_inc(rows_kept, 1)


def select_channels(v, link, dst, src, t, tmp, B):
    link(v.tensor_tensor(tmp, src, t["chan_mask"][:, :].unsqueeze(1).broadcast_to([P, B, 16]), ALU.mult))
    link(v.reduce_sum(dst, tmp, axis=AX.X))


def mix0(k):
    nc, t, B = k.nc, k.t, k.B
    XM, MV = t["XM"], t["MV"]
    chain, st_mm, w_loaded, w_ready, w_used = (k.sem(n) for n in
                                               ("mix0_chain", "mix0_stat_mm", "mix0_w_loaded", "mix0_w_ready", "mix0_w_used"))
    zs, z_done, xn_ready, z_ready, z_stored = (k.sem(n) for n in
                                               ("mix0_z_mm", "mix0_z_copied", "mix0_xm_ready", "mix0_z_ready", "mix0_z_stored"))
    st_in = k.sem("mix0_stat_in")
    NB = B * 16
    with ExitStack() as ctx:
        Z = k.sb("Z", [P, 8, M, B], F32, ctx)
        ZB = k.sb("ZB", [P, B, 8, M], F32, ctx)
        tmp = k.sb("mix0_tmp", [P, 8, M, B], F32, ctx)
        w = [k.sb(f"mix0_w{i}", [P, 2, M, C], F32, ctx) for i in range(2)]
        wy = [k.sb(f"mix0_wy{i}", [P, 2, M, C], F32, ctx) for i in range(2)]
        sq = k.sb("mix0_sq", [P, B, 16], F32, ctx)
        mb = k.sb("mix0_mb", [P, B, 16], F32, ctx)
        s = {n: k.sb("mix0_" + n, [P, B], F32, ctx) for n in
             ("mean", "var", "r", "u", "v", "z00", "my", "cov", "vy", "p1", "p2")}
        ps = k.ps("mix0_ps", ctx)
        psZ = [k.ps(f"mix0_psZ{q}", ctx) for q in range(4)]
        block = ctx.enter_context(nc.Block())
        mean1, invs, s1 = t["mean1"], t["invs"], t["s1"]

        @block.sync
        def _(sp):
            for kg in range(8):
                if kg >= 2:
                    sp.wait_ge(w_ready, kg - 1)
                sp.dma_start(w[kg % 2][:, :, :, :], k.a["l0_w"][kg]).then_inc(w_loaded, 16)
                sp.wait_ge(w_loaded, 16 * (kg + 1))
            sp.wait_ge(z_ready, 1)
            for q in range(4):
                for oj in range(4):
                    sp.dma_start(k.zd[oj, q].rearrange("b g o w -> o (b g) w"),
                                 ZB[32 * q + oj:32 * q + 32:4, :, :, :].rearrange("o b g w -> o (b g) w")).then_inc(z_stored, 16)
            sp.wait_ge(z_stored, 256)

        @block.tensor
        def _(pe):
            def avg(n, weights, src, width):
                pe.wait_ge(st_in, n)
                pe.matmul(ps[:, 0:width], weights, src, start=True, stop=True).then_inc(st_mm, 1)
            avg(1, t["ones_avg"][:, :], mb[:, :, :].rearrange("p b g -> p (b g)"), NB)
            avg(2, t["ones_avg"][:, :], sq[:, :, :].rearrange("p b g -> p (b g)"), NB)
            pe.wait_ge(xn_ready, 1)
            for kg in range(8):
                pe.wait_ge(w_ready, kg + 1)
                if kg >= 1:
                    pe.wait_ge(z_done, kg)
                for kw in range(M):
                    for q in range(4):
                        r = slice(32 * q, 32 * q + 32)
                        for f in range(2):
                            last = pe.matmul(psZ[q][r, kw * B:kw * B + B], wy[kg % 2][r, f, kw, :],
                                             XM[r, (f * 8 + kg) * M + kw, :], start=f == 0, stop=f == 1)
                last.then_inc(zs, 1)
            avg(3, t["group_avg"][:, :], s["z00"][:, :], B)
            avg(4, t["group_avg"][:, :], s["p1"][:, :], B)
            avg(5, t["group_avg"][:, :], s["p2"][:, :], B)

        @block.scalar
        def _(act):
            for kg in range(8):
                act.wait_ge(zs, kg + 1)
                for q in range(4):
                    r = slice(32 * q, 32 * q + 32)
                    last = act.mul(Z[r, kg, :, :].rearrange("p w b -> p (w b)"), psZ[q][r, 0:M * B], 0.5 / NPX)
                last.then_inc(z_done, 1)

        @block.vector
        def _(v):
            link = Chain(v, chain)
            v.tensor_copy(mb[:, :, :], MV[:, :, :, 0]).then_inc(st_in, 1)
            v.wait_ge(st_mm, 1)
            link(v.tensor_copy(mb[:, :, :], ps[:, 0:NB].rearrange("p (b g) -> p b g", g=16)))
            select_channels(v, link, s["mean"][:, :], mb[:, :, :], t, sq[:, :, :], B)
            link(v.tensor_tensor(sq[:, :, :], MV[:, :, :, 0], mb[:, :, :], ALU.subtract))
            link(v.tensor_tensor(sq[:, :, :], sq[:, :, :], sq[:, :, :], ALU.mult))
            v.tensor_tensor(sq[:, :, :], sq[:, :, :], MV[:, :, :, 1], ALU.add).then_inc(st_in, 1)
            v.wait_ge(st_mm, 2)
            link(v.tensor_copy(mb[:, :, :], ps[:, 0:NB].rearrange("p (b g) -> p b g", g=16)))
            select_channels(v, link, s["var"][:, :], mb[:, :, :], t, sq[:, :, :], B)
            link(v.tensor_scalar(s["u"][:, :], s["var"][:, :], 1e-5, None, ALU.add))
            rsqrt_chain(v, link, s["r"][:, :], s["u"][:, :], s["v"][:, :])
            link(v.tensor_scalar(s["v"][:, :], s["mean"][:, :], float(NPX), None, ALU.mult))
            for f in range(2):
                link(v.tensor_tensor(XM[0:32, f * 8 * M, :], XM[0:32, f * 8 * M, :], s["v"][0:32, :], ALU.subtract))
            v.tensor_tensor(XM[:, :, :], XM[:, :, :], s["r"][:, :].unsqueeze(1).broadcast_to([P, 2 * 8 * M, B]), ALU.mult)\
             .then_inc(xn_ready, 1)
            for kg in range(8):
                v.wait_ge(w_loaded, 16 * (kg + 1))
                if kg >= 2:
                    v.wait_ge(zs, kg - 1)
                v.tensor_tensor(wy[kg % 2][:, 0, :, :], w[kg % 2][:, 0, :, :], w[kg % 2][:, 1, :, :], ALU.add)
                v.tensor_tensor(wy[kg % 2][:, 1, :, :], w[kg % 2][:, 0, :, :], w[kg % 2][:, 1, :, :], ALU.subtract)\
                 .then_inc(w_ready, 1)
            v.wait_ge(z_done, 8)
            v.wait_ge(xn_ready, 1)
            link(v.memset(s["z00"][:, :], 0.0))
            v.tensor_scalar(s["z00"][0:32, :], Z[0:32, 0, 0, :], 4.0, None, ALU.mult).then_inc(st_in, 1)
            v.wait_ge(st_mm, 3)
            link(v.tensor_copy(s["my"][:, :], ps[:, 0:B]))
            link(v.tensor_tensor(tmp[:, :, :, :].rearrange("p g w b -> p (g w) b"), XM[:, 0:8 * M, :],
                                 Z[:, :, :, :].rearrange("p g w b -> p (g w) b"), ALU.mult))
            link(v.reduce_sum(s["u"][:, :], tmp[:, :, :, :].rearrange("p g w b -> p b (g w)"), axis=AX.X))
            v.tensor_scalar(s["p1"][:, :], s["u"][:, :], 4.0 / NPX, None, ALU.mult).then_inc(st_in, 1)
            v.wait_ge(st_mm, 4)
            link(v.tensor_copy(s["cov"][:, :], ps[:, 0:B]))
            link(v.tensor_copy(tmp[:, :, :, :], Z[:, :, :, :]))
            link(v.tensor_tensor(tmp[0:32, 0, 0, :], tmp[0:32, 0, 0, :], s["my"][0:32, :], ALU.subtract))
            link(v.tensor_tensor(tmp[:, :, :, :], tmp[:, :, :, :], tmp[:, :, :, :], ALU.mult))
            link(v.reduce_sum(s["u"][:, :], tmp[:, :, :, :].rearrange("p g w b -> p b (g w)"), axis=AX.X))
            v.tensor_scalar(s["p2"][:, :], s["u"][:, :], 4.0, None, ALU.mult).then_inc(st_in, 1)
            v.wait_ge(st_mm, 5)
            link(v.tensor_copy(s["vy"][:, :], ps[:, 0:B]))
            link(v.tensor_scalar(s["u"][:, :], s["var"][:, :], 1e-5, None, ALU.add))
            link(v.tensor_tensor(s["u"][:, :], s["u"][:, :], s["r"][:, :], ALU.mult))
            link(v.tensor_tensor(s["cov"][:, :], s["cov"][:, :], s["u"][:, :], ALU.mult))
            link(v.tensor_scalar(s["cov"][:, :], s["cov"][:, :], 2.0, 1e-5, ALU.mult, ALU.add))
            link(v.tensor_tensor(s["cov"][:, :], s["cov"][:, :], s["var"][:, :], ALU.add))
            link(v.tensor_tensor(s["u"][:, :], s["cov"][:, :], s["vy"][:, :], ALU.add))
            rsqrt_chain(v, link, s1[:, :], s["u"][:, :], s["v"][:, :])
            link(v.tensor_tensor(invs[:, :], s["u"][:, :], s1[:, :], ALU.mult))
            link(v.tensor_tensor(mean1[:, :], s["mean"][:, :], s["my"][:, :], ALU.add))
            link(v.tensor_tensor(s["v"][:, :], mean1[:, :], s1[:, :], ALU.mult))
            link(v.tensor_tensor(ZB[:, :, :, :].rearrange("p b g w -> p b (g w)"),
                                 Z[:, :, :, :].rearrange("p g w b -> p b (g w)"),
                                 s1[:, :].unsqueeze(2).broadcast_to([P, B, 8 * M]), ALU.mult))
            v.tensor_tensor(ZB[0:32, :, 0, 0], ZB[0:32, :, 0, 0], s["v"][0:32, :], ALU.subtract).then_inc(z_ready, 1)


def rows0(k):
    nc, t, B = k.nc, k.t, k.B
    z_loaded = [k.sem(f"rows0_z_loaded{i}") for i in range(2)]
    v_stored = [k.sem(f"rows0_v_stored{i}") for i in range(2)]
    mm_done, copied = k.sem("rows0_mm_done"), k.sem("rows0_copied")
    GR = 16
    with ExitStack() as ctx:
        ZT = [k.sb(f"ZT{i}", [P, 8, M], F32, ctx) for i in range(2)]
        V = [k.sb(f"V{i}", [M, HP, P], F32, ctx) for i in range(2)]
        ps = [k.ps(f"rows0_ps{i}", ctx) for i in range(4)]
        block = ctx.enter_context(nc.Block())

        @block.sync
        def _(sp):
            prime(sp, mm_done, copied)
            for u in range(2):
                sp.sem_inc(v_stored[u], 16)
            with sp.Fori(0, B // 2) as bh:
                for u in range(2):
                    if u == 0:
                        sp.wait_ge(mm_done, bh * (2 * GR) + PRIME)
                    sp.dma_start(ZT[u][:, :, :],
                                 k.zd[:, :, bass.ds(bh * 2 + u, 1)].rearrange("j q a g o w -> (j q a) g (o w)"))\
                      .then_inc(z_loaded[u], 16)
                for u in range(2):
                    sp.wait_ge(copied, (bh * 2 + u + 1) * GR + PRIME)
                    sp.dma_start(k.vd[bass.ds(bh * 2 + u, 1)].rearrange("a k h q -> (a k) h q"), V[u][:, :, :])\
                      .then_inc(v_stored[u], 16)
            for u in range(2):
                sp.wait_ge(v_stored[u], 16 * (B // 2) + 16)

        @block.tensor
        def _(pe):
            with pe.Fori(0, B // 2) as bh:
                for u in range(2):
                    pe.wait_ge(z_loaded[u], bh * 16 + 16)
                    for n in range(GR):
                        pe.wait_ge(copied, (bh * 2 + u) * GR + n - 3 + PRIME)
                        pe.matmul(ps[n % 4][0:M, :], ZT[u][:, n // 2, :],
                                  t["cas_bd"][:, 512 * (n % 2):512 * (n % 2) + 512],
                                  start=True, stop=True).then_inc(mm_done, 1)

        @block.scalar
        def _(act):
            with act.Fori(0, B // 2) as bh:
                for u in range(2):
                    act.wait_ge(v_stored[u], bh * 16 + 16)
                    for n in range(GR):
                        act.wait_ge(mm_done, (bh * 2 + u) * GR + n + 1 + PRIME)
                        c0 = 2 * n
                        for hj in range(2):
                            dst = V[u][:, :, :].rearrange("k h (p j c) -> k c j p h", p=2, j=2)
                            src = ps[n % 4][0:M, :].rearrange("k (c j p h) -> k c j p h", c=2, j=2, p=2)
                            last = act.copy(dst[:, c0:c0 + 2, hj, :, :], src[:, :, hj, :, :])
                        last.then_inc(copied, 1)


def forward(k):
    nc, t, x, B = k.nc, k.t, k.a["x"], k.B
    XH, s1 = t["XH"], t["s1"]
    x_loaded = [k.sem(f"fw_x_loaded{u}") for u in range(2)]
    v_loaded = [k.sem(f"fw_v_loaded{u}") for u in range(2)]
    xn_stored = [k.sem(f"fw_xn_stored{u}") for u in range(2)]
    names = ("y_done", "xn_done", "xt_done", "xt_copied", "l0_done", "g0_done", "l1_done", "g1_done", "gm_done",
             "gm_copied", "xw_done", "xwa_done", "xs_done", "xb_done",
             "bt_done", "bt_copied", "b0_done", "b0_gelu", "b1_done", "b1_gelu", "e_done", "e_copied", "xh_done", "xh_copied")
    S = {n: k.sem("fw_" + n) for n in names}
    zeroed = k.sem("fw_zeroed")
    N = ROWS * W
    with ExitStack() as ctx:
        sb = lambda name, shape: k.sb("fw_" + name, shape, F32, ctx)
        xin = [sb(f"x{u}", [P, CHUNK * W]) for u in range(2)]
        vch = [sb(f"v{u}", [M, CHUNK, P]) for u in range(2)]
        xn = [sb(f"xn{u}", [P, CHUNK * W]) for u in range(2)]
        h1 = sb("h1", [P, 2, ROWS, W])
        h2 = sb("h2", [P, 2, ROWS, 2, P])
        xT = [sb(f"xT{u}", [P, ROWS, 2, P]) for u in range(2)]
        gt = sb("gt", [P, ROWS, 2, 2, C])
        xs = sb("xs", [P, 8])
        xb = sb("xb", [P, 8, HID])
        xwa = sb("xwa", [P, 2 * M, HP])
        xwT = sb("xwT", [P, 16, 2, P])
        hb1 = sb("hb1", [P, 2, M, HP])
        hb2 = sb("hb2", [P, 16, 4, HID + 1])
        et = sb("et", [HID + 1, 2, 8, 4, C])
        psY, psT, psG, psW = (k.ps("fw_ps" + n, ctx) for n in "YTGW")
        psL0 = [k.ps(f"fw_psL0{p}", ctx) for p in range(2)]
        psL1 = [k.ps(f"fw_psL1{p}", ctx) for p in range(2)]
        block = ctx.enter_context(nc.Block())
        x_v = x.rearrange("b c (j p i u r) w -> b j p u i c (r w)", j=2, p=2, i=ITERS, u=2)
        v_v = k.vd.rearrange("b k (i u r) q -> b u i k (r q)", i=ITERS, u=2)

        @block.sync
        def _(sp):
            prime(sp, *S.values())
            for u in range(2):
                sp.sem_inc(xn_stored[u], 16)
            with sp.Fori(0, B) as b:
                with sp.Fori(0, ITERS) as i:
                    for u in range(2):
                        sp.wait_ge(S["xn_done"], done((b * ITERS + i) * STEPS + 2 * u - 3))
                        sp.dma_start(vch[u][:, :, :], v_v[bass.ds(b, 1), u, bass.ds(i, 1)]
                                     .rearrange("a e k (r q) -> (a e k) r q", r=CHUNK)).then_inc(v_loaded[u], 16)
                        for q in range(4):
                            sp.dma_start(xin[u][32 * q:32 * q + 32, :],
                                         x_v[bass.ds(b, 1), q % 2, q // 2, u, bass.ds(i, 1)]
                                         .rearrange("a e c n -> (a e c) n")).then_inc(x_loaded[u], 16)
            for u in range(2):
                sp.wait_ge(xn_stored[u], B * ITERS * 16 + 16)

        @block.tensor
        def _(pe):
            def y0(n, it, s):
                if s % 2 == 0:
                    pe.wait_ge(v_loaded[s // 2], (it + 1) * 16)
                pe.wait_ge(S["xn_done"], done(n - 1))
                for r in range(ROWS):
                    last = pe.matmul(psY[:, r * W:r * W + W], vch[s // 2][:, (s % 2) * ROWS + r, :], t["cas_k"][:, :],
                                     start=True, stop=True)
                last.then_inc(S["y_done"], 1)

            def transposes(n, s):
                pe.wait_ge(S["xn_done"], done(n))
                pe.wait_ge(S["xt_copied"], done(n - 1))
                for r in range(ROWS):
                    for g in range(2):
                        o = (s % 2) * N + r * W + g * P
                        last = pe.transpose(psT[:, (2 * r + g) * P:(2 * r + g) * P + P],
                                            xn[s // 2][:, o:o + P], t["ident"][:, :])
                last.then_inc(S["xt_done"], 1)

            def layer0(n, s):
                for p in range(2):
                    pe.wait_ge(S["g0_done"], done(2 * (n - 1) + p))
                    pe.matmul(psL0[p][:, :], t["coord_w"][:, :], t["coord_wc"][:, :], start=True, stop=False)
                    pe.matmul(psL0[p][:, :], t["bw0"][:, p, :], xn[s // 2][:, (s % 2) * N:(s % 2) * N + N],
                              start=False, stop=True).then_inc(S["l0_done"], 1)

            def layer1(n):
                for p in range(2):
                    pe.wait_ge(S["g0_done"], done(2 * n + p))
                    pe.wait_ge(S["g1_done"], done(2 * (n - 1) + p))
                    pe.matmul(psL1[p][:, :], t["ones3"][:, :], t["bias_bw1"][:, :, :].rearrange("a g n -> a (g n)"),
                              start=True, stop=False)
                    for r in range(ROWS):
                        for g in range(2):
                            last = pe.matmul(psL1[p][:, (2 * r + g) * P:(2 * r + g) * P + P],
                                             h1[:, p, r, g * P:g * P + P], t["bw1"][:, :], start=False, stop=r + g == 2)
                    last.then_inc(S["l1_done"], 1)

            def project(n, s):
                pe.wait_ge(S["g1_done"], done(2 * n + 1))
                pe.wait_ge(S["xt_copied"], done(n))
                pe.wait_ge(S["gm_copied"], done(n - 1))
                for r in range(ROWS):
                    for p in range(2):
                        for g in range(2):
                            last = pe.matmul(psG[:, (2 * r + p) * HID:(2 * r + p) * HID + HID], h2[:, p, r, g, :],
                                             xT[s % 2][:, r, g, p * HID:p * HID + HID], start=g == 0, stop=g == 1)
                last.then_inc(S["gm_done"], 1)

            def last_matrix(n, it, s):
                pe.wait_ge(S["gm_copied"], done(n))
                if s == 0:
                    pe.wait_ge(S["xwa_done"], done(it - 1))
                for r in range(ROWS):
                    for p in range(2):
                        last = pe.matmul(psW[p * HID:p * HID + HID, (ROWS * s + r) * HID:(ROWS * s + r + 1) * HID],
                                         gt[:, r, p, :, :], t["bw2"][:, :], start=True, stop=True)
                last.then_inc(S["xw_done"], 1)

            def iteration(it, first):
                for s in range(STEPS):
                    n = it * STEPS + s
                    y0(n, it, s)
                    if not (first and s == 0):
                        layer1(n - 1)
                    transposes(n, s)
                    layer0(n, s)
                    if not (first and s < 2):
                        last_matrix(n - 2, it if s >= 2 else it - 1, (s - 2) % STEPS)
                    if not (first and s == 0):
                        project(n - 1, (s - 1) % STEPS)

            def basis_h(b):
                pe.wait_ge(S["xwa_done"], done(b * ITERS + ITERS - 1))
                for i in range(8):
                    pe.wait_ge(S["bt_copied"], done(8 * b + i - 2))
                    for j in range(4):
                        mp, ri = 2 * i + j // 2, j % 2
                        last = pe.transpose((psT, psY)[i % 2][:, j * P:j * P + P],
                                            xwa[:, ri * M + 2 * mp:ri * M + 2 * mp + 2, :].rearrange("p m h -> p (m h)"),
                                            t["ident"][:, :])
                    last.then_inc(S["bt_done"], 1)
                for i in range(8):
                    mg, p = i // 2, i % 2
                    pe.wait_ge(S["b0_gelu"], done(8 * b + i - 2))
                    pe.matmul(psL0[p][:, :].rearrange("q (m h) -> q m h", m=8), t["coord_h"][:, :],
                              t["coord_hc"][:, p, :].unsqueeze(1).broadcast_to([18, 8, HP]), start=True, stop=False)
                    pe.matmul(psL0[p][:, :], t["bh0"][:, p, :], xwa[:, 8 * mg:8 * mg + 8, :].rearrange("p m h -> p (m h)"),
                              start=False, stop=True).then_inc(S["b0_done"], 1)
                for i in range(8):
                    pe.wait_ge(S["b0_gelu"], done(8 * b + 2 * (i // 2) + 1))
                    pe.wait_ge(S["b1_gelu"], done(8 * b + i - 2))
                    ps = psL1[i % 2]
                    pe.matmul(ps[:, :], t["ones3"][:, :], t["bias_bh1"][:, :, :].rearrange("a g n -> a (g n)"),
                              start=True, stop=False)
                    for j in range(4):
                        mp, p = 2 * i + j // 2, j % 2
                        last = pe.matmul(ps[:, j * P:j * P + P], hb1[:, p, 2 * mp:2 * mp + 2, :].rearrange("p m h -> p (m h)"),
                                         t["bh1"][:, :], start=False, stop=j == 3)
                    last.then_inc(S["b1_done"], 1)
                pe.wait_ge(S["bt_copied"], done(8 * b + 7))
                for i in range(4):
                    m2, half = i % 2, i // 2
                    rows = slice(HID * m2, HID * m2 + HID)
                    pe.wait_ge(S["b1_gelu"], done(8 * b + 4 * half + 3))
                    for j in range(8):
                        mp = 8 * half + j
                        for q in range(4):
                            last = pe.matmul((psG, psW, psT, psY)[i][0:HID + 1, j * HID:j * HID + HID], hb2[rows, mp, q, :],
                                             xwT[rows, mp, :, q * C:q * C + C], start=q == 0, stop=q == 3)
                    last.then_inc(S["e_done"], 1)
                pe.wait_ge(S["e_copied"], done(4 * b + 3))
                for m8 in range(8):
                    for ri in range(2):
                        last = pe.matmul(psG[:, m8 * HID:m8 * HID + HID], et[:, ri, m8, :, :].rearrange("f g c -> f (g c)"), t["bh2"][:, ri, :],
                                         start=ri == 0, stop=ri == 1)
                last.then_inc(S["xh_done"], 1)

            with pe.Fori(0, B) as b:
                pe.wait_ge(S["xh_copied"], done(b - 1))
                iteration(b * ITERS, True)
                with pe.Fori(1, ITERS) as i:
                    iteration(b * ITERS + i, False)
                it = b * ITERS + ITERS - 1
                n = it * STEPS + STEPS - 1
                layer1(n)
                last_matrix(n - 1, it, STEPS - 2)
                project(n, STEPS - 1)
                last_matrix(n, it, STEPS - 1)
                basis_h(b)

        @block.scalar
        def _(act):
            def gelu0(n):
                for p in range(2):
                    act.wait_ge(S["l0_done"], done(2 * n + p))
                    act.wait_ge(S["l1_done"], done(2 * (n - 1) + p))
                    act.activation(h1[:, p, :, :].rearrange("q r w -> q (r w)"), psL0[p][:, :], ACT.Gelu,
                                   bias=t["bw0_b"][:, :]).then_inc(S["g0_done"], 1)

            def gelu1(n):
                for p in range(2):
                    act.wait_ge(S["l1_done"], done(2 * n + p))
                    act.wait_ge(S["gm_done"], done(n - 1))
                    act.activation(h2[:, p, :, :, :].rearrange("q r g f -> q (r g f)"), psL1[p][:, :], ACT.Gelu)\
                       .then_inc(S["g1_done"], 1)

            def iteration(b, i, first):
                it = b * ITERS + i
                for s in range(STEPS):
                    n = it * STEPS + s
                    if not (first and s == 0):
                        gelu1(n - 1)
                    gelu0(n)
                    if s % 2 == 1:
                        act.wait_ge(S["xn_done"], done(n))
                        act.dma_start(k.xnd[bass.ds(b * (2 * ITERS) + 2 * i + s // 2, 1)].rearrange("a p n -> (a p) n"),
                                      xn[s // 2][:, :]).then_inc(xn_stored[s // 2], 16)

            with act.Fori(0, B) as b:
                iteration(b, 0, True)
                with act.Fori(1, ITERS) as i:
                    iteration(b, i, False)
                gelu1((b * ITERS + ITERS - 1) * STEPS + STEPS - 1)
                for i in range(8):
                    mg, p = i // 2, i % 2
                    act.wait_ge(S["b0_done"], done(8 * b + i))
                    act.wait_ge(S["b1_done"], done(8 * b - 1))
                    act.activation(hb1[:, p, 8 * mg:8 * mg + 8, :].rearrange("q m h -> q (m h)"), psL0[p][:, :], ACT.Gelu,
                                   bias=t["bh0_b"][:, :]).then_inc(S["b0_gelu"], 1)
                for i in range(8):
                    act.wait_ge(S["b1_done"], done(8 * b + i))
                    act.wait_ge(S["e_done"], done(4 * b - 1))
                    act.activation(hb2[:, 2 * i:2 * i + 2, :, 0:HID].rearrange("q a c f -> q (a c) f"),
                                   psL1[i % 2][:, :].rearrange("q (a f) -> q a f", f=HID), ACT.Gelu)\
                       .then_inc(S["b1_gelu"], 1)

        @block.vector
        def _(v):
            def copy_g(n):
                v.wait_ge(S["gm_done"], done(n))
                v.wait_ge(S["xw_done"], done(n - 1))
                for hj in range(2):
                    r = slice(HID * hj, HID * hj + HID)
                    last = v.tensor_copy(gt[r, :, :, hj, :].rearrange("q r p c -> q (r p) c"),
                                         psG[r, 0:4 * HID].rearrange("q (a c) -> q a c", c=HID)[:, :, hj * C:hj * C + C])
                last.then_inc(S["gm_copied"], 1)

            def copy_xw(b, it, i):
                v.wait_ge(S["xw_done"], done(it * STEPS + STEPS - 1))
                v.wait_ge(S["xb_done"], done(it))
                v.wait_ge(S["b0_done"], done(8 * b - 1))
                v.wait_ge(S["bt_done"], done(8 * b - 1))
                v.tensor_tensor(xwa[:, :, bass.ds(i * 8, 8)], psW[:, :].rearrange("q (h m) -> q m h", h=8),
                                xb[:, :, :].rearrange("q h m -> q m h"), ALU.add).then_inc(S["xwa_done"], 1)

            def iteration(b, i, first):
                it = b * ITERS + i
                for s in range(STEPS):
                    n = it * STEPS + s
                    u, cols = s // 2, slice((s % 2) * N, (s % 2) * N + N)
                    if s % 2 == 0:
                        v.wait_ge(x_loaded[u], (it + 1) * 64)
                        v.wait_ge(xn_stored[u], (it + 1) * 16)
                        v.wait_ge(S["l0_done"], done(2 * (n - 3) + 1))
                        v.wait_ge(S["xs_done"], done(n - 3))
                    v.wait_ge(S["y_done"], done(n))
                    v.scalar_tensor_tensor(xn[u][:, cols], xin[u][:, cols], s1[:, bass.ds(b, 1)], psY[:, :],
                                           ALU.mult, ALU.add).then_inc(S["xn_done"], 1)
                    v.wait_ge(S["xt_done"], done(n))
                    v.wait_ge(S["gm_done"], done(n - 2))
                    v.tensor_copy(xT[s % 2][:, :, :, :].rearrange("q r g c -> q (r g c)"), psT[:, :]).then_inc(S["xt_copied"], 1)
                    if s == 0:
                        v.wait_ge(S["xb_done"], done(it - 1))
                    v.wait_ge(S["xn_done"], done(n))
                    v.reduce_sum(xs[:, ROWS * s:ROWS * s + ROWS], xn[u][:, cols].rearrange("q (r w) -> q r w", r=ROWS),
                                 axis=AX.X).then_inc(S["xs_done"], 1)
                    if s == 2 and not first:
                        copy_xw(b, it - 1, i - 1)
                    if not (first and s == 0):
                        copy_g(n - 1)

            v.memset(hb2[:, :, :, HID:HID + 1], 1.0)
            v.memset(gt[:, :, :, :, :], 0.0).then_inc(zeroed, 1)
            v.wait_ge(zeroed, 1)
            with v.Fori(0, B) as b:
                iteration(b, 0, True)
                with v.Fori(1, ITERS) as i:
                    iteration(b, i, False)
                it = b * ITERS + ITERS - 1
                copy_g(it * STEPS + STEPS - 1)
                copy_xw(b, it, ITERS - 1)
                for i in range(8):
                    v.wait_ge(S["bt_done"], done(8 * b + i))
                    v.wait_ge(S["e_done"], done(4 * b - 1))
                    v.tensor_copy(xwT[:, 2 * i:2 * i + 2, :, :].rearrange("q a r c -> q (a r c)"),
                                  (psT, psY)[i % 2][:, :]).then_inc(S["bt_copied"], 1)
                for i in range(4):
                    m2, half = i % 2, i // 2
                    v.wait_ge(S["e_done"], done(4 * b + i))
                    v.wait_ge(S["xh_done"], done(b - 1))
                    for g in range(2):
                        src = (psG, psW, psT, psY)[i][0:HID + 1, 256 * g:256 * g + 256]
                        last = v.tensor_copy(et[:, :, m2:8:2, 2 * half + g, :].rearrange("q r m c -> q m r c"),
                                             src.rearrange("q (m r c) -> q m r c", m=4, r=2))
                    last.then_inc(S["e_copied"], 1)
                v.wait_ge(S["xh_done"], done(b))
                v.tensor_copy(XH[:, :, bass.ds(b, 1)], psG[:, :].rearrange("q (n a) -> q n a", a=1)).then_inc(S["xh_copied"], 1)

        @block.gpsimd
        def _(g):
            with g.Fori(0, B * ITERS) as it:
                g.wait_ge(S["xs_done"], done(it * STEPS + STEPS - 1))
                g.wait_ge(S["xwa_done"], done(it - 1))
                g.tensor_tensor(xb[:, :, :], t["bw2_b"][:, :].unsqueeze(1).broadcast_to([P, 8, HID]),
                                xs[:, :].unsqueeze(2).broadcast_to([P, 8, HID]), ALU.mult).then_inc(S["xb_done"], 1)


def mix1(k):
    nc, t, B = k.nc, k.t, k.B
    XH = t["XH"]
    KH = M // 2
    w_loaded = [k.sem(f"mix1_w_loaded{u}") for u in range(2)]
    stored = [k.sem(f"mix1_stored{u}") for u in range(2)]
    zeroed, w_ready, mm_done, copied = (k.sem(n) for n in ("mix1_zeroed", "mix1_w_ready", "mix1_mm_done", "mix1_copied"))
    with ExitStack() as ctx:
        wa = [k.sb(f"mix1_wa{u}", [P, KH, 4, 2, C], F32, ctx) for u in range(2)]
        wb = [k.sb(f"mix1_wb{u}", [P, KH, 4, 2, C], F32, ctx) for u in range(2)]
        xf = [k.sb(f"mix1_xf{u}", [B, 2, KH, 4, C], F32, ctx) for u in range(2)]
        ps = [k.ps(f"mix1_ps{i}", ctx) for i in range(4)]
        block = ctx.enter_context(nc.Block())
        units = [(m8, kh) for m8 in range(8) for kh in range(2)]

        @block.sync
        def _(sp):
            sp.wait_ge(zeroed, 1)

            def store(n):
                m8, kh = units[n]
                sp.wait_ge(copied, 8 * (n + 1))
                sp.dma_start(k.xfd[m8, :, :, kh * KH:kh * KH + KH].rearrange("b r k g o -> b r (k g o)"),
                             xf[n % 2][:, :, :, :, :].rearrange("b r k g o -> b r (k g o)")).then_inc(stored[n % 2], 16)
            for n, (m8, kh) in enumerate(units):
                if n >= 2:
                    sp.wait_ge(w_ready, n - 1)
                    sp.wait_ge(mm_done, 8 * (n - 1))
                for g in range(4):
                    r = slice(32 * g, 32 * g + 32)
                    sp.dma_start(wa[n % 2][r, :, g, :, :].rearrange("c k r o -> c k (r o)"),
                                 k.a["l1_w"][m8, r, kh * KH:kh * KH + KH].rearrange("c k r o -> c k (r o)"))\
                      .then_inc(w_loaded[n % 2], 16)
                if n >= 1:
                    store(n - 1)
            store(len(units) - 1)
            for u in range(2):
                sp.wait_ge(stored[u], 16 * len(units) // 2)

        @block.vector
        def _(v):
            for u in range(2):
                v.memset(wa[u][:, :, :, :, :], 0.0)
                last = v.memset(wb[u][:, :, :, :, :], 0.0)
            last.then_inc(zeroed, 1)
            v.wait_ge(zeroed, 1)
            for n in range(len(units)):
                v.wait_ge(w_loaded[n % 2], 64 * (n // 2 + 1))
                if n >= 2:
                    v.wait_ge(mm_done, 8 * (n - 1))
                for g in range(4):
                    r = slice(32 * g, 32 * g + 32)
                    v.tensor_scalar(wb[n % 2][r, :, g, 0, :], wa[n % 2][r, :, g, 1, :], -1.0, None, ALU.mult)
                    last = v.tensor_copy(wb[n % 2][r, :, g, 1, :], wa[n % 2][r, :, g, 0, :])
                last.then_inc(w_ready, 1)

        @block.tensor
        def _(pe):
            for n, (m8, kh) in enumerate(units):
                pe.wait_ge(w_ready, n + 1)
                for j in range(8):
                    g = 8 * n + j
                    if g >= 4:
                        pe.wait_ge(copied, g - 3)
                    for i in range(2):
                        kk = kh * KH + 2 * j + i
                        for ri in range(2):
                            w = (wa, wb)[ri][n % 2][:, 2 * j + i, :, :, :].rearrange("c g r o -> c (g r o)")
                            last = pe.matmul(ps[g % 4][0:B, 256 * i:256 * i + 256], XH[:, (2 * m8 + ri) * M + kk, :], w,
                                             start=ri == 0, stop=ri == 1)
                    last.then_inc(mm_done, 1)

        @block.scalar
        def _(act):
            for n in range(len(units)):
                if n >= 2:
                    act.wait_ge(stored[n % 2], 16 * (n // 2))
                for j in range(8):
                    g = 8 * n + j
                    act.wait_ge(mm_done, g + 1)
                    for i in range(2):
                        last = act.copy(xf[n % 2][:, :, 2 * j + i, :, :].rearrange("b r g o -> b g r o"),
                                        ps[g % 4][0:B, 256 * i:256 * i + 256].rearrange("b (g r o) -> b g r o", g=4, r=2))
                    last.then_inc(copied, 1)


NSTEP = ITERS * STEPS


class Step:

    def __init__(self, b, i, s, edge=None):
        self.b, self.i, self.s, self.edge = b, i, s, edge

    def n(self, lag):
        return self.b * NSTEP + self.i * STEPS + (self.s - lag)

    def it(self, lag):
        return self.b * ITERS + self.i + (self.s - lag) // STEPS

    def pair(self, lag):
        return self.b * (NSTEP // 2) + self.i * (STEPS // 2) + (self.s - lag) // 2

    def row(self, lag):
        h0 = self.i * (ROWS * STEPS) + ROWS * (self.s - lag)
        return h0 % HP if isinstance(h0, int) else h0

    def slot(self, lag, of):
        return (self.s - lag) % of

    def live(self, lag):
        m = self.i * STEPS + self.s - lag if self.edge else None
        return m >= 0 if self.edge == "first" else m < 0 if self.edge == "last" else True

    def opens_image(self, lag):
        return isinstance(self.i, int) and self.edge != "last" and self.i * STEPS + self.s == lag


HEAD = 3


def all_steps(eng, B, image, step, last_lag):
    def head(b, edge):
        image(b)
        for s in range(HEAD * STEPS):
            step(Step(b, s // STEPS, s % STEPS, edge))

    def body(b):
        with eng.Fori(HEAD, ITERS) as i:
            for s in range(STEPS):
                step(Step(b, i, s))
    head(0, "first")
    with eng.Fori(1, B) as b:
        body(b - 1)
        head(b, None)
    body(B - 1)
    for s in range(last_lag):
        step(Step(B, s // STEPS, s % STEPS, "last"))


def inverse(k):
    nc, t, B = k.nc, k.t, k.B
    XF_LOADED, OUT = k.sem("iv_xf_loaded"), k.out
    xn_loaded = [k.sem(f"iv_xn_loaded{u}") for u in range(2)]
    out_stored = [k.sem(f"iv_out_stored{u}") for u in range(2)]
    zeroed = k.sem("iv_zeroed")
    names = ("pre_done", "g1_done", "l1_done", "g2_done", "tp_done", "tp_copied", "y_done", "yc_done", "sq_done",
             "var_done", "rs_done", "rb_done", "bc_done", "yn_done", "gy_done", "sc_done", "t_done", "gs_done",
             "res_done", "out_done", "yb_set", "ivm_set",
             "cond_done", "cond_copied", "td_done", "td_copied", "ah_done", "ah_copied", "hg0_done", "hl1_done",
             "hg1_done", "r_done", "r_copied", "aw_done", "rh_done", "rh_copied", "rt_done", "rt_copied", "rt_half_copied", "aw_copied", "newton", "held")
    S = {n: k.sem("iv_" + n) for n in names}
    N = ROWS * W
    with ExitStack() as ctx:
        sb = lambda name, shape: k.sb("iv_" + name, shape, F32, ctx)
        two = lambda name, shape: [sb(f"{name}{u}", shape) for u in range(2)]
        xfk = sb("xfk", [2 * M, 2, 16, C])
        ch = sb("ch", [C, 2, 2, 16])
        tb_row = sb("tb_row", [P, 16])
        td = sb("td", [P, 16, 2, 2, C])
        ah = sb("ah", [P, 16])
        ha = sb("ha", [P, 16, H])
        hb = sb("hb", [P, 16, H])
        R = sb("R", [P, 16, H])
        rh = ha[:, :, :].rearrange("q a (u n) -> q (a u n)", u=2).rearrange("q (j o c) -> q j o c", j=2, o=C)
        rt = sb("rt", [P, C, P])
        aw = sb("aw", [P, P])
        yb = sb("yb", [P, HP])
        yb_next = sb("yb_next", [P, HP])
        wc_w = sb("wc_w", [P, W])
        ivm = sb("ivm", [P, 2])
        pre, wg1, wg2 = two("pre", [P, 2, ROWS, W]), two("wg1", [P, 2, ROWS, W]), two("wg2", [P, 2, ROWS, W])
        tp = sb("tp", [P, 8, 2, 2, C])
        yc = [sb(f"yc{i}", [P, N]) for i in range(4)]
        sq, yn, gy, tt, gs = (two(n, [P, N]) for n in ("sq", "yn", "gy", "tt", "gs"))
        res = [sb(f"res{i}", [P, N]) for i in range(4)]
        xv, xh, nt = (sb(n, [P, 32]) for n in ("xv", "xh", "nt"))
        rs, rsb = two("rs", [P, 32]), two("rsb", [P, 16, C])
        xn, osb = two("xn", [P, CHUNK * W]), two("osb", [P, CHUNK * W])
        psL = ctx.enter_context(nc.psum_tensor("iv_psL", [P, 2, 512], F32))
        psY, psV, psR, psS, psP, psX = (k.ps("iv_ps" + n, ctx) for n in "YVRSPX")
        block = ctx.enter_context(nc.Block())
        out_v = OUT.rearrange("b c (j p i r) w -> b j p i c (r w)", j=2, p=2, i=2 * ITERS)

        def copy_rt(copy, j, u):
            hj, og = j // 4, j % 4
            return copy(rt[HID * hj:HID * hj + HID, 8 * og + u:8 * og + u + 7:2, :],
                        (psP, psX)[j % 2][HID * u:HID * u + HID, :].rearrange("q (o h) -> q o h", h=P))

        @block.sync
        def _(sp):
            prime(sp, *S.values())
            for u in range(2):
                sp.sem_inc(out_stored[u], 64)

            def load_modes(b):
                sp.wait_ge(S["cond_done"], done(b - 1))
                sp.wait_ge(S["td_done"], done(2 * b - 1))
                sp.dma_start(xfk[:, :, :, :].rearrange("q a m o -> q (a m o)").rearrange("q (m n) -> q m n", m=8),
                             k.xfd[:, bass.ds(b, 1)].rearrange("m a r k g o -> (a r k) m (g o)")).then_inc(XF_LOADED, 16)

            def store(b):
                with sp.Fori(0, ITERS) as i:
                    for u in range(2):
                        sp.wait_ge(S["out_done"], done(b * NSTEP + i * STEPS + 2 * u + 1))
                        for q in range(4):
                            sp.dma_start(out_v[bass.ds(b, 1), q % 2, q // 2, bass.ds(i * 2 + u, 1)]
                                         .rearrange("a e c n -> (a e c) n"), osb[u][32 * q:32 * q + 32, :])\
                              .then_inc(out_stored[u], 16)
            load_modes(0)
            with sp.Fori(0, B - 1) as b:
                load_modes(b + 1)
                store(b)
            store(B - 1)
            for u in range(2):
                sp.wait_ge(out_stored[u], B * ITERS * 64 + 64)

        @block.tensor
        def _(pe):
            def image(b):
                for name, lag in (("g2_done", 2), ("yc_done", 3)):
                    pe.wait_ge(S[name], done(b * NSTEP - 1 - lag))
                pe.wait_ge(S["tp_copied"], done(b * ITERS - 1))
                pe.wait_ge(S["aw_copied"], done(b - 1))
                pe.wait_ge(XF_LOADED, (b + 1) * 16)
                pe.sem_inc(S["held"], 1)
                for m in range(M):
                    last = pe.matmul(psX[0:C, 4 * m:4 * m + 4], xfk[:, m // 16, m % 16, :], t["cond_h"][:, :],
                                     start=True, stop=True)
                last.then_inc(S["cond_done"], 1)
                for ri in range(2):
                    for mj in range(2):
                        last = pe.matmul(psL[HID * mj:HID * mj + HID, ri, :], t["hi2"][:, ri, :],
                                         xfk[:, mj, :, :].rearrange("q m o -> q (m o)"), start=True, stop=True)
                    last.then_inc(S["td_done"], 1)
                pe.wait_ge(S["cond_copied"], done(b))
                for mj in range(2):
                    for ri in range(2):
                        last = pe.matmul(psY[HID * mj:HID * mj + HID, 0:16], t["hi0"][:, ri, :], ch[:, ri, mj, :],
                                         start=ri == 0, stop=ri == 1)
                last.then_inc(S["ah_done"], 1)
                pe.wait_ge(S["td_copied"], done(2 * b + 1))

                def hidden(j):
                    pe.wait_ge(S["hg0_done"], done(8 * b + j))
                    pe.wait_ge(S["hg1_done"], done(8 * b + j - 2))
                    pe.matmul(psL[:, j % 2, :], t["hi1"][:, :], ha[:, 2 * j:2 * j + 2, :].rearrange("q a h -> q (a h)"),
                              start=True, stop=True).then_inc(S["hl1_done"], 1)
                hidden(0)
                hidden(1)
                for j in range(8):
                    if j + 2 < 8:
                        hidden(j + 2)
                    pe.wait_ge(S["hg1_done"], done(8 * b + j))
                    pe.wait_ge(S["r_copied"], done(8 * b + j - 2))
                    for u in range(2):
                        last = pe.matmul((psP, psX)[j % 2][:, u * H:u * H + H], td[:, 2 * j + u, :, :, :].rearrange("q a r o -> q (a r o)"),
                                         hb[:, 2 * j + u, :], start=True, stop=True)
                    last.then_inc(S["r_done"], 1)
                pe.wait_ge(S["r_copied"], done(8 * b + 7))
                for mp in range(16):
                    last = pe.matmul(psY[0:HID + C, 0:H], t["cond_y_w"][:, mp, :], R[:, mp, :], start=mp == 0, stop=mp == 15)
                last.then_inc(S["aw_done"], 1)
                for j in range(8):
                    hj, mg = j // 4, j % 4
                    pe.wait_ge(S["rh_copied"], done(8 * b + j - 2))
                    for a in range(4):
                        mp = 4 * mg + a
                        last = pe.matmul(psL[:, j % 2, a * P:a * P + P], R[:, mp, hj * P:hj * P + P], t["mix_bd"][:, :],
                                         start=True, stop=True)
                    last.then_inc(S["rh_done"], 1)
                for j in range(8):
                    hj, og = j // 4, j % 4
                    pe.wait_ge(S["rh_copied"], done(8 * b + 7))
                    pe.wait_ge(S["rt_copied"], done(8 * b + j - 2))
                    pe.wait_ge(S["rt_half_copied"], done(8 * b + j - 2))
                    for a in range(4):
                        o = 8 * og + 2 * a
                        last = pe.transpose((psP, psX)[j % 2][:, a * P:a * P + P],
                                            rh[:, hj, o:o + 2, :].rearrange("q o j -> q (o j)"), t["ident"][:, :])
                    last.then_inc(S["rt_done"], 1)
                pe.wait_ge(S["rt_copied"], done(8 * b + 7))
                pe.wait_ge(S["rt_half_copied"], done(8 * b + 7))
                pe.wait_ge(S["aw_copied"], done(b))

            def step(st):
                if st.s == 3 and st.live(3):
                    pe.wait_ge(S["tp_copied"], done(st.it(3) - 1))
                    h0 = st.row(3)
                    w = rt[:, :, :].rearrange("q o (p h) -> q h p o", p=2)
                    w = w[:, bass.ds(h0, 8)] if not isinstance(h0, int) else w[:, h0:h0 + 8]
                    pe.matmul(psP[:, :].rearrange("q (h p o) -> q h p o", h=8, p=2), t["wi2"][:, :], w,
                              start=True, stop=True).then_inc(S["tp_done"], 1)
                if st.live(7):
                    n, u = st.n(7), st.slot(7, 2)
                    pe.wait_ge(S["rb_done"], done(n))
                    pe.wait_ge(S["yn_done"], done(n - 1))
                    for a in range(4):
                        last = pe.matmul(psR[:, a * P:a * P + P], rsb[u][:, 4 * a:4 * a + 4, :].rearrange("q l o -> q (l o)"),
                                         t["ident"][:, :], start=True, stop=True)
                    last.then_inc(S["bc_done"], 1)
                if st.live(2):
                    n, u = st.n(2), st.slot(2, 2)
                    pe.wait_ge(S["g1_done"], done(n))
                    pe.wait_ge(S["g2_done"], done(n - 1))
                    for p in range(2):
                        last = pe.matmul(psL[:, p, :], t["wi1"][:, :], wg1[u][:, p, :, :].rearrange("q r w -> q (r w)"),
                                         start=True, stop=True)
                    last.then_inc(S["l1_done"], 1)
                if st.live(3):
                    n, u, c = st.n(3), st.slot(3, 2), st.slot(3, 4)
                    pe.wait_ge(S["g2_done"], done(n))
                    pe.wait_ge(S["yc_done"], done(n - 1))
                    pe.wait_ge(S["tp_copied"], done(st.it(3)))
                    for r in range(ROWS):
                        for p in range(2):
                            last = pe.matmul(psY[HID * p:HID * p + HID, r * W:r * W + W],
                                             tp[:, ROWS * c + r, p, :, :].rearrange("q j o -> q (j o)"),
                                             wg2[u][:, p, r, :], start=True, stop=True)
                    last.then_inc(S["y_done"], 1)
                if st.live(8):
                    n, c = st.n(8), st.slot(8, 4)
                    if c % 2 == 0:
                        pe.wait_ge(xn_loaded[c // 2], (st.it(8) + 1) * 16)
                    pe.wait_ge(S["t_done"], done(n - 1))
                    pe.matmul(psS[:, :], t["sc"][:, :], xn[c // 2][:, (c % 2) * N:(c % 2) * N + N],
                              start=True, stop=True).then_inc(S["sc_done"], 1)
                if st.live(4):
                    n, u = st.n(4), st.slot(4, 2)
                    pe.wait_ge(S["sq_done"], done(n))
                    if u == 0:
                        pe.wait_ge(S["rs_done"], done(st.pair(4) - 1))
                    for a in range(4):
                        last = pe.matmul(psV[:, 16 * u + 4 * a:16 * u + 4 * a + 4], sq[u][:, a * P:a * P + P], t["lane_avg"][:, :],
                                         start=True, stop=True)
                    last.then_inc(S["var_done"], 1)

            all_steps(pe, B, image, step, 9)

        @block.scalar
        def _(act):
            def image(b):
                act.wait_ge(S["ah_copied"], done(b))
                act.wait_ge(S["rt_done"], done(8 * b - 1))
                act.wait_ge(S["r_done"], done(8 * b - 1))

                def first(j):
                    for mp in (2 * j, 2 * j + 1):
                        last = act.activation(ha[:, mp, :], t["hc_row"][:, :], ACT.Gelu, scale=t["hi0_c"][:, :], bias=ah[:, mp:mp + 1])
                    last.then_inc(S["hg0_done"], 1)
                first(0)
                first(1)
                for j in range(8):
                    if j + 2 < 8:
                        first(j + 2)
                    act.wait_ge(S["hl1_done"], done(8 * b + j))
                    act.activation(hb[:, 2 * j:2 * j + 2, :].rearrange("q a h -> q (a h)"), psL[:, j % 2, :],
                                   ACT.Gelu, bias=t["hi1_b"][:, :]).then_inc(S["hg1_done"], 1)
                for j in range(8):
                    hj, mg = j // 4, j % 4
                    act.wait_ge(S["rh_done"], done(8 * b + j))
                    act.wait_ge(S["hl1_done"], done(8 * b + 7))
                    act.copy(rh[:, hj, :, 16 * mg:16 * mg + 16].rearrange("q o c -> q c o"),
                             psL[:, j % 2, :].rearrange("q (c o) -> q c o", o=C)).then_inc(S["rh_copied"], 1)
                act.wait_ge(S["tp_done"], done(b * ITERS - 1))
                for j in range(8):
                    act.wait_ge(S["rt_done"], done(8 * b + j))
                    copy_rt(act.copy, j, 1).then_inc(S["rt_half_copied"], 1)

            def step(st):
                if st.s % 2 == 0 and st.live(6):
                    u = st.slot(6, 4) // 2
                    act.wait_ge(S["sc_done"], done(st.n(9)))
                    act.wait_ge(S["res_done"], done(st.n(9)))
                    act.dma_start(xn[u][:, :], k.xnd[bass.ds(st.b * (2 * ITERS) + 2 * st.i + (st.s - 6) // 2, 1)]
                                  .rearrange("a p n -> (a p) n")).then_inc(xn_loaded[u], 16)
                if st.live(1):
                    n, u = st.n(1), st.slot(1, 2)
                    act.wait_ge(S["pre_done"], done(n))
                    act.wait_ge(S["l1_done"], done(n - 2))
                    act.activation(wg1[u][:, :, :, :].rearrange("q p r w -> q (p r w)"),
                                   pre[u][:, :, :, :].rearrange("q p r w -> q (p r w)"), ACT.Gelu).then_inc(S["g1_done"], 1)
                if st.live(8):
                    n, u = st.n(8), st.slot(8, 2)
                    act.wait_ge(S["yn_done"], done(n))
                    act.wait_ge(S["t_done"], done(n - 2))
                    act.activation(gy[u][:, :], yn[u][:, :], ACT.Gelu, scale=t["ln_g"][:, :], bias=t["ln_b"][:, :])\
                       .then_inc(S["gy_done"], 1)
                if st.live(10):
                    n, u = st.n(10), st.slot(10, 2)
                    act.wait_ge(S["t_done"], done(n))
                    act.wait_ge(S["out_done"], done(n - 2))
                    act.activation(gs[u][:, :], tt[u][:, :], ACT.Gelu, bias=t["sc_b"][:, :]).then_inc(S["gs_done"], 1)
                if st.live(2):
                    n, u = st.n(2), st.slot(2, 2)
                    act.wait_ge(S["l1_done"], done(n))
                    act.wait_ge(S["y_done"], done(n - 2))
                    act.activation(wg2[u][:, :, :, :].rearrange("q p r w -> q (p r w)"),
                                   psL[:, :, :].rearrange("q p n -> q (p n)"), ACT.Gelu, bias=t["wi1_b"][:, :]).then_inc(S["g2_done"], 1)
                if st.live(6):
                    n, u = st.n(6), st.slot(6, 2)
                    act.wait_ge(S["rs_done"], done(st.pair(6)))
                    act.wait_ge(S["bc_done"], done(n - 2))
                    act.copy(rsb[u][:, :, :], rs[st.slot(6, 4) // 2][:, 16 * u:16 * u + 16].unsqueeze(2).broadcast_to([P, 16, C]))\
                       .then_inc(S["rb_done"], 1)

            all_steps(act, B, image, step, 11)

        @block.vector
        def _(v):
            def image(b):
                v.wait_ge(S["cond_done"], done(b))
                c_ps = psX[0:C, 0:P].rearrange("q (a m f) -> q f a m", a=2, f=4)
                v.wait_ge(S["ah_done"], done(b - 1))
                v.tensor_scalar(ch[:, :, :, :].rearrange("q r a m -> q r (a m)"),
                                psX[0:C, 0:P].rearrange("q (m f) -> q f m", f=4)[:, 0:2, :], t["comp_h_b"][:, :], None, ALU.add)
                v.wait_ge(S["r_copied"], done(8 * b - 1))
                for mj in range(2):
                    for ri in range(2):
                        q = 2 * mj + ri
                        last = v.tensor_copy(tb_row[C * q:C * q + C, :], c_ps[:, 2 + ri, mj, :])
                last.then_inc(S["cond_copied"], 1)
                v.wait_ge(S["r_done"], done(8 * b - 1))
                for ri in range(2):
                    v.wait_ge(S["td_done"], done(2 * b + ri))
                    for mj in range(2):
                        r = slice(HID * mj, HID * mj + HID)
                        last = v.tensor_copy(td[r, :, mj, ri, :], psL[r, ri, :].rearrange("q (m o) -> q m o", o=C))
                    last.then_inc(S["td_copied"], 1)
                v.wait_ge(S["ah_done"], done(b))
                v.wait_ge(S["hg0_done"], done(8 * b - 1))
                v.tensor_scalar(ah[:, :], psY[:, 0:16], t["hi0_b"][:, :], None, ALU.add).then_inc(S["ah_copied"], 1)
                v.wait_ge(S["rh_done"], done(8 * b - 1))
                v.wait_ge(S["cond_copied"], done(b))
                for j in range(8):
                    v.wait_ge(S["r_done"], done(8 * b + j))
                    for u in range(2):
                        last = v.tensor_scalar(R[:, 2 * j + u, :], (psP, psX)[j % 2][:, u * H:u * H + H],
                                               tb_row[:, 2 * j + u:2 * j + u + 1], None, ALU.add)
                    last.then_inc(S["r_copied"], 1)
                v.wait_ge(S["aw_done"], done(b))
                v.wait_ge(S["pre_done"], done(b * NSTEP - 1))
                v.wait_ge(S["yb_set"], done(b - 1))
                for hj in range(2):
                    v.tensor_scalar(aw[HID * hj:HID * hj + HID, :], psY[0:HID, hj * P:hj * P + P], wi0_const, None, ALU.add)
                for q in range(4):
                    h0 = (q % 2) * P + (q // 2) * HP
                    last = v.tensor_scalar(yb_next[C * q:C * q + C, :], psY[HID:HID + C, h0:h0 + HP], y_const, None, ALU.add)
                last.then_inc(S["aw_copied"], 1)
                v.wait_ge(S["tp_done"], done(b * ITERS - 1))
                for j in range(8):
                    v.wait_ge(S["rt_done"], done(8 * b + j))
                    copy_rt(v.tensor_copy, j, 0).then_inc(S["rt_copied"], 1)

            wi0_const, y_const = t["wi0_const"][0:HID, :], t["y_const"][HID:HID + C, :]

            def newton(y):
                ops = [lambda: v.tensor_scalar(xv[:, :], psV[:, 0:32], 1e-5, None, ALU.add),
                       lambda: v.tensor_scalar(y.bitcast(I32), xv[:, :].bitcast(I32), -0.5, MAGIC, ALU.mult, ALU.add),
                       lambda: v.tensor_scalar(xh[:, :], xv[:, :], -0.5, None, ALU.mult)]
                for _ in range(3):
                    ops += [lambda: v.tensor_tensor(nt[:, :], y, y, ALU.mult),
                            lambda: v.tensor_tensor(nt[:, :], nt[:, :], xh[:, :], ALU.mult),
                            lambda: v.scalar_tensor_tensor(y, nt[:, :], 1.5, y, ALU.add, ALU.mult)]
                return ops

            def step(st):
                if st.opens_image(8):
                    v.wait_ge(S["res_done"], done(st.n(9)))
                    v.tensor_copy(ivm[:, 0:1], t["invs"][:, bass.ds(st.b, 1)])
                    v.tensor_copy(ivm[:, 1:2], t["mean1"][:, bass.ds(st.b, 1)]).then_inc(S["ivm_set"], 1)
                if st.s == 3 and st.live(3):
                    v.wait_ge(S["tp_done"], done(st.it(3)))
                    v.wait_ge(S["y_done"], done(st.n(4)))
                    for hj in range(2):
                        r = slice(HID * hj, HID * hj + HID)
                        last = v.tensor_copy(tp[r, :, :, hj, :].rearrange("q h p o -> q (h p) o"),
                                             psP[r, :].rearrange("q (a o) -> q a o", o=C))
                    last.then_inc(S["tp_copied"], 1)
                if st.s % 2 == 0 and st.live(6):
                    pair, y = st.pair(6), rs[st.slot(6, 4) // 2][:, :]
                    v.wait_ge(S["var_done"], done(st.n(5)))
                    v.wait_ge(S["rb_done"], done(st.n(9)))
                    ops = newton(y)
                    for j, op in enumerate(ops):
                        if j:
                            v.wait_ge(S["newton"], pair * (len(ops) - 1) + j + PRIME)
                        else:
                            v.wait_ge(S["rs_done"], done(pair - 1))
                        op().then_inc(S["newton"] if j < len(ops) - 1 else S["rs_done"], 1)
                if st.live(7):
                    n, c, u = st.n(7), st.slot(7, 4), st.slot(7, 2)
                    v.wait_ge(S["bc_done"], done(n))
                    v.wait_ge(S["gy_done"], done(n - 2))
                    v.wait_ge(S["yc_done"], done(n))
                    v.tensor_tensor(yn[u][:, :], yc[c][:, :], psR[:, :], ALU.mult).then_inc(S["yn_done"], 1)
                if st.live(9):
                    n, u = st.n(9), st.slot(9, 2)
                    v.wait_ge(S["gy_done"], done(n))
                    v.wait_ge(S["sc_done"], done(n))
                    v.wait_ge(S["gs_done"], done(n - 2))
                    v.tensor_tensor(tt[u][:, :], gy[u][:, :], psS[:, :], ALU.add).then_inc(S["t_done"], 1)
                if st.opens_image(3):
                    v.wait_ge(S["yc_done"], done(st.n(4)))
                    v.wait_ge(S["aw_copied"], done(st.b))
                    v.tensor_copy(yb[:, :], yb_next[:, :]).then_inc(S["yb_set"], 1)
                    v.wait_ge(S["yb_set"], done(st.b))
                if st.live(3):
                    n, c = st.n(3), st.slot(3, 4)
                    v.wait_ge(S["y_done"], done(n))
                    v.wait_ge(S["yn_done"], done(n - 4))
                    v.wait_ge(S["sq_done"], done(n - 4))
                    h0 = st.row(3)
                    bias = yb[:, bass.ds(h0, ROWS)] if not isinstance(h0, int) else yb[:, h0:h0 + ROWS]
                    v.tensor_tensor(yc[c][:, :].rearrange("q (r w) -> q r w", r=ROWS), psY[:, :].rearrange("q (r w) -> q r w", r=ROWS),
                                    bias.unsqueeze(2).broadcast_to([P, ROWS, W]), ALU.add).then_inc(S["yc_done"], 1)
                if st.live(11):
                    n, c, u = st.n(11), st.slot(11, 4), st.slot(11, 2)
                    v.wait_ge(S["gs_done"], done(n))
                    v.wait_ge(S["res_done"], done(n))
                    if c % 2 == 0:
                        v.wait_ge(out_stored[c // 2], (st.it(11) + 1) * 64)
                    v.tensor_tensor(osb[c // 2][:, (c % 2) * N:(c % 2) * N + N], res[c][:, :], gs[u][:, :], ALU.add)\
                     .then_inc(S["out_done"], 1)

            v.memset(td[:, :, :, :, :], 0.0)
            v.memset(tp[:, :, :, :, :], 0.0)
            v.tensor_scalar(wc_w[:, :], t["wc_row"][:, :], t["wi0_c"][:, :], None, ALU.mult).then_inc(zeroed, 1)
            v.wait_ge(zeroed, 1)
            all_steps(v, B, image, step, 12)

        @block.gpsimd
        def _(g):
            def image(b):
                g.wait_ge(S["aw_copied"], done(b))

            def step(st):
                if st.live(8):
                    n, c = st.n(8), st.slot(8, 4)
                    if st.opens_image(8):
                        g.wait_ge(S["ivm_set"], done(st.b))
                    if c % 2 == 0:
                        g.wait_ge(xn_loaded[c // 2], (st.it(8) + 1) * 16)
                    g.wait_ge(S["out_done"], done(n - 4))
                    g.sem_inc(S["held"], 1)
                    g.tensor_scalar(res[c][:, :], xn[c // 2][:, (c % 2) * N:(c % 2) * N + N], ivm[:, 0:1], ivm[:, 1:2],
                                    ALU.mult, ALU.add).then_inc(S["res_done"], 1)
                if st.live(0):
                    n, u = st.n(0), st.slot(0, 2)
                    g.wait_ge(S["g1_done"], done(n - 2))
                    h0 = st.row(0)
                    a = aw[:, :].rearrange("q (p h) -> q p h", p=2)
                    a = a[:, :, bass.ds(h0, ROWS)] if not isinstance(h0, int) else a[:, :, h0:h0 + ROWS]
                    g.tensor_tensor(pre[u][:, :, :, :], wc_w[:, :].unsqueeze(1).unsqueeze(1).broadcast_to([P, 2, ROWS, W]),
                                    a.unsqueeze(3).broadcast_to([P, 2, ROWS, W]), ALU.add).then_inc(S["pre_done"], 1)
                if st.live(3):
                    n, c, u = st.n(3), st.slot(3, 4), st.slot(3, 2)
                    g.wait_ge(S["yc_done"], done(n))
                    g.wait_ge(S["var_done"], done(n - 2))
                    g.tensor_tensor(sq[u][:, :], yc[c][:, :], yc[c][:, :], ALU.mult).then_inc(S["sq_done"], 1)

            g.wait_ge(zeroed, 1)
            all_steps(g, B, image, step, 9)


def build(nc, a, out):
    with ExitStack() as ctx:
        k = Kit(nc, ctx, a, out)
        B = k.B
        k.zd = nc.dram_tensor("zd", (4, 4, B, 8, 8, M), F32).ap()
        k.vd = nc.dram_tensor("vd", (B, M, HP, P), F32).ap()
        k.xnd = nc.dram_tensor("xnd", (B * 2 * ITERS, P, CHUNK * W), F32).ap()
        k.xfd = nc.dram_tensor("xfd", (8, B, 2, M, 4, C), F32).ap()
        setup(k)
        for n in ("mean1", "invs", "s1"):
            k.sb(n, [P, B])
        with ExitStack() as c0:
            k.sb("XM", [P, 2 * 8 * M, B], F32, c0)
            k.sb("MV", [P, B, 16, 2], F32, c0)
            dht(k)
            mix0(k)
        rows0(k)
        with ExitStack() as c1:
            k.sb("XH", [P, 8 * 2 * M, B], F32, c1)
            forward(k)
            mix1(k)
        inverse(k)


def weight_layouts(w):
    f = np.float32
    t = {n: np.zeros(s, f) for n, s in TABLES.items()}
    n, kk = np.arange(W), np.arange(M)
    ang = 2 * np.pi * ((n[:, None] * kk[None, :]) % W) / W
    cas = (np.cos(ang) + np.sin(ang)).astype(f)
    flip = (-kk) % M
    t["cas_n"][:, :, :M] = cas.reshape(2, P, M).transpose(1, 0, 2)
    t["cas_n"][:, :, 2 * M:] = t["cas_n"][:, :, :M]
    t["cas_n"][:, :, M:2 * M] = cas[:, flip].reshape(2, P, M).transpose(1, 0, 2)
    t["cas_k"][:] = cas.T
    for j in range(4):
        t["cas_bd"][32 * j:32 * j + 32, H * j:H * j + H] = cas.T.reshape(8, 4, H).transpose(1, 0, 2).reshape(M, H)
    t["ident"][:] = np.eye(P, dtype=f)
    c = np.arange(P) % C
    t["chan_mask"][:] = c[:, None] // 2 == np.arange(16)[None, :]
    t["group_avg"][:] = (c[:, None] // 2 == c[None, :] // 2) * f(1 / 8)
    t["ones_avg"][:] = f(1 / P)
    t["lane_avg"][:] = (np.arange(P)[:, None] // C == np.arange(4)[None, :]) * f(1 / C)

    def two(m):
        r, q = m.shape
        z = np.zeros((2 * r, 2 * q), f)
        z[:r, :q] = m
        z[r:, q:] = m
        return z

    for name in ("bw", "bh"):
        for p in range(2):
            for hj in range(2):
                q = 2 * p + hj
                t[name + "0"][32 * q:32 * q + 32, p, HID * hj:HID * hj + HID] = w[name + "0_w"][:C]
    for name in ("bw", "bh", "hi", "wi"):
        t[name + "1"][:] = two(w[name + "1_w"])
        t[name + "0_b"][:, 0] = np.tile(w[name + "0_b"], 2)
    for name in ("hi", "wi"):
        t[name + "1_b"][:, 0] = np.tile(w[name + "1_b"], 2)
        t[name + "0_c"][:, 0] = np.tile(w[name + "0_w"][0], 2)
    t["bw2"][:] = np.tile(w["bw2_w"], (2, 1))
    t["bw2_b"][:] = w["bw2_b"][None, :]
    bh2 = np.concatenate([w["bh2_w"], w["bh2_b"][None, :]], 0)
    t["bh2"][:, 0] = bh2
    t["bh2"][:, 1] = np.concatenate([bh2[:, M:], bh2[:, :M]], 1)
    ch, b2 = w["comp_h_w"], w["hi2_b"]
    t["cond_h"][:M, 0] = ch
    t["cond_h"][M:, 1] = ch
    t["cond_h"][:, 2] = b2
    t["cond_h"][:M, 3] = b2[M:]
    t["cond_h"][M:, 3] = b2[:M]
    t["comp_h_b"][:] = w["comp_h_b"][None, :]
    t["hi0"][:] = w["hi0_w"][1:].reshape(2, C, HID).transpose(1, 0, 2)
    hc = np.linspace(-1.0, 1.0, H, dtype=f)
    t["hc_row"][:] = hc[None, :]
    t["wc_row"][:] = hc[None, :]
    t["hi2"][:, 0] = w["hi2_w"].T
    t["hi2"][:M, 1] = w["hi2_w"].T[M:]
    t["hi2"][M:, 1] = w["hi2_w"].T[:M]
    t["wi0"][:] = np.tile(w["wi0_w"][1:], (2, 1))
    t["wi0_sum"][:] = np.tile(w["wi0_w"][1:], (1, 2))
    t["comp_w_b"][:] = w["comp_w_b"][None, :]
    place = np.array([[(mp % 4) * 8 + mj * 4 + mp // 4 for mp in range(16)] for mj in range(2)])
    t["comp_w"][:] = np.repeat(w["comp_w_w"][place], HID, 0)
    t["mixer"][:] = np.tile(w["mixer_w"].T, (4, 1))
    t["mixer_b"][:] = w["mixer_b"][None, :]
    t["mixer_own"][:, 0] = np.tile(w["mixer_b"], 4)
    b2 = w["wi2_b"].reshape(2, M)[:, place]
    t["wi2_b"][:] = np.repeat(b2.transpose(1, 0, 2).reshape(4, 16), C, 0)
    w2 = w["wi2_w"].reshape(HID, 2, M)[:, :, place].transpose(3, 2, 1, 0).reshape(HID, HID)
    t["wi2"][:] = two(w2)
    t["sc"][:] = two(two(w["sc_w"].T))
    for name, src in (("sc_b", "sc_b"), ("ln_g", "ln_g"), ("ln_b", "ln_b")):
        t[name][:, 0] = np.tile(w[src], 4)
    t["coord_w"] = np.tile(w["bw0_w"][C], (9, 2))
    t["coord_wc"] = np.tile(hc, (9, ROWS))
    t["coord_h"] = np.tile(w["bh0_w"][C], (9, 2))
    t["coord_hc"] = np.tile(hc.reshape(1, H), (9, 1))
    t["bias_bw1"] = np.tile(w["bw1_b"], (9, 8))
    t["bias_bh1"] = np.tile(w["bh1_b"], (9, 8))
    w0 = w["l0"]
    both = np.stack([w0, w0[:, :, flip][:, :, :, flip]], 0)
    t["l0_w"] = both.reshape(2, C, C, 8, 4, M).transpose(3, 4, 1, 0, 5, 2).reshape(8, P, 2, M, C)
    wf = np.stack([w["wf_real"], w["wf_imag"]], 0).reshape(2, C, C, M, 4, 8)
    t["l1_w"] = wf.transpose(5, 4, 2, 3, 0, 1).reshape(8, P, M, 2, C)
    return {n: np.ascontiguousarray(v, dtype=f) for n, v in t.items()}


def kernel(**inputs):
    import concourse.bacc as bacc
    from concourse.bass_utils import run_bass_kernel_spmd as run

    w = {n[len("L1_conv_"):]: np.asarray(v) for n, v in inputs.items() if n.startswith("L1_conv_")}
    w["l0"] = np.asarray(inputs["L0_conv_weights1"])
    arrays = weight_layouts(w)
    arrays["x"] = np.asarray(inputs["x"])
    nc = bacc.Bacc("TRN2", target_bir_lowering=False, num_devices=1)
    a = {n: nc.dram_tensor("in_" + n, v.shape, mybir.dt.from_np(v.dtype), kind="ExternalInput").ap()
         for n, v in arrays.items()}
    out = nc.dram_tensor("out", arrays["x"].shape, F32, kind="ExternalOutput").ap()
    build(nc, a, out)
    r = run(nc, [{"in_" + n: v for n, v in arrays.items()}], core_ids=[0])
    return r.results[0]["out"]
```

```python
import numpy as np
import concourse.bass as bass
from concourse import mybir
from contextlib import ExitStack

F32 = mybir.dt.float32

I32 = mybir.dt.int32
ACT = mybir.ActivationFunctionType
ALU = mybir.AluOpType
AX = mybir.AxisListType

C, H, W, M, HID = 32, 256, 256, 32, 64
P = 128
NPX = H * W
HP = 64
ROWS = 2
CHUNK = 4
STEPS = 4
ITERS = HP // (ROWS * STEPS)
PRIME = 12
MAGIC = 1597463007.0


def done(step):
    return step + 1 + PRIME


class Kit:

    def __init__(self, nc, ctx, a, out):
        self.nc, self.ctx, self.a, self.out = nc, ctx, a, out
        self.B = a["x"].shape[0]
        self.t = {}

    def sb(self, name, shape, dt=F32, ctx=None):
        t = (ctx or self.ctx).enter_context(self.nc.sbuf_tensor(name, shape, dt))
        self.t[name] = t
        return t

    def ps(self, name, ctx, shape=(P, 512)):
        return ctx.enter_context(self.nc.psum_tensor(name, list(shape), F32))

    def sem(self, name):
        return self.ctx.enter_context(self.nc.semaphore(name))


def prime(eng, *sems):
    for s in sems:
        eng.sem_inc(s, PRIME)


class Chain:

    def __init__(self, eng, sem):
        self.eng, self.sem, self.n = eng, sem, 0

    def __call__(self, ins):
        ins.then_inc(self.sem, 1)
        self.n += 1
        self.eng.wait_ge(self.sem, self.n)


def rsqrt_chain(v, link, y, x, t):
    link(v.tensor_scalar(y.bitcast(I32), x.bitcast(I32), -0.5, MAGIC, ALU.mult, ALU.add))
    for _ in range(3):
        link(v.tensor_tensor(t, y, y, ALU.mult))
        link(v.tensor_tensor(t, t, x, ALU.mult))
        link(v.tensor_scalar(t, t, -0.5, 1.5, ALU.mult, ALU.add))
        link(v.tensor_tensor(y, y, t, ALU.mult))


TABLES = {
    "cas_n": (P, 2, 3 * M), "cas_k": (M, W), "cas_bd": (P, 4 * H), "ident": (P, P),
    "chan_mask": (P, 16), "group_avg": (P, P), "ones_avg": (P, P),
    "bw0": (P, 2, P), "bh0": (P, 2, P), "bw1": (P, P), "bh1": (P, P), "hi1": (P, P), "wi1": (P, P),
    "bw0_b": (P, 1), "bh0_b": (P, 1), "hi1_b": (P, 1), "wi1_b": (P, 1), "hi0_b": (P, 1), "wi0_b": (P, 1),
    "bw0_c": (P, 1), "bh0_c": (P, 1), "bw1_row": (P, HID), "bh1_row": (P, HID), "hc_rows": (P, 2, HP),
    "bw2": (P, HID), "bw2_b": (P, HID), "bh2": (HID + 1, 2, 2 * M),
    "cond_h": (2 * M, 4), "comp_h_b": (C, 1), "hi0": (C, 2, HID), "hi0_c": (P, 1), "hc_row": (P, H),
    "hi2": (2 * M, 2, HID), "wi0": (P, HID), "wi0_c": (P, 1), "wc_row": (P, W), "comp_w": (P, 16),
    "wi0_sum": (2 * C, P), "comp_w_b": (2 * C, 1), "mixer": (P, C), "mixer_b": (P, C), "mixer_own": (P, 1),
    "wi2_b": (P, 16), "wi2": (P, P), "lane_avg": (P, 4), "sc": (P, P), "sc_b": (P, 1), "ln_g": (P, 1), "ln_b": (P, 1),
}


def setup(k):
    nc, a = k.nc, k.a
    loaded, chain = k.sem("tables_loaded"), k.sem("setup_chain")
    for name, shape in TABLES.items():
        k.sb(name, list(shape))
    t = k.t
    mix_c = k.sb("mix_c", [P, C])
    mix_bd = k.sb("mix_bd", [P, P])
    cond_y_w = k.sb("cond_y_w", [P, 16, HID + C])
    wi0_const = k.sb("wi0_const", [P, 1])
    y_const = k.sb("y_const", [P, 1])
    with ExitStack() as ctx:
        mean = k.sb("setup_mean", [P, 4], F32, ctx)
        ps = k.ps("setup_ps", ctx)
        n_loads = len(TABLES)
        mm = k.sem("setup_mm")
        block = ctx.enter_context(nc.Block())

        @block.sync
        def _(sp):
            for name in TABLES:
                sp.dma_start(t[name][tuple(slice(None) for _ in TABLES[name])], a[name]).then_inc(loaded, 16)

        @block.vector
        def _(v):
            link = Chain(v, chain)
            v.wait_ge(loaded, 16 * n_loads)
            link(v.memset(mix_bd[:, :], 0.0))
            link(v.tensor_scalar(t["bh2"][:, 1, 0:M], t["bh2"][:, 1, 0:M], -1.0, None, ALU.mult))
            link(v.tensor_scalar(t["cond_h"][0:M, 3:4], t["cond_h"][0:M, 3:4], -1.0, None, ALU.mult))
            link(v.tensor_scalar(t["hi2"][0:M, 1, :], t["hi2"][0:M, 1, :], -1.0, None, ALU.mult))
            link(v.reduce_sum(mean[:, 0:1], t["mixer"][:, :], axis=AX.X))
            link(v.tensor_scalar(mean[:, 1:2], mean[:, 0:1], 1.0 / C, None, ALU.mult))
            link(v.tensor_scalar(mix_c[:, :], t["mixer"][:, :], mean[:, 1:2], 1.0 / NPX, ALU.subtract, ALU.mult))
            for q in range(4):
                r = slice(32 * q, 32 * q + 32)
                link(v.tensor_copy(mix_bd[r, r], mix_c[r, :]))
            link(v.reduce_sum(mean[:, 2:3], t["mixer_b"][:, :], axis=AX.X))
            link(v.tensor_scalar(mean[:, 3:4], mean[:, 2:3], 1.0 / C, None, ALU.mult))
            link(v.tensor_tensor(y_const[:, :], t["mixer_own"][:, :], mean[:, 3:4], ALU.subtract))
            for mp in range(16):
                v.tensor_scalar(cond_y_w[:, mp, HID:HID + C], mix_c[:, :], t["wi2_b"][:, mp:mp + 1], None, ALU.mult)
                last = v.tensor_scalar(cond_y_w[:, mp, 0:HID], t["wi0"][:, :], t["comp_w"][:, mp:mp + 1], None, ALU.mult)
            link(last)
            v.wait_ge(mm, 1)
            link(v.tensor_tensor(wi0_const[:, :], ps[:, 0:1], t["wi0_b"][:, :], ALU.add))

        @block.tensor
        def _(pe):
            pe.wait_ge(loaded, 16 * n_loads)
            pe.matmul(ps[:, 0:1], t["wi0_sum"][:, :], t["comp_w_b"][:, :], start=True, stop=True).then_inc(mm, 1)


def dht(k):
    nc, t, x, B = k.nc, k.t, k.a["x"], k.B
    CH = 4
    KEEP = t["cas_n"].shape[2]
    NJ = C // CH
    loaded = [k.sem(f"dht_x_loaded{i}") for i in range(4)]
    cols_done, a1_done, stats_done = k.sem("dht_cols_done"), k.sem("dht_a1_done"), k.sem("dht_stats_done")
    modes_done, xm_done, rows_agg, rows_kept = (k.sem(n) for n in ("dht_modes_done", "dht_xm_done", "dht_rows_agg", "dht_rows_kept"))
    XM, MV = t["XM"], t["MV"]
    with ExitStack() as ctx:
        xa = [k.sb(f"dht_x{i}", [P, CH, 2, W], F32, ctx) for i in range(4)]
        A1 = k.sb("dht_a1", [P, 2, 2 * M, C], F32, ctx)
        ST = k.sb("dht_stats", [P, C, 6], F32, ctx)
        AG = k.sb("dht_agg", [P, 16, 2], F32, ctx)
        pad = k.sb("dht_pad", [P, 1], F32, ctx)
        psA = [ctx.enter_context(nc.psum_tensor(f"dht_psA{i}", [P, 2, 512], F32)) for i in range(2)]
        psX = k.ps("dht_psX", ctx)
        block = ctx.enter_context(nc.Block())

        @block.sync
        def _(sp):
            prime(sp, cols_done, a1_done, stats_done, modes_done, xm_done, rows_agg, rows_kept)
            with sp.Fori(0, B) as b:
                for j in range(NJ):
                    sp.wait_ge(cols_done, done(b * NJ + j - 4))
                    sp.wait_ge(stats_done, done(b * NJ + j - 4))
                    sp.dma_start(xa[j % 4][:, :, :, :],
                                 x[bass.ds(b, 1), CH * j:CH * j + CH].rearrange("a c (g p) w -> p (a c) g w", p=P))\
                      .then_inc(loaded[j % 4], 16)

        @block.tensor
        def _(pe):
            with pe.Fori(0, B) as b:
                for j in range(NJ):
                    pe.wait_ge(loaded[j % 4], (b * 2 + j // 4 + 1) * 16)
                    pe.wait_ge(a1_done, done(b * NJ + j - 2))
                    ps = psA[j % 2][:, :, 0:4 * KEEP].rearrange("p k (c g n) -> p k c g n", c=2, g=2)
                    for c in range(CH):
                        for g in range(2):
                            for hh in range(2):
                                last = pe.matmul(ps[:, c // 2, c % 2, g, :], xa[j % 4][:, c, hh, g * P:g * P + P],
                                                 t["cas_n"][:, hh, :], start=hh == 0, stop=hh == 1)
                    last.then_inc(cols_done, 1)
                pe.wait_ge(a1_done, done(b * NJ + NJ - 1))
                pe.wait_ge(xm_done, done(b - 1))
                for f in range(2):
                    for kg in range(8):
                        for g in range(2):
                            last = pe.matmul(psX[:, (f * 8 + kg) * M:(f * 8 + kg + 1) * M],
                                             A1[:, g, f * M + 4 * kg:f * M + 4 * kg + 4, :],
                                             t["cas_n"][:, g, f * M:f * M + M], start=g == 0, stop=g == 1)
                last.then_inc(modes_done, 1)

        @block.scalar
        def _(act):
            with act.Fori(0, B) as b:
                for j in range(NJ):
                    act.wait_ge(cols_done, done(b * NJ + j))
                    if j == 0:
                        act.wait_ge(modes_done, done(b - 1))
                    for bank in range(2):
                        last = act.copy(A1[:, :, :, CH * j + 2 * bank:CH * j + 2 * bank + 2].rearrange("p g n c -> p c g n"),
                                        psA[j % 2][:, bank, 0:4 * KEEP].rearrange("p (c g n) -> p c g n", c=2, g=2)[:, :, :, 0:2 * M])
                    last.then_inc(a1_done, 1)
                act.wait_ge(modes_done, done(b))
                act.copy(XM[:, :, bass.ds(b, 1)], psX[:, :].rearrange("p (n a) -> p n a", a=1)).then_inc(xm_done, 1)

        @block.vector
        def _(v):
            with v.Fori(0, B) as b:
                for j in range(NJ):
                    v.wait_ge(loaded[j % 4], (b * 2 + j // 4 + 1) * 16)
                    if j == 0:
                        v.wait_ge(rows_agg, done(b - 1))
                    for c in range(CH):
                        last = v.bn_stats(ST[:, CH * j + c, :], xa[j % 4][:, c, :, :].rearrange("p g w -> p (g w)"))
                    last.then_inc(stats_done, 1)
                v.wait_ge(stats_done, done(b * NJ + NJ - 1))
                v.wait_ge(rows_kept, done(b - 1))
                v.memset(pad[:, :], 0.0)
                for g in range(16):
                    last = v.bn_aggr(AG[:, g, :], ST[:, 2 * g:2 * g + 2, :].rearrange("p a s -> p (a s)"))
                last.then_inc(rows_agg, 1)
                v.wait_ge(rows_agg, done(b))
                v.tensor_copy(MV[:, bass.ds(b, 1), :, :], AG[:, :, :].rearrange("p (a g) s -> p a g s", a=1)).then_inc(rows_kept, 1)


def select_channels(v, link, dst, src, t, tmp, B):
    link(v.tensor_tensor(tmp, src, t["chan_mask"][:, :].unsqueeze(1).broadcast_to([P, B, 16]), ALU.mult))
    link(v.reduce_sum(dst, tmp, axis=AX.X))


def mix0(k):
    nc, t, B = k.nc, k.t, k.B
    XM, MV = t["XM"], t["MV"]
    chain, st_mm, w_loaded, w_ready, w_used = (k.sem(n) for n in
                                               ("mix0_chain", "mix0_stat_mm", "mix0_w_loaded", "mix0_w_ready", "mix0_w_used"))
    zs, z_done, xn_ready, z_ready, z_stored = (k.sem(n) for n in
                                               ("mix0_z_mm", "mix0_z_copied", "mix0_xm_ready", "mix0_z_ready", "mix0_z_stored"))
    st_in = k.sem("mix0_stat_in")
    NB = B * 16
    with ExitStack() as ctx:
        Z = k.sb("Z", [P, 8, M, B], F32, ctx)
        ZB = k.sb("ZB", [P, B, 8, M], F32, ctx)
        tmp = k.sb("mix0_tmp", [P, 8, M, B], F32, ctx)
        w = [k.sb(f"mix0_w{i}", [P, 2, M, C], F32, ctx) for i in range(2)]
        wy = [k.sb(f"mix0_wy{i}", [P, 2, M, C], F32, ctx) for i in range(2)]
        sq = k.sb("mix0_sq", [P, B, 16], F32, ctx)
        mb = k.sb("mix0_mb", [P, B, 16], F32, ctx)
        s = {n: k.sb("mix0_" + n, [P, B], F32, ctx) for n in
             ("mean", "var", "r", "u", "v", "z00", "my", "cov", "vy", "p1", "p2")}
        ps = k.ps("mix0_ps", ctx)
        psZ = [k.ps(f"mix0_psZ{q}", ctx) for q in range(4)]
        block = ctx.enter_context(nc.Block())
        mean1, invs, s1 = t["mean1"], t["invs"], t["s1"]

        @block.sync
        def _(sp):
            for kg in range(8):
                if kg >= 2:
                    sp.wait_ge(w_ready, kg - 1)
                sp.dma_start(w[kg % 2][:, :, :, :], k.a["l0_w"][kg]).then_inc(w_loaded, 16)
                sp.wait_ge(w_loaded, 16 * (kg + 1))
            sp.wait_ge(z_ready, 1)
            for q in range(4):
                for oj in range(4):
                    sp.dma_start(k.zd[oj, q].rearrange("b g o w -> o (b g) w"),
                                 ZB[32 * q + oj:32 * q + 32:4, :, :, :].rearrange("o b g w -> o (b g) w")).then_inc(z_stored, 16)
            sp.wait_ge(z_stored, 256)

        @block.tensor
        def _(pe):
            def avg(n, weights, src, width):
                pe.wait_ge(st_in, n)
                pe.matmul(ps[:, 0:width], weights, src, start=True, stop=True).then_inc(st_mm, 1)
            avg(1, t["ones_avg"][:, :], mb[:, :, :].rearrange("p b g -> p (b g)"), NB)
            avg(2, t["ones_avg"][:, :], sq[:, :, :].rearrange("p b g -> p (b g)"), NB)
            pe.wait_ge(xn_ready, 1)
            for kg in range(8):
                pe.wait_ge(w_ready, kg + 1)
                if kg >= 1:
                    pe.wait_ge(z_done, kg)
                for kw in range(M):
                    for q in range(4):
                        r = slice(32 * q, 32 * q + 32)
                        for f in range(2):
                            last = pe.matmul(psZ[q][r, kw * B:kw * B + B], wy[kg % 2][r, f, kw, :],
                                             XM[r, (f * 8 + kg) * M + kw, :], start=f == 0, stop=f == 1)
                last.then_inc(zs, 1)
            avg(3, t["group_avg"][:, :], s["z00"][:, :], B)
            avg(4, t["group_avg"][:, :], s["p1"][:, :], B)
            avg(5, t["group_avg"][:, :], s["p2"][:, :], B)

        @block.scalar
        def _(act):
            for kg in range(8):
                act.wait_ge(zs, kg + 1)
                for q in range(4):
                    r = slice(32 * q, 32 * q + 32)
                    last = act.mul(Z[r, kg, :, :].rearrange("p w b -> p (w b)"), psZ[q][r, 0:M * B], 0.5 / NPX)
                last.then_inc(z_done, 1)

        @block.vector
        def _(v):
            link = Chain(v, chain)
            v.tensor_copy(mb[:, :, :], MV[:, :, :, 0]).then_inc(st_in, 1)
            v.wait_ge(st_mm, 1)
            link(v.tensor_copy(mb[:, :, :], ps[:, 0:NB].rearrange("p (b g) -> p b g", g=16)))
            select_channels(v, link, s["mean"][:, :], mb[:, :, :], t, sq[:, :, :], B)
            link(v.tensor_tensor(sq[:, :, :], MV[:, :, :, 0], mb[:, :, :], ALU.subtract))
            link(v.tensor_tensor(sq[:, :, :], sq[:, :, :], sq[:, :, :], ALU.mult))
            v.tensor_tensor(sq[:, :, :], sq[:, :, :], MV[:, :, :, 1], ALU.add).then_inc(st_in, 1)
            v.wait_ge(st_mm, 2)
            link(v.tensor_copy(mb[:, :, :], ps[:, 0:NB].rearrange("p (b g) -> p b g", g=16)))
            select_channels(v, link, s["var"][:, :], mb[:, :, :], t, sq[:, :, :], B)
            link(v.tensor_scalar(s["u"][:, :], s["var"][:, :], 1e-5, None, ALU.add))
            rsqrt_chain(v, link, s["r"][:, :], s["u"][:, :], s["v"][:, :])
            link(v.tensor_scalar(s["v"][:, :], s["mean"][:, :], float(NPX), None, ALU.mult))
            for f in range(2):
                link(v.tensor_tensor(XM[0:32, f * 8 * M, :], XM[0:32, f * 8 * M, :], s["v"][0:32, :], ALU.subtract))
            v.tensor_tensor(XM[:, :, :], XM[:, :, :], s["r"][:, :].unsqueeze(1).broadcast_to([P, 2 * 8 * M, B]), ALU.mult)\
             .then_inc(xn_ready, 1)
            for kg in range(8):
                v.wait_ge(w_loaded, 16 * (kg + 1))
                if kg >= 2:
                    v.wait_ge(zs, kg - 1)
                v.tensor_tensor(wy[kg % 2][:, 0, :, :], w[kg % 2][:, 0, :, :], w[kg % 2][:, 1, :, :], ALU.add)
                v.tensor_tensor(wy[kg % 2][:, 1, :, :], w[kg % 2][:, 0, :, :], w[kg % 2][:, 1, :, :], ALU.subtract)\
                 .then_inc(w_ready, 1)
            v.wait_ge(z_done, 8)
            v.wait_ge(xn_ready, 1)
            link(v.memset(s["z00"][:, :], 0.0))
            v.tensor_scalar(s["z00"][0:32, :], Z[0:32, 0, 0, :], 4.0, None, ALU.mult).then_inc(st_in, 1)
            v.wait_ge(st_mm, 3)
            link(v.tensor_copy(s["my"][:, :], ps[:, 0:B]))
            link(v.tensor_tensor(tmp[:, :, :, :].rearrange("p g w b -> p (g w) b"), XM[:, 0:8 * M, :],
                                 Z[:, :, :, :].rearrange("p g w b -> p (g w) b"), ALU.mult))
            link(v.reduce_sum(s["u"][:, :], tmp[:, :, :, :].rearrange("p g w b -> p b (g w)"), axis=AX.X))
            v.tensor_scalar(s["p1"][:, :], s["u"][:, :], 4.0 / NPX, None, ALU.mult).then_inc(st_in, 1)
            v.wait_ge(st_mm, 4)
            link(v.tensor_copy(s["cov"][:, :], ps[:, 0:B]))
            link(v.tensor_copy(tmp[:, :, :, :], Z[:, :, :, :]))
            link(v.tensor_tensor(tmp[0:32, 0, 0, :], tmp[0:32, 0, 0, :], s["my"][0:32, :], ALU.subtract))
            link(v.tensor_tensor(tmp[:, :, :, :], tmp[:, :, :, :], tmp[:, :, :, :], ALU.mult))
            link(v.reduce_sum(s["u"][:, :], tmp[:, :, :, :].rearrange("p g w b -> p b (g w)"), axis=AX.X))
            v.tensor_scalar(s["p2"][:, :], s["u"][:, :], 4.0, None, ALU.mult).then_inc(st_in, 1)
            v.wait_ge(st_mm, 5)
            link(v.tensor_copy(s["vy"][:, :], ps[:, 0:B]))
            link(v.tensor_scalar(s["u"][:, :], s["var"][:, :], 1e-5, None, ALU.add))
            link(v.tensor_tensor(s["u"][:, :], s["u"][:, :], s["r"][:, :], ALU.mult))
            link(v.tensor_tensor(s["cov"][:, :], s["cov"][:, :], s["u"][:, :], ALU.mult))
            link(v.tensor_scalar(s["cov"][:, :], s["cov"][:, :], 2.0, 1e-5, ALU.mult, ALU.add))
            link(v.tensor_tensor(s["cov"][:, :], s["cov"][:, :], s["var"][:, :], ALU.add))
            link(v.tensor_tensor(s["u"][:, :], s["cov"][:, :], s["vy"][:, :], ALU.add))
            rsqrt_chain(v, link, s1[:, :], s["u"][:, :], s["v"][:, :])
            link(v.tensor_tensor(invs[:, :], s["u"][:, :], s1[:, :], ALU.mult))
            link(v.tensor_tensor(mean1[:, :], s["mean"][:, :], s["my"][:, :], ALU.add))
            link(v.tensor_tensor(s["v"][:, :], mean1[:, :], s1[:, :], ALU.mult))
            link(v.tensor_tensor(ZB[:, :, :, :].rearrange("p b g w -> p b (g w)"),
                                 Z[:, :, :, :].rearrange("p g w b -> p b (g w)"),
                                 s1[:, :].unsqueeze(2).broadcast_to([P, B, 8 * M]), ALU.mult))
            v.tensor_tensor(ZB[0:32, :, 0, 0], ZB[0:32, :, 0, 0], s["v"][0:32, :], ALU.subtract).then_inc(z_ready, 1)


def rows0(k):
    nc, t, B = k.nc, k.t, k.B
    z_loaded = [k.sem(f"rows0_z_loaded{i}") for i in range(2)]
    v_stored = [k.sem(f"rows0_v_stored{i}") for i in range(2)]
    mm_done = k.sem("rows0_mm_done")
    copied = [k.sem(f"rows0_copied_{n}") for n in ("act", "dve")]
    GR = 4
    with ExitStack() as ctx:
        ZT = [k.sb(f"ZT{i}", [P, 8, M], F32, ctx) for i in range(2)]
        V = [k.sb(f"V{i}", [M, HP, P], F32, ctx) for i in range(2)]
        ps = [k.ps(f"rows0_ps{i}", ctx) for i in range(GR)]
        block = ctx.enter_context(nc.Block())

        def image(b, u):
            return b * 2 + u

        def copies(eng, copy, bh, u, half):
            eng.wait_ge(v_stored[u], bh * 16 + 16)
            for n in range(half, GR, 2):
                eng.wait_ge(mm_done, image(bh, u) * GR + n + 1 + PRIME)
                for g in range(4):
                    c0 = (4 * (n // 2) + g) * 4 + 2 * (n % 2)
                    dst = V[u][:, :, :].rearrange("k h (p j c) -> k c j p h", p=2, j=2)
                    src = ps[n][M * g:M * g + M, :].rearrange("k (c j p h) -> k c j p h", c=2, j=2, p=2)
                    for hj in range(2):
                        last = copy(dst[:, c0:c0 + 2, hj, :, :], src[:, :, hj, :, :])
                last.then_inc(copied[half], 1)

        @block.sync
        def _(sp):
            prime(sp, mm_done, *copied)
            for u in range(2):
                sp.sem_inc(v_stored[u], 16)
            with sp.Fori(0, B // 2) as bh:
                for u in range(2):
                    if u == 0:
                        sp.wait_ge(mm_done, bh * (2 * GR) + PRIME)
                    sp.dma_start(ZT[u][:, :, :],
                                 k.zd[:, :, bass.ds(bh * 2 + u, 1)].rearrange("j q a g o w -> (j q a) g (o w)"))\
                      .then_inc(z_loaded[u], 16)
                for u in range(2):
                    for done_copies in copied:
                        sp.wait_ge(done_copies, image(bh, u) * (GR // 2) + GR // 2 + PRIME)
                    sp.dma_start(k.vd[bass.ds(bh * 2 + u, 1)].rearrange("a k h q -> (a k) h q"), V[u][:, :, :])\
                      .then_inc(v_stored[u], 16)
            for u in range(2):
                sp.wait_ge(v_stored[u], 16 * (B // 2) + 16)

        @block.tensor
        def _(pe):
            with pe.Fori(0, B // 2) as bh:
                for u in range(2):
                    pe.wait_ge(z_loaded[u], bh * 16 + 16)
                    for n in range(GR):
                        pe.wait_ge(copied[n % 2], image(bh, u) * (GR // 2) + n // 2 + 1 - GR // 2 + PRIME)
                        pe.matmul(ps[n][:, :], ZT[u][:, 4 * (n // 2):4 * (n // 2) + 4, :].rearrange("q g w -> q (g w)"),
                                  t["cas_bd"][:, 512 * (n % 2):512 * (n % 2) + 512],
                                  start=True, stop=True).then_inc(mm_done, 1)

        @block.scalar
        def _(act):
            with act.Fori(0, B // 2) as bh:
                for u in range(2):
                    copies(act, act.copy, bh, u, 0)

        @block.vector
        def _(v):
            with v.Fori(0, B // 2) as bh:
                for u in range(2):
                    copies(v, v.tensor_copy, bh, u, 1)


NSTEP = ITERS * STEPS


class Step:

    def __init__(self, b, i, s, edge=None):
        self.b, self.i, self.s, self.edge = b, i, s, edge

    def n(self, lag):
        return self.b * NSTEP + self.i * STEPS + (self.s - lag)

    def it(self, lag):
        return self.b * ITERS + self.i + (self.s - lag) // STEPS

    def pair(self, lag):
        return self.b * (NSTEP // 2) + self.i * (STEPS // 2) + (self.s - lag) // 2

    def row(self, lag):
        h0 = self.i * (ROWS * STEPS) + ROWS * (self.s - lag)
        return h0 % HP if isinstance(h0, int) else h0

    def slot(self, lag, of):
        return (self.s - lag) % of

    def live(self, lag):
        m = self.i * STEPS + self.s - lag if self.edge else None
        return m >= 0 if self.edge == "first" else m < 0 if self.edge == "last" else True

    def opens_image(self, lag):
        return isinstance(self.i, int) and self.edge != "last" and self.i * STEPS + self.s == lag


def turns_and_ends(eng, B, step, end):
    def first_turns(b, edge):
        for s in range(STEPS):
            step(Step(b, 0, s, edge))

    def other_turns(b):
        with eng.Fori(1, ITERS) as i:
            for s in range(STEPS):
                step(Step(b, i, s))
    first_turns(0, "first")
    with eng.Fori(1, B) as b:
        other_turns(b - 1)
        first_turns(b, None)
        end(b - 1, False)
    other_turns(B - 1)
    first_turns(B, "last")
    end(B - 1, True)


def forward(k):
    nc, t, x, B = k.nc, k.t, k.a["x"], k.B
    XH, s1 = t["XH"], t["s1"]
    x_loaded = [k.sem(f"fw_x_loaded{u}") for u in range(2)]
    v_loaded = [k.sem(f"fw_v_loaded{u}") for u in range(2)]
    xn_stored = [k.sem(f"fw_xn_stored{u}") for u in range(2)]
    names = ("y_done", "xn_done", "xt_done", "xt_copied", "l0_done", "p0_done", "g0_done", "l1_done", "p1_done", "g1_done", "gm_done",
             "gm_copied", "xw_done", "xwa_done", "xs_done", "xb_done",
             "bt_done", "bt_copied", "b0_done", "b0_added", "b0_gelu", "b1_done", "b1_added", "b1_gelu", "e_done", "e_copied", "xh_done", "xh_copied")
    S = {n: k.sem("fw_" + n) for n in names}
    zeroed = k.sem("fw_zeroed")
    N = ROWS * W
    with ExitStack() as ctx:
        sb = lambda name, shape: k.sb("fw_" + name, shape, F32, ctx)
        xin = [sb(f"x{u}", [P, CHUNK * W]) for u in range(2)]
        vch = [sb(f"v{u}", [M, CHUNK, P]) for u in range(2)]
        xn = [sb(f"xn{u}", [P, CHUNK * W]) for u in range(2)]
        h1 = [sb(f"h1{u}", [P, 2, ROWS, W]) for u in range(2)]
        h2 = [sb(f"h2{u}", [P, 2, ROWS, 2, P]) for u in range(2)]
        xT = [sb(f"xT{u}", [P, ROWS, 2, P]) for u in range(4)]
        coord_w = sb("coord_w", [P, W])
        coord_h = sb("coord_h", [P, 2, HP])
        gt = sb("gt", [P, ROWS, 2, 2, C])
        xs = sb("xs", [P, 8])
        xb = sb("xb", [P, 8, HID])
        xwa = sb("xwa", [P, 2 * M, HP])
        xwT = sb("xwT", [P, 16, 2, P])
        hb1 = sb("hb1", [P, 2, M, HP])
        hb2 = sb("hb2", [P, 16, 4, HID + 1])
        et = sb("et", [HID + 1, 2, 8, 4, C])
        psY, psT, psG, psW = (k.ps("fw_ps" + n, ctx) for n in "YTGW")
        psL0 = [k.ps(f"fw_psL0{p}", ctx) for p in range(2)]
        psL1 = [k.ps(f"fw_psL1{p}", ctx) for p in range(2)]
        block = ctx.enter_context(nc.Block())
        x_v = x.rearrange("b c (j p i u r) w -> b j p u i c (r w)", j=2, p=2, i=ITERS, u=2)
        v_v = k.vd.rearrange("b k (i u r) q -> b u i k (r q)", i=ITERS, u=2)

        @block.sync
        def _(sp):
            prime(sp, *S.values())
            for u in range(2):
                sp.sem_inc(xn_stored[u], 16)
            with sp.Fori(0, B) as b:
                with sp.Fori(0, ITERS) as i:
                    for u in range(2):
                        sp.wait_ge(S["xn_done"], done((b * ITERS + i) * STEPS + 2 * u - 3))
                        sp.dma_start(vch[u][:, :, :], v_v[bass.ds(b, 1), u, bass.ds(i, 1)]
                                     .rearrange("a e k (r q) -> (a e k) r q", r=CHUNK)).then_inc(v_loaded[u], 16)
                        for q in range(4):
                            sp.dma_start(xin[u][32 * q:32 * q + 32, :],
                                         x_v[bass.ds(b, 1), q % 2, q // 2, u, bass.ds(i, 1)]
                                         .rearrange("a e c n -> (a e c) n")).then_inc(x_loaded[u], 16)
            for u in range(2):
                sp.wait_ge(xn_stored[u], B * ITERS * 16 + 16)

        @block.tensor
        def _(pe):
            def step(st):
                s = st.s
                if st.live(0):
                    n = st.n(0)
                    if s % 2 == 0:
                        pe.wait_ge(v_loaded[s // 2], (st.it(0) + 1) * 16)
                    pe.wait_ge(S["xn_done"], done(n - 1))
                    for r in range(ROWS):
                        last = pe.matmul(psY[:, r * W:r * W + W], vch[s // 2][:, (s % 2) * ROWS + r, :], t["cas_k"][:, :],
                                         start=True, stop=True)
                    last.then_inc(S["y_done"], 1)
                if st.live(1):
                    n, c = st.n(1), st.slot(1, 4)
                    pe.wait_ge(S["xn_done"], done(n))
                    pe.wait_ge(S["xt_copied"], done(n - 1))
                    for r in range(ROWS):
                        for g in range(2):
                            o = (c % 2) * N + r * W + g * P
                            last = pe.transpose(psT[:, (2 * r + g) * P:(2 * r + g) * P + P],
                                                xn[c // 2][:, o:o + P], t["ident"][:, :])
                    last.then_inc(S["xt_done"], 1)
                    for p in range(2):
                        pe.wait_ge(S["p0_done"], done(2 * (n - 1) + p))
                        pe.matmul(psL0[p][:, :], t["bw0"][:, p, :], xn[c // 2][:, (c % 2) * N:(c % 2) * N + N],
                                  start=True, stop=True).then_inc(S["l0_done"], 1)
                if st.live(4):
                    n, c = st.n(4), st.slot(4, 4)
                    pe.wait_ge(S["gm_copied"], done(n))
                    if c == 0:
                        pe.wait_ge(S["xwa_done"], done(st.it(4) - 1))
                    for r in range(ROWS):
                        for p in range(2):
                            last = pe.matmul(psW[p * HID:p * HID + HID, (ROWS * c + r) * HID:(ROWS * c + r + 1) * HID],
                                             gt[:, r, p, :, :], t["bw2"][:, :], start=True, stop=True)
                    last.then_inc(S["xw_done"], 1)
                if st.live(3):
                    n, c = st.n(3), st.slot(3, 4)
                    pe.wait_ge(S["g1_done"], done(2 * n + 1))
                    pe.wait_ge(S["xt_copied"], done(n))
                    pe.wait_ge(S["gm_copied"], done(n - 1))
                    for r in range(ROWS):
                        for p in range(2):
                            for g in range(2):
                                last = pe.matmul(psG[:, (2 * r + p) * HID:(2 * r + p) * HID + HID], h2[c % 2][:, p, r, g, :],
                                                 xT[c][:, r, g, p * HID:p * HID + HID], start=g == 0, stop=g == 1)
                    last.then_inc(S["gm_done"], 1)
                if st.live(2):
                    n, u = st.n(2), st.slot(2, 2)
                    for p in range(2):
                        pe.wait_ge(S["g0_done"], done(2 * n + p))
                        pe.wait_ge(S["p1_done"], done(2 * (n - 1) + p))
                        for r in range(ROWS):
                            for g in range(2):
                                last = pe.matmul(psL1[p][:, (2 * r + g) * P:(2 * r + g) * P + P],
                                                 h1[u][:, p, r, g * P:g * P + P], t["bw1"][:, :], start=True, stop=True)
                        last.then_inc(S["l1_done"], 1)

            def basis_h(b, last_image):
                end = (b + 1) * NSTEP - 1
                ahead = 0 if last_image else STEPS
                pe.wait_ge(S["xn_done"], done(end + ahead))
                pe.wait_ge(S["xt_copied"], done(end + max(ahead - 1, 0)))
                pe.wait_ge(S["p0_done"], done(2 * (end + max(ahead - 1, 0)) + 1))
                pe.wait_ge(S["gm_copied"], done(end + max(ahead - 3, 0)))
                pe.wait_ge(S["xwa_done"], done(b * ITERS + ITERS - 1))
                for i in range(8):
                    pe.wait_ge(S["bt_copied"], done(8 * b + i - 2))
                    for j in range(4):
                        mp, ri = 2 * i + j // 2, j % 2
                        last = pe.transpose((psT, psY)[i % 2][:, j * P:j * P + P],
                                            xwa[:, ri * M + 2 * mp:ri * M + 2 * mp + 2, :].rearrange("p m h -> p (m h)"),
                                            t["ident"][:, :])
                    last.then_inc(S["bt_done"], 1)
                for i in range(8):
                    mg, p = i // 2, i % 2
                    pe.wait_ge(S["b0_added"], done(8 * b + i - 2))
                    pe.matmul(psL0[p][:, :], t["bh0"][:, p, :], xwa[:, 8 * mg:8 * mg + 8, :].rearrange("p m h -> p (m h)"),
                              start=True, stop=True).then_inc(S["b0_done"], 1)
                for i in range(8):
                    pe.wait_ge(S["b0_gelu"], done(8 * b + 2 * (i // 2) + 1))
                    pe.wait_ge(S["b1_added"], done(8 * b + i - 2))
                    ps = (psG, psW)[i % 2]
                    for j in range(4):
                        mp, p = 2 * i + j // 2, j % 2
                        last = pe.matmul(ps[:, j * P:j * P + P], hb1[:, p, 2 * mp:2 * mp + 2, :].rearrange("p m h -> p (m h)"),
                                         t["bh1"][:, :], start=True, stop=True)
                    last.then_inc(S["b1_done"], 1)
                pe.wait_ge(S["bt_copied"], done(8 * b + 7))
                for i in range(4):
                    m2, half = i % 2, i // 2
                    rows = slice(HID * m2, HID * m2 + HID)
                    pe.wait_ge(S["b1_gelu"], done(8 * b + 4 * half + 3))
                    for j in range(8):
                        mp = 8 * half + j
                        for q in range(4):
                            last = pe.matmul((psT, psY, psL0[0], psL0[1])[i][0:HID + 1, j * HID:j * HID + HID], hb2[rows, mp, q, :],
                                             xwT[rows, mp, :, q * C:q * C + C], start=q == 0, stop=q == 3)
                    last.then_inc(S["e_done"], 1)
                pe.wait_ge(S["e_copied"], done(4 * b + 3))
                for m8 in range(8):
                    for ri in range(2):
                        last = pe.matmul(psG[:, m8 * HID:m8 * HID + HID], et[:, ri, m8, :, :].rearrange("f g c -> f (g c)"), t["bh2"][:, ri, :],
                                         start=ri == 0, stop=ri == 1)
                last.then_inc(S["xh_done"], 1)
                pe.wait_ge(S["xh_copied"], done(b))

            turns_and_ends(pe, B, step, basis_h)

        @block.scalar
        def _(act):
            def step(st):
                if st.live(3):
                    n, u = st.n(3), st.slot(3, 2)
                    for p in range(2):
                        act.wait_ge(S["p1_done"], done(2 * n + p))
                        y = h2[u][:, p, :, :, :].rearrange("q r g f -> q (r g f)")
                        act.activation(y, y, ACT.Gelu).then_inc(S["g1_done"], 1)
                if st.live(1):
                    n, u = st.n(1), st.slot(1, 2)
                    for p in range(2):
                        act.wait_ge(S["p0_done"], done(2 * n + p))
                        y = h1[u][:, p, :, :].rearrange("q r w -> q (r w)")
                        act.activation(y, y, ACT.Gelu, bias=t["bw0_b"][:, :]).then_inc(S["g0_done"], 1)
                if st.s % 2 == 1 and st.live(0):
                    u = st.s // 2
                    act.wait_ge(S["xn_done"], done(st.n(0)))
                    act.dma_start(k.xnd[bass.ds(st.b * (2 * ITERS) + 2 * st.i + u, 1)].rearrange("a p n -> (a p) n"),
                                  xn[u][:, :]).then_inc(xn_stored[u], 16)

            def basis_h(b, last_image):
                for i in range(8):
                    mg, p = i // 2, i % 2
                    act.wait_ge(S["b0_added"], done(8 * b + i))
                    y = hb1[:, p, 8 * mg:8 * mg + 8, :].rearrange("q m h -> q (m h)")
                    act.activation(y, y, ACT.Gelu, bias=t["bh0_b"][:, :]).then_inc(S["b0_gelu"], 1)
                for i in range(8):
                    act.wait_ge(S["b1_added"], done(8 * b + i))
                    y = hb2[:, 2 * i:2 * i + 2, :, 0:HID].rearrange("q a c f -> q (a c) f")
                    act.activation(y, y, ACT.Gelu).then_inc(S["b1_gelu"], 1)

            turns_and_ends(act, B, step, basis_h)

        @block.vector
        def _(v):
            def step(st):
                s = st.s
                if st.live(3):
                    n, u = st.n(3), st.slot(3, 2)
                    for p in range(2):
                        v.wait_ge(S["l1_done"], done(2 * n + p))
                        v.wait_ge(S["gm_done"], done(n - 2))
                        v.tensor_tensor(h2[u][:, p, :, :, :].rearrange("q r g (j f) -> q (r g j) f", j=2),
                                        psL1[p][:, :].rearrange("q (a f) -> q a f", f=HID),
                                        t["bw1_row"][:, :].unsqueeze(1).broadcast_to([P, 8, HID]), ALU.add).then_inc(S["p1_done"], 1)
                if st.live(0):
                    n = st.n(0)
                    u, cols = s // 2, slice((s % 2) * N, (s % 2) * N + N)
                    if s % 2 == 0:
                        v.wait_ge(x_loaded[u], (st.it(0) + 1) * 64)
                        v.wait_ge(xn_stored[u], (st.it(0) + 1) * 16)
                        v.wait_ge(S["l0_done"], done(2 * (n - 3) + 1))
                        v.wait_ge(S["xs_done"], done(n - 3))
                    v.wait_ge(S["y_done"], done(n))
                    v.scalar_tensor_tensor(xn[u][:, cols], xin[u][:, cols], s1[:, bass.ds(st.b, 1)], psY[:, :],
                                           ALU.mult, ALU.add).then_inc(S["xn_done"], 1)
                if st.live(1):
                    n, u, c = st.n(1), st.slot(1, 2), st.slot(1, 4)
                    v.wait_ge(S["xt_done"], done(n))
                    v.wait_ge(S["gm_done"], done(n - 4))
                    v.tensor_copy(xT[c][:, :, :, :].rearrange("q r g c -> q (r g c)"), psT[:, :]).then_inc(S["xt_copied"], 1)
                    for p in range(2):
                        v.wait_ge(S["l0_done"], done(2 * n + p))
                        v.wait_ge(S["l1_done"], done(2 * (n - 2) + p))
                        v.tensor_tensor(h1[u][:, p, :, :], psL0[p][:, :].rearrange("q (r w) -> q r w", r=ROWS),
                                        coord_w[:, :].unsqueeze(1).broadcast_to([P, ROWS, W]), ALU.add).then_inc(S["p0_done"], 1)
                    if c == 0:
                        v.wait_ge(S["xb_done"], done(st.it(1) - 1))
                    v.wait_ge(S["xn_done"], done(n))
                    v.reduce_sum(xs[:, ROWS * c:ROWS * c + ROWS],
                                 xn[c // 2][:, (c % 2) * N:(c % 2) * N + N].rearrange("q (r w) -> q r w", r=ROWS),
                                 axis=AX.X).then_inc(S["xs_done"], 1)
                if s == 3 and st.live(4):
                    it, i = st.it(4), st.i - 1
                    v.wait_ge(S["xw_done"], done(st.n(4)))
                    v.wait_ge(S["xb_done"], done(it))
                    own = st.b - 1 if isinstance(st.i, int) else st.b
                    v.wait_ge(S["b0_done"], done(8 * own - 1))
                    v.wait_ge(S["bt_done"], done(8 * own - 1))
                    at = slice(HP - 8, HP) if isinstance(i, int) else bass.ds(i * 8, 8)
                    v.tensor_tensor(xwa[:, :, at], psW[:, :].rearrange("q (h m) -> q m h", h=8),
                                    xb[:, :, :].rearrange("q h m -> q m h"), ALU.add).then_inc(S["xwa_done"], 1)
                if st.live(3):
                    n = st.n(3)
                    v.wait_ge(S["gm_done"], done(n))
                    v.wait_ge(S["xw_done"], done(n - 1))
                    for hj in range(2):
                        r = slice(HID * hj, HID * hj + HID)
                        last = v.tensor_copy(gt[r, :, :, hj, :].rearrange("q r p c -> q (r p) c"),
                                             psG[r, 0:4 * HID].rearrange("q (a c) -> q a c", c=HID)[:, :, hj * C:hj * C + C])
                    last.then_inc(S["gm_copied"], 1)

            def basis_h(b, last_image):
                for i in range(8):
                    v.wait_ge(S["bt_done"], done(8 * b + i))
                    v.wait_ge(S["e_done"], done(4 * b - 1))
                    v.tensor_copy(xwT[:, 2 * i:2 * i + 2, :, :].rearrange("q a r c -> q (a r c)"),
                                  (psT, psY)[i % 2][:, :]).then_inc(S["bt_copied"], 1)
                for i in range(8):
                    mg, p = i // 2, i % 2
                    v.wait_ge(S["b0_done"], done(8 * b + i))
                    v.wait_ge(S["b1_done"], done(8 * b - 1))
                    v.tensor_tensor(hb1[:, p, 8 * mg:8 * mg + 8, :], psL0[p][:, :].rearrange("q (m h) -> q m h", m=8),
                                    coord_h[:, p, :].unsqueeze(1).broadcast_to([P, 8, HP]), ALU.add).then_inc(S["b0_added"], 1)
                for i in range(8):
                    v.wait_ge(S["b1_done"], done(8 * b + i))
                    v.wait_ge(S["e_done"], done(4 * b - 1))
                    v.tensor_tensor(hb2[:, 2 * i:2 * i + 2, :, 0:HID].rearrange("q a c f -> q (a c) f"),
                                    (psG, psW)[i % 2][:, :].rearrange("q (a f) -> q a f", f=HID),
                                    t["bh1_row"][:, :].unsqueeze(1).broadcast_to([P, 8, HID]), ALU.add).then_inc(S["b1_added"], 1)
                for i in range(4):
                    m2, half = i % 2, i // 2
                    v.wait_ge(S["e_done"], done(4 * b + i))
                    v.wait_ge(S["xh_done"], done(b - 1))
                    for g in range(2):
                        src = (psT, psY, psL0[0], psL0[1])[i][0:HID + 1, 256 * g:256 * g + 256]
                        last = v.tensor_copy(et[:, :, m2:8:2, 2 * half + g, :].rearrange("q r m c -> q m r c"),
                                             src.rearrange("q (m r c) -> q m r c", m=4, r=2))
                    last.then_inc(S["e_copied"], 1)
                v.wait_ge(S["xh_done"], done(b))
                v.tensor_copy(XH[:, :, bass.ds(b, 1)], psG[:, :].rearrange("q (n a) -> q n a", a=1)).then_inc(S["xh_copied"], 1)

            v.memset(hb2[:, :, :, HID:HID + 1], 1.0)
            v.tensor_scalar(coord_w[:, :], t["wc_row"][:, :], t["bw0_c"][:, :], None, ALU.mult)
            v.tensor_scalar(coord_h[:, :, :], t["hc_rows"][:, :, :], t["bh0_c"][:, :], None, ALU.mult)
            v.memset(gt[:, :, :, :, :], 0.0).then_inc(zeroed, 1)
            v.wait_ge(zeroed, 1)
            turns_and_ends(v, B, step, basis_h)

        @block.gpsimd
        def _(g):
            with g.Fori(0, B * ITERS) as it:
                g.wait_ge(S["xs_done"], done(it * STEPS + STEPS - 1))
                g.wait_ge(S["xwa_done"], done(it - 1))
                g.tensor_tensor(xb[:, :, :], t["bw2_b"][:, :].unsqueeze(1).broadcast_to([P, 8, HID]),
                                xs[:, :].unsqueeze(2).broadcast_to([P, 8, HID]), ALU.mult).then_inc(S["xb_done"], 1)


def mix1(k):
    nc, t, B = k.nc, k.t, k.B
    XH = t["XH"]
    KH = M // 2
    w_loaded = [k.sem(f"mix1_w_loaded{u}") for u in range(2)]
    stored = [k.sem(f"mix1_stored{u}") for u in range(2)]
    zeroed, w_ready, mm_done, copied = (k.sem(n) for n in ("mix1_zeroed", "mix1_w_ready", "mix1_mm_done", "mix1_copied"))
    with ExitStack() as ctx:
        wa = [k.sb(f"mix1_wa{u}", [P, KH, 4, 2, C], F32, ctx) for u in range(2)]
        wb = [k.sb(f"mix1_wb{u}", [P, KH, 4, 2, C], F32, ctx) for u in range(2)]
        xf = [k.sb(f"mix1_xf{u}", [B, 2, KH, 4, C], F32, ctx) for u in range(2)]
        ps = [k.ps(f"mix1_ps{i}", ctx) for i in range(4)]
        block = ctx.enter_context(nc.Block())
        units = [(m8, kh) for m8 in range(8) for kh in range(2)]

        @block.sync
        def _(sp):
            sp.wait_ge(zeroed, 1)

            def store(n):
                m8, kh = units[n]
                sp.wait_ge(copied, 8 * (n + 1))
                sp.dma_start(k.xfd[m8, :, :, kh * KH:kh * KH + KH].rearrange("b r k g o -> b r (k g o)"),
                             xf[n % 2][:, :, :, :, :].rearrange("b r k g o -> b r (k g o)")).then_inc(stored[n % 2], 16)
            for n, (m8, kh) in enumerate(units):
                if n >= 2:
                    sp.wait_ge(w_ready, n - 1)
                    sp.wait_ge(mm_done, 8 * (n - 1))
                for g in range(4):
                    r = slice(32 * g, 32 * g + 32)
                    sp.dma_start(wa[n % 2][r, :, g, :, :].rearrange("c k r o -> c k (r o)"),
                                 k.a["l1_w"][m8, r, kh * KH:kh * KH + KH].rearrange("c k r o -> c k (r o)"))\
                      .then_inc(w_loaded[n % 2], 16)
                if n >= 1:
                    store(n - 1)
            store(len(units) - 1)
            for u in range(2):
                sp.wait_ge(stored[u], 16 * len(units) // 2)

        @block.vector
        def _(v):
            for u in range(2):
                v.memset(wa[u][:, :, :, :, :], 0.0)
                last = v.memset(wb[u][:, :, :, :, :], 0.0)
            last.then_inc(zeroed, 1)
            v.wait_ge(zeroed, 1)
            for n in range(len(units)):
                v.wait_ge(w_loaded[n % 2], 64 * (n // 2 + 1))
                if n >= 2:
                    v.wait_ge(mm_done, 8 * (n - 1))
                for g in range(4):
                    r = slice(32 * g, 32 * g + 32)
                    v.tensor_scalar(wb[n % 2][r, :, g, 0, :], wa[n % 2][r, :, g, 1, :], -1.0, None, ALU.mult)
                    last = v.tensor_copy(wb[n % 2][r, :, g, 1, :], wa[n % 2][r, :, g, 0, :])
                last.then_inc(w_ready, 1)

        @block.tensor
        def _(pe):
            for n, (m8, kh) in enumerate(units):
                pe.wait_ge(w_ready, n + 1)
                for j in range(8):
                    g = 8 * n + j
                    if g >= 4:
                        pe.wait_ge(copied, g - 3)
                    for i in range(2):
                        kk = kh * KH + 2 * j + i
                        for ri in range(2):
                            w = (wa, wb)[ri][n % 2][:, 2 * j + i, :, :, :].rearrange("c g r o -> c (g r o)")
                            last = pe.matmul(ps[g % 4][0:B, 256 * i:256 * i + 256], XH[:, (2 * m8 + ri) * M + kk, :], w,
                                             start=ri == 0, stop=ri == 1)
                    last.then_inc(mm_done, 1)

        @block.scalar
        def _(act):
            for n in range(len(units)):
                if n >= 2:
                    act.wait_ge(stored[n % 2], 16 * (n // 2))
                for j in range(8):
                    g = 8 * n + j
                    act.wait_ge(mm_done, g + 1)
                    for i in range(2):
                        last = act.copy(xf[n % 2][:, :, 2 * j + i, :, :].rearrange("b r g o -> b g r o"),
                                        ps[g % 4][0:B, 256 * i:256 * i + 256].rearrange("b (g r o) -> b g r o", g=4, r=2))
                    last.then_inc(copied, 1)


HEAD = 3


def all_steps(eng, B, image, step, last_lag):
    def head(b, edge):
        image(b)
        for s in range(HEAD * STEPS):
            step(Step(b, s // STEPS, s % STEPS, edge))

    def body(b):
        with eng.Fori(HEAD, ITERS) as i:
            for s in range(STEPS):
                step(Step(b, i, s))
    head(0, "first")
    with eng.Fori(1, B) as b:
        body(b - 1)
        head(b, None)
    body(B - 1)
    for s in range(last_lag):
        step(Step(B, s // STEPS, s % STEPS, "last"))


def inverse(k):
    nc, t, B = k.nc, k.t, k.B
    XF_LOADED, OUT = k.sem("iv_xf_loaded"), k.out
    xn_loaded = [k.sem(f"iv_xn_loaded{u}") for u in range(2)]
    out_stored = [k.sem(f"iv_out_stored{u}") for u in range(2)]
    yb_stored = k.sem("iv_yb_stored")
    yb_loaded = [k.sem(f"iv_yb_loaded{u}") for u in range(2)]
    zeroed = k.sem("iv_zeroed")
    names = ("pre_done", "g1_done", "l1_done", "g2_done", "tp_done", "tp_copied", "y_done", "yc_done", "sq_done",
             "sum_done", "rs_done", "yn_done", "tr_done", "gy_done", "sc_done", "t_done", "gs_done",
             "res_done", "out_done", "yt_done", "yt_copied", "ivm_set",
             "cond_done", "cond_copied", "td_done", "td_copied", "ah_done", "ah_copied", "hg0_done", "hl1_done",
             "hg1_done", "r_done", "r_copied", "aw_done", "rh_done", "rh_copied", "rt_done", "rt_copied", "rt_half_copied", "aw_copied", "newton", "held")
    S = {n: k.sem("iv_" + n) for n in names}
    N = ROWS * W
    with ExitStack() as ctx:
        sb = lambda name, shape: k.sb("iv_" + name, shape, F32, ctx)
        two = lambda name, shape: [sb(f"{name}{u}", shape) for u in range(2)]
        xfk = sb("xfk", [2 * M, 2, 16, C])
        ch = sb("ch", [C, 2, 2, 16])
        tb_row = sb("tb_row", [P, 16])
        td = sb("td", [P, 16, 2, 2, C])
        ah = sb("ah", [P, 16])
        ha = sb("ha", [P, 16, H])
        hb = sb("hb", [P, 16, H])
        R = sb("R", [P, 16, H])
        rh = ha[:, :, :].rearrange("q a (u n) -> q (a u n)", u=2).rearrange("q (j o c) -> q j o c", j=2, o=C)
        rt = sb("rt", [P, C, P])
        aw = sb("aw", [P, P])
        yb = sb("yb", [P, HP])
        ybt = sb("ybt", [HP, P])
        ybb = [sb(f"ybb{u}", [P, CHUNK, P]) for u in range(2)]
        wc_w = sb("wc_w", [P, W])
        ivm = sb("ivm", [P, 2])
        pre, wg1, wg2 = two("pre", [P, 2, ROWS, W]), two("wg1", [P, 2, ROWS, W]), two("wg2", [P, 2, ROWS, W])
        tp = sb("tp", [P, 8, 2, 2, C])
        yc = [sb(f"yc{i}", [P, N]) for i in range(4)]
        sq, yn, gy, tt, gs = (two(n, [P, N]) for n in ("sq", "yn", "gy", "tt", "gs"))
        res = [sb(f"res{i}", [P, N]) for i in range(4)]
        vs, xv, xh, nt = (sb(n, [P, 32]) for n in ("vs", "xv", "xh", "nt"))
        rs = two("rs", [P, 32])
        xn, osb = two("xn", [P, CHUNK * W]), two("osb", [P, CHUNK * W])
        psL = ctx.enter_context(nc.psum_tensor("iv_psL", [P, 2, 512], F32))
        psY, psR, psP, psX = (k.ps("iv_ps" + n, ctx) for n in "YRPX")
        psS = [k.ps(f"iv_psS{u}", ctx) for u in range(2)]
        block = ctx.enter_context(nc.Block())
        out_v = OUT.rearrange("b c (j p i r) w -> b j p i c (r w)", j=2, p=2, i=2 * ITERS)

        def copy_rt(copy, j, u):
            hj, og = j // 4, j % 4
            return copy(rt[HID * hj:HID * hj + HID, 8 * og + u:8 * og + u + 7:2, :],
                        (psP, psX)[j % 2][HID * u:HID * u + HID, :].rearrange("q (o h) -> q o h", h=P))

        @block.sync
        def _(sp):
            prime(sp, *S.values())
            for u in range(2):
                sp.sem_inc(out_stored[u], 64)

            def load_modes(b):
                sp.wait_ge(S["cond_done"], done(b - 1))
                sp.wait_ge(S["td_done"], done(2 * b - 1))
                sp.dma_start(xfk[:, :, :, :].rearrange("q a m o -> q (a m o)").rearrange("q (m n) -> q m n", m=8),
                             k.xfd[:, bass.ds(b, 1)].rearrange("m a r k g o -> (a r k) m (g o)")).then_inc(XF_LOADED, 16)

            def store(b):
                with sp.Fori(0, ITERS) as i:
                    for u in range(2):
                        sp.wait_ge(S["out_done"], done(b * NSTEP + i * STEPS + 2 * u + 1))
                        for q in range(4):
                            sp.dma_start(out_v[bass.ds(b, 1), q % 2, q // 2, bass.ds(i * 2 + u, 1)]
                                         .rearrange("a e c n -> (a e c) n"), osb[u][32 * q:32 * q + 32, :])\
                              .then_inc(out_stored[u], 16)
            load_modes(0)
            with sp.Fori(0, B - 1) as b:
                load_modes(b + 1)
                store(b)
            store(B - 1)
            for u in range(2):
                sp.wait_ge(out_stored[u], B * ITERS * 64 + 64)

        @block.tensor
        def _(pe):
            def image(b):
                for name, lag in (("g2_done", 2), ("yc_done", 3)):
                    pe.wait_ge(S[name], done(b * NSTEP - 1 - lag))
                pe.wait_ge(S["tp_copied"], done(b * ITERS - 1))
                pe.wait_ge(S["aw_copied"], done(b - 1))
                pe.wait_ge(XF_LOADED, (b + 1) * 16)
                pe.sem_inc(S["held"], 1)
                for m in range(M):
                    last = pe.matmul(psX[0:C, 4 * m:4 * m + 4], xfk[:, m // 16, m % 16, :], t["cond_h"][:, :],
                                     start=True, stop=True)
                last.then_inc(S["cond_done"], 1)
                for ri in range(2):
                    for mj in range(2):
                        last = pe.matmul(psL[HID * mj:HID * mj + HID, ri, :], t["hi2"][:, ri, :],
                                         xfk[:, mj, :, :].rearrange("q m o -> q (m o)"), start=True, stop=True)
                    last.then_inc(S["td_done"], 1)
                pe.wait_ge(S["cond_copied"], done(b))
                for mj in range(2):
                    for ri in range(2):
                        last = pe.matmul(psY[HID * mj:HID * mj + HID, 0:16], t["hi0"][:, ri, :], ch[:, ri, mj, :],
                                         start=ri == 0, stop=ri == 1)
                last.then_inc(S["ah_done"], 1)
                pe.wait_ge(S["td_copied"], done(2 * b + 1))

                def hidden(j):
                    pe.wait_ge(S["hg0_done"], done(8 * b + j))
                    pe.wait_ge(S["hg1_done"], done(8 * b + j - 2))
                    pe.matmul(psL[:, j % 2, :], t["hi1"][:, :], ha[:, 2 * j:2 * j + 2, :].rearrange("q a h -> q (a h)"),
                              start=True, stop=True).then_inc(S["hl1_done"], 1)
                hidden(0)
                hidden(1)
                for j in range(8):
                    if j + 2 < 8:
                        hidden(j + 2)
                    pe.wait_ge(S["hg1_done"], done(8 * b + j))
                    pe.wait_ge(S["r_copied"], done(8 * b + j - 2))
                    for u in range(2):
                        last = pe.matmul((psP, psX)[j % 2][:, u * H:u * H + H], td[:, 2 * j + u, :, :, :].rearrange("q a r o -> q (a r o)"),
                                         hb[:, 2 * j + u, :], start=True, stop=True)
                    last.then_inc(S["r_done"], 1)
                pe.wait_ge(S["r_copied"], done(8 * b + 7))
                for mp in range(16):
                    last = pe.matmul(psY[0:HID + C, 0:H], t["cond_y_w"][:, mp, :], R[:, mp, :], start=mp == 0, stop=mp == 15)
                last.then_inc(S["aw_done"], 1)
                for j in range(8):
                    hj, mg = j // 4, j % 4
                    pe.wait_ge(S["rh_copied"], done(8 * b + j - 2))
                    for a in range(4):
                        mp = 4 * mg + a
                        last = pe.matmul(psL[:, j % 2, a * P:a * P + P], R[:, mp, hj * P:hj * P + P], t["mix_bd"][:, :],
                                         start=True, stop=True)
                    last.then_inc(S["rh_done"], 1)
                pe.wait_ge(S["aw_copied"], done(b))
                pe.sem_inc(S["held"], 1)
                pe.transpose(psY[0:HP, 0:P], yb[:, :], t["ident"][:, :]).then_inc(S["yt_done"], 1)
                for j in range(8):
                    hj, og = j // 4, j % 4
                    pe.wait_ge(S["rh_copied"], done(8 * b + 7))
                    pe.wait_ge(S["rt_copied"], done(8 * b + j - 2))
                    pe.wait_ge(S["rt_half_copied"], done(8 * b + j - 2))
                    for a in range(4):
                        o = 8 * og + 2 * a
                        last = pe.transpose((psP, psX)[j % 2][:, a * P:a * P + P],
                                            rh[:, hj, o:o + 2, :].rearrange("q o j -> q (o j)"), t["ident"][:, :])
                    last.then_inc(S["rt_done"], 1)
                pe.wait_ge(S["rt_copied"], done(8 * b + 7))
                pe.wait_ge(S["rt_half_copied"], done(8 * b + 7))
                pe.wait_ge(S["yt_copied"], done(b))

            def step(st):
                if st.live(7):
                    n, u = st.n(7), st.slot(7, 2)
                    pe.wait_ge(S["yn_done"], done(n))
                    pe.wait_ge(S["gy_done"], done(n - 1))
                    for g in range(2):
                        for r in range(ROWS):
                            o = (g * ROWS + r) * P
                            last = pe.transpose(psR[:, r * W + g * P:r * W + g * P + P], yn[u][:, o:o + P], t["ident"][:, :])
                    last.then_inc(S["tr_done"], 1)
                if st.live(2):
                    n, u = st.n(2), st.slot(2, 2)
                    pe.wait_ge(S["g1_done"], done(n))
                    pe.wait_ge(S["g2_done"], done(n - 1))
                    for p in range(2):
                        last = pe.matmul(psL[:, p, :], t["wi1"][:, :], wg1[u][:, p, :, :].rearrange("q r w -> q (r w)"),
                                         start=True, stop=True)
                    last.then_inc(S["l1_done"], 1)
                if st.live(3):
                    n, u, c = st.n(3), st.slot(3, 2), st.slot(3, 4)
                    pe.wait_ge(S["g2_done"], done(n))
                    pe.wait_ge(S["yc_done"], done(n - 1))
                    pe.wait_ge(S["tp_copied"], done(st.it(3)))
                    for g in range(2):
                        for r in range(ROWS):
                            for p in range(2):
                                o = (2 * (g * ROWS + r) + p) * HID
                                last = pe.matmul(psY[:, o:o + HID], wg2[u][:, p, r, g * P:g * P + P],
                                                 tp[:, ROWS * c + r, p, :, :].rearrange("q j o -> q (j o)"), start=True, stop=True)
                    last.then_inc(S["y_done"], 1)
                if st.s == 2 and st.live(2):
                    pe.wait_ge(S["tp_copied"], done(st.it(2) - 1))
                    h0 = st.row(2)
                    w = rt[:, :, :].rearrange("q o (p h) -> q h p o", p=2)
                    w = w[:, bass.ds(h0, 8)] if not isinstance(h0, int) else w[:, h0:h0 + 8]
                    pe.matmul(psP[:, :].rearrange("q (h p o) -> q h p o", h=8, p=2), t["wi2"][:, :], w,
                              start=True, stop=True).then_inc(S["tp_done"], 1)
                if st.live(7):
                    n, c = st.n(7), st.slot(7, 4)
                    if c % 2 == 0:
                        pe.wait_ge(xn_loaded[c // 2], (st.it(7) + 1) * 16)
                    pe.wait_ge(S["t_done"], done(n - 2))
                    pe.matmul(psS[c % 2][:, :], t["sc"][:, :], xn[c // 2][:, (c % 2) * N:(c % 2) * N + N],
                              start=True, stop=True).then_inc(S["sc_done"], 1)

            all_steps(pe, B, image, step, 8)

        @block.scalar
        def _(act):
            def image(b):
                act.wait_ge(S["ah_copied"], done(b))
                act.wait_ge(S["rt_done"], done(8 * b - 1))
                act.wait_ge(S["r_done"], done(8 * b - 1))

                def first(j):
                    for mp in (2 * j, 2 * j + 1):
                        last = act.activation(ha[:, mp, :], t["hc_row"][:, :], ACT.Gelu, scale=t["hi0_c"][:, :], bias=ah[:, mp:mp + 1])
                    last.then_inc(S["hg0_done"], 1)
                first(0)
                first(1)
                for j in range(8):
                    if j + 2 < 8:
                        first(j + 2)
                    act.wait_ge(S["hl1_done"], done(8 * b + j))
                    act.activation(hb[:, 2 * j:2 * j + 2, :].rearrange("q a h -> q (a h)"), psL[:, j % 2, :],
                                   ACT.Gelu, bias=t["hi1_b"][:, :]).then_inc(S["hg1_done"], 1)
                for j in range(8):
                    hj, mg = j // 4, j % 4
                    act.wait_ge(S["rh_done"], done(8 * b + j))
                    act.wait_ge(S["hl1_done"], done(8 * b + 7))
                    act.copy(rh[:, hj, :, 16 * mg:16 * mg + 16].rearrange("q o c -> q c o"),
                             psL[:, j % 2, :].rearrange("q (c o) -> q c o", o=C)).then_inc(S["rh_copied"], 1)
                act.wait_ge(S["yt_copied"], done(b))
                act.dma_start(k.ybd[bass.ds(b * (2 * ITERS), 2 * ITERS)].rearrange("a (h c) -> (a h) c", h=CHUNK), ybt[:, :])\
                   .then_inc(yb_stored, 16)
                act.wait_ge(S["tp_done"], done(b * ITERS - 1))
                for j in range(8):
                    act.wait_ge(S["rt_done"], done(8 * b + j))
                    copy_rt(act.copy, j, 1).then_inc(S["rt_half_copied"], 1)

            def step(st):
                if st.live(1):
                    n, u = st.n(1), st.slot(1, 2)
                    act.wait_ge(S["pre_done"], done(n))
                    act.wait_ge(S["l1_done"], done(n - 2))
                    act.activation(wg1[u][:, :, :, :].rearrange("q p r w -> q (p r w)"),
                                   pre[u][:, :, :, :].rearrange("q p r w -> q (p r w)"), ACT.Gelu).then_inc(S["g1_done"], 1)
                if st.live(7):
                    n, u = st.n(7), st.slot(7, 2)
                    act.wait_ge(S["tr_done"], done(n))
                    act.wait_ge(S["t_done"], done(n - 2))
                    act.activation(gy[u][:, :], psR[:, :], ACT.Gelu, scale=t["ln_g"][:, :], bias=t["ln_b"][:, :])\
                       .then_inc(S["gy_done"], 1)
                if st.live(9):
                    n, u = st.n(9), st.slot(9, 2)
                    act.wait_ge(S["t_done"], done(n))
                    act.wait_ge(S["out_done"], done(n - 2))
                    act.activation(gs[u][:, :], tt[u][:, :], ACT.Gelu, bias=t["sc_b"][:, :]).then_inc(S["gs_done"], 1)
                if st.live(2):
                    n, u = st.n(2), st.slot(2, 2)
                    act.wait_ge(S["l1_done"], done(n))
                    act.wait_ge(S["y_done"], done(n - 2))
                    act.activation(wg2[u][:, :, :, :].rearrange("q p r w -> q (p r w)"),
                                   psL[:, :, :].rearrange("q p n -> q (p n)"), ACT.Gelu, bias=t["wi1_b"][:, :]).then_inc(S["g2_done"], 1)
                if st.s % 2 == 1 and st.live(5):
                    u = st.slot(5, 4) // 2
                    act.wait_ge(S["sc_done"], done(st.n(8)))
                    act.wait_ge(S["res_done"], done(st.n(8)))
                    act.dma_start(xn[u][:, :], k.xnd[bass.ds(st.b * (2 * ITERS) + 2 * st.i + (st.s - 5) // 2, 1)]
                                  .rearrange("a p n -> (a p) n")).then_inc(xn_loaded[u], 16)
                if st.s % 2 == 1 and st.live(1):
                    u = st.slot(1, 4) // 2
                    if st.opens_image(1):
                        act.wait_ge(yb_stored, (st.b + 1) * 16)
                    act.wait_ge(S["yc_done"], done(st.n(4)))
                    act.dma_start(ybb[u][:, :, :].rearrange("q h c -> q (h c)"),
                                  k.ybd[bass.ds(st.b * (2 * ITERS) + 2 * st.i + st.s // 2, 1)].broadcast_to([P, CHUNK * P]))\
                       .then_inc(yb_loaded[u], 16)

            all_steps(act, B, image, step, 10)

        @block.vector
        def _(v):
            def image(b):
                v.wait_ge(S["cond_done"], done(b))
                c_ps = psX[0:C, 0:P].rearrange("q (a m f) -> q f a m", a=2, f=4)
                v.wait_ge(S["ah_done"], done(b - 1))
                v.tensor_scalar(ch[:, :, :, :].rearrange("q r a m -> q r (a m)"),
                                psX[0:C, 0:P].rearrange("q (m f) -> q f m", f=4)[:, 0:2, :], t["comp_h_b"][:, :], None, ALU.add)
                v.wait_ge(S["r_copied"], done(8 * b - 1))
                for mj in range(2):
                    for ri in range(2):
                        q = 2 * mj + ri
                        last = v.tensor_copy(tb_row[C * q:C * q + C, :], c_ps[:, 2 + ri, mj, :])
                last.then_inc(S["cond_copied"], 1)
                v.wait_ge(S["r_done"], done(8 * b - 1))
                for ri in range(2):
                    v.wait_ge(S["td_done"], done(2 * b + ri))
                    for mj in range(2):
                        r = slice(HID * mj, HID * mj + HID)
                        last = v.tensor_copy(td[r, :, mj, ri, :], psL[r, ri, :].rearrange("q (m o) -> q m o", o=C))
                    last.then_inc(S["td_copied"], 1)
                v.wait_ge(S["ah_done"], done(b))
                v.wait_ge(S["hg0_done"], done(8 * b - 1))
                v.tensor_scalar(ah[:, :], psY[:, 0:16], t["hi0_b"][:, :], None, ALU.add).then_inc(S["ah_copied"], 1)
                v.wait_ge(S["rh_done"], done(8 * b - 1))
                v.wait_ge(S["cond_copied"], done(b))
                for j in range(8):
                    v.wait_ge(S["r_done"], done(8 * b + j))
                    for u in range(2):
                        last = v.tensor_scalar(R[:, 2 * j + u, :], (psP, psX)[j % 2][:, u * H:u * H + H],
                                               tb_row[:, 2 * j + u:2 * j + u + 1], None, ALU.add)
                    last.then_inc(S["r_copied"], 1)
                v.wait_ge(S["aw_done"], done(b))
                v.wait_ge(S["pre_done"], done(b * NSTEP - 1))
                v.wait_ge(S["yt_done"], done(b - 1))
                for hj in range(2):
                    v.tensor_scalar(aw[HID * hj:HID * hj + HID, :], psY[0:HID, hj * P:hj * P + P], wi0_const, None, ALU.add)
                for q in range(4):
                    h0 = (q % 2) * P + (q // 2) * HP
                    last = v.tensor_scalar(yb[C * q:C * q + C, :], psY[HID:HID + C, h0:h0 + HP], y_const, None, ALU.add)
                last.then_inc(S["aw_copied"], 1)
                v.wait_ge(yb_stored, b * 16)
                v.wait_ge(S["yt_done"], done(b))
                v.tensor_copy(ybt[:, :], psY[0:HP, 0:P]).then_inc(S["yt_copied"], 1)
                v.wait_ge(S["tp_done"], done(b * ITERS - 1))
                for j in range(8):
                    v.wait_ge(S["rt_done"], done(8 * b + j))
                    copy_rt(v.tensor_copy, j, 0).then_inc(S["rt_copied"], 1)

            wi0_const, y_const = t["wi0_const"][0:HID, :], t["y_const"][HID:HID + C, :]

            def newton(y):
                ops = [lambda: v.tensor_scalar(xv[:, :], vs[:, :], 1.0 / C, 1e-5, ALU.mult, ALU.add),
                       lambda: v.tensor_scalar(y.bitcast(I32), xv[:, :].bitcast(I32), -0.5, MAGIC, ALU.mult, ALU.add),
                       lambda: v.tensor_scalar(xh[:, :], xv[:, :], -0.5, None, ALU.mult)]
                for _ in range(3):
                    ops += [lambda: v.tensor_tensor(nt[:, :], y, y, ALU.mult),
                            lambda: v.tensor_tensor(nt[:, :], nt[:, :], xh[:, :], ALU.mult),
                            lambda: v.scalar_tensor_tensor(y, nt[:, :], 1.5, y, ALU.add, ALU.mult)]
                return ops

            NEWTON, HALF = 12, 6

            def newton_part(pair, y, first, end):
                for j, op in enumerate(newton(y)[first:end], first):
                    if j:
                        v.wait_ge(S["newton"], pair * (NEWTON - 1) + j + PRIME)
                    op().then_inc(S["newton"] if j < NEWTON - 1 else S["rs_done"], 1)

            def step(st):
                if st.opens_image(7):
                    v.wait_ge(S["res_done"], done(st.n(8)))
                    v.tensor_copy(ivm[:, 0:1], t["invs"][:, bass.ds(st.b, 1)])
                    v.tensor_copy(ivm[:, 1:2], t["mean1"][:, bass.ds(st.b, 1)]).then_inc(S["ivm_set"], 1)
                if st.s == 3 and st.live(3):
                    v.wait_ge(S["tp_done"], done(st.it(3)))
                    v.wait_ge(S["y_done"], done(st.n(4)))
                    for hj in range(2):
                        r = slice(HID * hj, HID * hj + HID)
                        last = v.tensor_copy(tp[r, :, :, hj, :].rearrange("q h p o -> q (h p) o"),
                                             psP[r, :].rearrange("q (a o) -> q a o", o=C))
                    last.then_inc(S["tp_copied"], 1)
                if st.s % 2 == 0 and st.live(6):
                    newton_part(st.pair(6), rs[st.slot(6, 4) // 2][:, :], HALF, NEWTON)
                if st.live(6):
                    n, c, u = st.n(6), st.slot(6, 4), st.slot(6, 2)
                    v.wait_ge(S["rs_done"], done(st.pair(6)))
                    v.wait_ge(S["tr_done"], done(n - 2))
                    v.wait_ge(S["yc_done"], done(n))
                    v.tensor_tensor(yn[u][:, :].rearrange("q (a o) -> q a o", o=C), yc[c][:, :].rearrange("q (a o) -> q a o", o=C),
                                    rs[c // 2][:, 16 * u:16 * u + 16].unsqueeze(2).broadcast_to([P, 16, C]), ALU.mult)\
                     .then_inc(S["yn_done"], 1)
                if st.live(8):
                    n, u = st.n(8), st.slot(8, 2)
                    v.wait_ge(S["gy_done"], done(n))
                    v.wait_ge(S["sc_done"], done(n))
                    v.wait_ge(S["gs_done"], done(n - 2))
                    v.tensor_tensor(tt[u][:, :], gy[u][:, :], psS[u][:, :], ALU.add).then_inc(S["t_done"], 1)
                if st.live(4):
                    n, u = st.n(4), st.slot(4, 2)
                    v.wait_ge(S["sq_done"], done(n))
                    if u == 0:
                        v.wait_ge(S["rs_done"], done(st.pair(4) - 1))
                    v.reduce_sum(vs[:, 16 * u:16 * u + 16], sq[u][:, :].rearrange("q (a o) -> q a o", o=C), axis=AX.X)\
                     .then_inc(S["sum_done"], 1)
                if st.live(3):
                    n, c = st.n(3), st.slot(3, 4)
                    v.wait_ge(S["y_done"], done(n))
                    v.wait_ge(S["yn_done"], done(n - 4))
                    v.wait_ge(S["sq_done"], done(n - 4))
                    if c % 2 == 0:
                        v.wait_ge(yb_loaded[c // 2], (st.it(3) + 1) * 16)
                    bias = ybb[c // 2][:, (c % 2) * ROWS:(c % 2) * ROWS + ROWS, :].rearrange("q r c -> q (r c)")
                    v.tensor_tensor(yc[c][:, :].rearrange("q (g n) -> q g n", g=2), psY[:, :].rearrange("q (g n) -> q g n", g=2),
                                    bias.unsqueeze(1).broadcast_to([P, 2, ROWS * P]), ALU.add).then_inc(S["yc_done"], 1)
                if st.live(10):
                    n, c, u = st.n(10), st.slot(10, 4), st.slot(10, 2)
                    v.wait_ge(S["gs_done"], done(n))
                    v.wait_ge(S["res_done"], done(n))
                    if c % 2 == 0:
                        v.wait_ge(out_stored[c // 2], (st.it(10) + 1) * 64)
                    v.tensor_tensor(osb[c // 2][:, (c % 2) * N:(c % 2) * N + N], res[c][:, :], gs[u][:, :], ALU.add)\
                     .then_inc(S["out_done"], 1)
                if st.s % 2 == 1 and st.live(5):
                    v.wait_ge(S["sum_done"], done(st.n(4)))
                    v.wait_ge(S["yn_done"], done(st.n(8)))
                    v.wait_ge(S["rs_done"], done(st.pair(5) - 1))
                    newton_part(st.pair(5), rs[st.slot(5, 4) // 2][:, :], 0, HALF)

            v.memset(td[:, :, :, :, :], 0.0)
            v.memset(tp[:, :, :, :, :], 0.0)
            v.tensor_scalar(wc_w[:, :], t["wc_row"][:, :], t["wi0_c"][:, :], None, ALU.mult).then_inc(zeroed, 1)
            v.wait_ge(zeroed, 1)
            all_steps(v, B, image, step, 11)

        @block.gpsimd
        def _(g):
            def image(b):
                g.wait_ge(S["aw_copied"], done(b))

            def step(st):
                if st.live(7):
                    n, c = st.n(7), st.slot(7, 4)
                    if st.opens_image(7):
                        g.wait_ge(S["ivm_set"], done(st.b))
                    if c % 2 == 0:
                        g.wait_ge(xn_loaded[c // 2], (st.it(7) + 1) * 16)
                    g.wait_ge(S["out_done"], done(n - 4))
                    g.sem_inc(S["held"], 1)
                    g.tensor_scalar(res[c][:, :], xn[c // 2][:, (c % 2) * N:(c % 2) * N + N], ivm[:, 0:1], ivm[:, 1:2],
                                    ALU.mult, ALU.add).then_inc(S["res_done"], 1)
                if st.live(0):
                    n, u = st.n(0), st.slot(0, 2)
                    g.wait_ge(S["g1_done"], done(n - 2))
                    h0 = st.row(0)
                    a = aw[:, :].rearrange("q (p h) -> q p h", p=2)
                    a = a[:, :, bass.ds(h0, ROWS)] if not isinstance(h0, int) else a[:, :, h0:h0 + ROWS]
                    g.tensor_tensor(pre[u][:, :, :, :], wc_w[:, :].unsqueeze(1).unsqueeze(1).broadcast_to([P, 2, ROWS, W]),
                                    a.unsqueeze(3).broadcast_to([P, 2, ROWS, W]), ALU.add).then_inc(S["pre_done"], 1)
                if st.live(3):
                    n, c, u = st.n(3), st.slot(3, 4), st.slot(3, 2)
                    g.wait_ge(S["yc_done"], done(n))
                    g.wait_ge(S["sum_done"], done(n - 2))
                    g.tensor_tensor(sq[u][:, :], yc[c][:, :], yc[c][:, :], ALU.mult).then_inc(S["sq_done"], 1)

            g.wait_ge(zeroed, 1)
            all_steps(g, B, image, step, 8)


def build(nc, a, out):
    with ExitStack() as ctx:
        k = Kit(nc, ctx, a, out)
        B = k.B
        k.zd = nc.dram_tensor("zd", (4, 4, B, 8, 8, M), F32).ap()
        k.vd = nc.dram_tensor("vd", (B, M, HP, P), F32).ap()
        k.xnd = nc.dram_tensor("xnd", (B * 2 * ITERS, P, CHUNK * W), F32).ap()
        k.xfd = nc.dram_tensor("xfd", (8, B, 2, M, 4, C), F32).ap()
        k.ybd = nc.dram_tensor("ybd", (B * 2 * ITERS, CHUNK * P), F32).ap()
        setup(k)
        for n in ("mean1", "invs", "s1"):
            k.sb(n, [P, B])
        with ExitStack() as c0:
            k.sb("XM", [P, 2 * 8 * M, B], F32, c0)
            k.sb("MV", [P, B, 16, 2], F32, c0)
            dht(k)
            mix0(k)
        rows0(k)
        with ExitStack() as c1:
            k.sb("XH", [P, 8 * 2 * M, B], F32, c1)
            forward(k)
            mix1(k)
        inverse(k)


def weight_layouts(w):
    f = np.float32
    t = {n: np.zeros(s, f) for n, s in TABLES.items()}
    n, kk = np.arange(W), np.arange(M)
    ang = 2 * np.pi * ((n[:, None] * kk[None, :]) % W) / W
    cas = (np.cos(ang) + np.sin(ang)).astype(f)
    flip = (-kk) % M
    t["cas_n"][:, :, :M] = cas.reshape(2, P, M).transpose(1, 0, 2)
    t["cas_n"][:, :, 2 * M:] = t["cas_n"][:, :, :M]
    t["cas_n"][:, :, M:2 * M] = cas[:, flip].reshape(2, P, M).transpose(1, 0, 2)
    t["cas_k"][:] = cas.T
    for j in range(4):
        t["cas_bd"][32 * j:32 * j + 32, H * j:H * j + H] = cas.T.reshape(8, 4, H).transpose(1, 0, 2).reshape(M, H)
    t["ident"][:] = np.eye(P, dtype=f)
    c = np.arange(P) % C
    t["chan_mask"][:] = c[:, None] // 2 == np.arange(16)[None, :]
    t["group_avg"][:] = (c[:, None] // 2 == c[None, :] // 2) * f(1 / 8)
    t["ones_avg"][:] = f(1 / P)
    t["lane_avg"][:] = (np.arange(P)[:, None] // C == np.arange(4)[None, :]) * f(1 / C)

    def two(m):
        r, q = m.shape
        z = np.zeros((2 * r, 2 * q), f)
        z[:r, :q] = m
        z[r:, q:] = m
        return z

    for name in ("bw", "bh"):
        for p in range(2):
            for hj in range(2):
                q = 2 * p + hj
                t[name + "0"][32 * q:32 * q + 32, p, HID * hj:HID * hj + HID] = w[name + "0_w"][:C]
    for name in ("bw", "bh", "hi", "wi"):
        t[name + "1"][:] = two(w[name + "1_w"])
        t[name + "0_b"][:, 0] = np.tile(w[name + "0_b"], 2)
    for name in ("bw", "bh"):
        t[name + "0_c"][:, 0] = np.tile(w[name + "0_w"][C], 2)
        t[name + "1_row"][:] = w[name + "1_b"][None, :]
    for name in ("hi", "wi"):
        t[name + "1_b"][:, 0] = np.tile(w[name + "1_b"], 2)
        t[name + "0_c"][:, 0] = np.tile(w[name + "0_w"][0], 2)
    t["bw2"][:] = np.tile(w["bw2_w"], (2, 1))
    t["bw2_b"][:] = w["bw2_b"][None, :]
    bh2 = np.concatenate([w["bh2_w"], w["bh2_b"][None, :]], 0)
    t["bh2"][:, 0] = bh2
    t["bh2"][:, 1] = np.concatenate([bh2[:, M:], bh2[:, :M]], 1)
    ch, b2 = w["comp_h_w"], w["hi2_b"]
    t["cond_h"][:M, 0] = ch
    t["cond_h"][M:, 1] = ch
    t["cond_h"][:, 2] = b2
    t["cond_h"][:M, 3] = b2[M:]
    t["cond_h"][M:, 3] = b2[:M]
    t["comp_h_b"][:] = w["comp_h_b"][None, :]
    t["hi0"][:] = w["hi0_w"][1:].reshape(2, C, HID).transpose(1, 0, 2)
    hc = np.linspace(-1.0, 1.0, H, dtype=f)
    t["hc_row"][:] = hc[None, :]
    t["hc_rows"][:] = np.repeat(hc.reshape(2, 2, HP), HID, 0)
    t["wc_row"][:] = hc[None, :]
    t["hi2"][:, 0] = w["hi2_w"].T
    t["hi2"][:M, 1] = w["hi2_w"].T[M:]
    t["hi2"][M:, 1] = w["hi2_w"].T[:M]
    t["wi0"][:] = np.tile(w["wi0_w"][1:], (2, 1))
    t["wi0_sum"][:] = np.tile(w["wi0_w"][1:], (1, 2))
    t["comp_w_b"][:] = w["comp_w_b"][None, :]
    place = np.array([[(mp % 4) * 8 + mj * 4 + mp // 4 for mp in range(16)] for mj in range(2)])
    t["comp_w"][:] = np.repeat(w["comp_w_w"][place], HID, 0)
    t["mixer"][:] = np.tile(w["mixer_w"].T, (4, 1))
    t["mixer_b"][:] = w["mixer_b"][None, :]
    t["mixer_own"][:, 0] = np.tile(w["mixer_b"], 4)
    b2 = w["wi2_b"].reshape(2, M)[:, place]
    t["wi2_b"][:] = np.repeat(b2.transpose(1, 0, 2).reshape(4, 16), C, 0)
    w2 = w["wi2_w"].reshape(HID, 2, M)[:, :, place].transpose(3, 2, 1, 0).reshape(HID, HID)
    t["wi2"][:] = two(w2)
    t["sc"][:] = two(two(w["sc_w"].T))
    for name, src in (("sc_b", "sc_b"), ("ln_g", "ln_g"), ("ln_b", "ln_b")):
        t[name][:, 0] = np.tile(w[src], 4)
    w0 = w["l0"]
    both = np.stack([w0, w0[:, :, flip][:, :, :, flip]], 0)
    t["l0_w"] = both.reshape(2, C, C, 8, 4, M).transpose(3, 4, 1, 0, 5, 2).reshape(8, P, 2, M, C)
    wf = np.stack([w["wf_real"], w["wf_imag"]], 0).reshape(2, C, C, M, 4, 8)
    t["l1_w"] = wf.transpose(5, 4, 2, 3, 0, 1).reshape(8, P, M, 2, C)
    return {n: np.ascontiguousarray(v, dtype=f) for n, v in t.items()}


def kernel(**inputs):
    import concourse.bacc as bacc
    from concourse.bass_utils import run_bass_kernel_spmd as run

    w = {n[len("L1_conv_"):]: np.asarray(v) for n, v in inputs.items() if n.startswith("L1_conv_")}
    w["l0"] = np.asarray(inputs["L0_conv_weights1"])
    arrays = weight_layouts(w)
    arrays["x"] = np.asarray(inputs["x"])
    nc = bacc.Bacc("TRN2", target_bir_lowering=False, num_devices=1)
    a = {n: nc.dram_tensor("in_" + n, v.shape, mybir.dt.from_np(v.dtype), kind="ExternalInput").ap()
         for n, v in arrays.items()}
    out = nc.dram_tensor("out", arrays["x"].shape, F32, kind="ExternalOutput").ap()
    build(nc, a, out)
    r = run(nc, [{"in_" + n: v for n, v in arrays.items()}], core_ids=[0])
    return r.results[0]["out"]
```

```python
import numpy as np
import concourse.bass as bass
from concourse import mybir
from contextlib import ExitStack

F32 = mybir.dt.float32

I32 = mybir.dt.int32
ACT = mybir.ActivationFunctionType
ALU = mybir.AluOpType
AX = mybir.AxisListType

C, H, W, M, HID = 32, 256, 256, 32, 64
P = 128
NPX = H * W
HP = 64
ROWS = 2
CHUNK = 4
STEPS = 4
ITERS = HP // (ROWS * STEPS)
PRIME = 12
MAGIC = 1597463007.0


def done(step):
    return step + 1 + PRIME


class Kit:

    def __init__(self, nc, ctx, a, out):
        self.nc, self.ctx, self.a, self.out = nc, ctx, a, out
        self.B = a["x"].shape[0]
        self.t = {}

    def sb(self, name, shape, dt=F32, ctx=None):
        t = (ctx or self.ctx).enter_context(self.nc.sbuf_tensor(name, shape, dt))
        self.t[name] = t
        return t

    def ps(self, name, ctx, shape=(P, 512)):
        return ctx.enter_context(self.nc.psum_tensor(name, list(shape), F32))

    def sem(self, name):
        return self.ctx.enter_context(self.nc.semaphore(name))


def prime(eng, *sems):
    for s in sems:
        eng.sem_inc(s, PRIME)


class Chain:

    def __init__(self, eng, sem):
        self.eng, self.sem, self.n = eng, sem, 0

    def __call__(self, ins):
        ins.then_inc(self.sem, 1)
        self.n += 1
        self.eng.wait_ge(self.sem, self.n)


def rsqrt_chain(v, link, y, x, t):
    link(v.tensor_scalar(y.bitcast(I32), x.bitcast(I32), -0.5, MAGIC, ALU.mult, ALU.add))
    for _ in range(3):
        link(v.tensor_tensor(t, y, y, ALU.mult))
        link(v.tensor_tensor(t, t, x, ALU.mult))
        link(v.tensor_scalar(t, t, -0.5, 1.5, ALU.mult, ALU.add))
        link(v.tensor_tensor(y, y, t, ALU.mult))


TABLES = {
    "cas_n": (P, 2, 3 * M), "cas_k": (M, W), "cas_bd": (P, 4 * H), "ident": (P, P),
    "chan_mask": (P, 16), "group_avg": (P, P), "ones_avg": (P, P),
    "bw0": (P, 2, P), "bh0": (P, 2, P), "bw1": (P, P), "bh1": (P, P), "hi1": (P, P), "wi1": (P, P),
    "bw0_b": (P, 1), "bh0_b": (P, 1), "hi1_b": (P, 1), "wi1_b": (P, 1), "hi0_b": (P, 1), "wi0_b": (P, 1),
    "bw0_c": (P, 1), "bh0_c": (P, 1), "bw1_row": (P, HID), "bh1_row": (P, HID), "hc_rows": (P, 2, HP),
    "bw2": (P, HID), "bw2_b": (P, HID), "bh2": (HID + 1, 2, 2 * M),
    "cond_h": (2 * M, 4), "comp_h_b": (C, 1), "hi0": (C, 2, HID), "hi0_c": (P, 1), "hc_row": (P, H),
    "hi2": (2 * M, 2, HID), "wi0": (P, HID), "wi0_c": (P, 1), "wc_row": (P, W), "comp_w": (P, 16),
    "wi0_sum": (2 * C, P), "comp_w_b": (2 * C, 1), "mixer": (P, C), "mixer_b": (P, C), "mixer_own": (P, 1),
    "wi2_b": (P, 16), "wi2": (P, P), "sc": (P, P), "sc_b": (P, 1), "ln_g": (P, 1), "ln_b": (P, 1),
}


def place_tables(k):
    for name, shape in TABLES.items():
        k.sb(name, list(shape))
    k.sb("mix_c", [P, C])
    k.sb("mix_bd", [P, P])
    k.sb("wi0_const", [P, 1])
    k.sb("y_const", [P, 1])
    k.cas_loaded, k.tables_loaded = k.sem("cas_loaded"), k.sem("tables_loaded")


def load_table(k, eng, name, loaded):
    eng.dma_start(k.t[name][tuple(slice(None) for _ in TABLES[name])], k.a[name]).then_inc(loaded, 16)


def setup(k):
    nc, t = k.nc, k.t
    mix_c, mix_bd, wi0_const, y_const = (t[n] for n in ("mix_c", "mix_bd", "wi0_const", "y_const"))
    chain = k.sem("setup_chain")
    with ExitStack() as ctx:
        mean = k.sb("setup_mean", [P, 4], F32, ctx)
        ps = k.ps("setup_ps", ctx)
        n_loads = len(TABLES) - 1
        mm = k.sem("setup_mm")
        block = ctx.enter_context(nc.Block())

        @block.vector
        def _(v):
            link = Chain(v, chain)
            v.wait_ge(k.tables_loaded, 16 * n_loads)
            link(v.memset(mix_bd[:, :], 0.0))
            link(v.tensor_scalar(t["bh2"][:, 1, 0:M], t["bh2"][:, 1, 0:M], -1.0, None, ALU.mult))
            link(v.tensor_scalar(t["cond_h"][0:M, 3:4], t["cond_h"][0:M, 3:4], -1.0, None, ALU.mult))
            link(v.tensor_scalar(t["hi2"][0:M, 1, :], t["hi2"][0:M, 1, :], -1.0, None, ALU.mult))
            link(v.reduce_sum(mean[:, 0:1], t["mixer"][:, :], axis=AX.X))
            link(v.tensor_scalar(mean[:, 1:2], mean[:, 0:1], 1.0 / C, None, ALU.mult))
            link(v.tensor_scalar(mix_c[:, :], t["mixer"][:, :], mean[:, 1:2], 1.0 / NPX, ALU.subtract, ALU.mult))
            for q in range(4):
                r = slice(32 * q, 32 * q + 32)
                link(v.tensor_copy(mix_bd[r, r], mix_c[r, :]))
            link(v.reduce_sum(mean[:, 2:3], t["mixer_b"][:, :], axis=AX.X))
            link(v.tensor_scalar(mean[:, 3:4], mean[:, 2:3], 1.0 / C, None, ALU.mult))
            link(v.tensor_tensor(y_const[:, :], t["mixer_own"][:, :], mean[:, 3:4], ALU.subtract))
            v.wait_ge(mm, 1)
            link(v.tensor_tensor(wi0_const[:, :], ps[:, 0:1], t["wi0_b"][:, :], ALU.add))

        @block.tensor
        def _(pe):
            pe.wait_ge(k.tables_loaded, 16 * n_loads)
            pe.matmul(ps[:, 0:1], t["wi0_sum"][:, :], t["comp_w_b"][:, :], start=True, stop=True).then_inc(mm, 1)


def dht(k):
    nc, t, x, B = k.nc, k.t, k.a["x"], k.B
    CH = 4
    KEEP = t["cas_n"].shape[2]
    NJ = C // CH
    loaded = [k.sem(f"dht_x_loaded{i}") for i in range(4)]
    cols_done, a1_done, stats_done = k.sem("dht_cols_done"), k.sem("dht_a1_done"), k.sem("dht_stats_done")
    modes_done, xm_done, rows_agg, rows_kept = (k.sem(n) for n in ("dht_modes_done", "dht_xm_done", "dht_rows_agg", "dht_rows_kept"))
    XM, MV = t["XM"], t["MV"]
    with ExitStack() as ctx:
        xa = [k.sb(f"dht_x{i}", [P, CH, 2, W], F32, ctx) for i in range(4)]
        A1 = [k.sb(f"dht_a1{u}", [P, 2, 2 * M, C], F32, ctx) for u in range(2)]
        ST = k.sb("dht_stats", [P, C, 6], F32, ctx)
        AG = k.sb("dht_agg", [P, 16, 2], F32, ctx)
        pad = k.sb("dht_pad", [P, 1], F32, ctx)
        psA = [ctx.enter_context(nc.psum_tensor(f"dht_psA{i}", [P, 2, 512], F32)) for i in range(2)]
        psX = [k.ps(f"dht_psX{u}", ctx) for u in range(2)]
        block = ctx.enter_context(nc.Block())

        @block.sync
        def _(sp):
            prime(sp, cols_done, a1_done, stats_done, modes_done, xm_done, rows_agg, rows_kept)
            load_table(k, sp, "cas_n", k.cas_loaded)
            with sp.Fori(0, B) as b:
                for j in range(NJ):
                    sp.wait_ge(cols_done, done(b * NJ + j - 4))
                    sp.wait_ge(stats_done, done(b * NJ + j - 4))
                    sp.dma_start(xa[j % 4][:, :, :, :],
                                 x[bass.ds(b, 1), CH * j:CH * j + CH].rearrange("a c (g p) w -> p (a c) g w", p=P))\
                      .then_inc(loaded[j % 4], 16)

        def images(eng, columns, both, modes):
            columns(0, 0)
            if B > 2:
                with eng.Fori(0, B // 2 - 1) as bh:
                    both(bh * 2 + 1, 1)
                    both(bh * 2 + 2, 0)
            both(B - 1, 1)
            modes(B - 1, 1)

        @block.tensor
        def _(pe):
            def columns_of(b, u, j):
                pe.wait_ge(loaded[j % 4], (b * 2 + j // 4 + 1) * 16)
                pe.wait_ge(a1_done, done(b * NJ + j - 2))
                ps = psA[j % 2][:, :, 0:4 * KEEP].rearrange("p k (c g n) -> p k c g n", c=2, g=2)
                for c in range(CH):
                    for g in range(2):
                        for hh in range(2):
                            last = pe.matmul(ps[:, c // 2, c % 2, g, :], xa[j % 4][:, c, hh, g * P:g * P + P],
                                             t["cas_n"][:, hh, :], start=hh == 0, stop=hh == 1)
                last.then_inc(cols_done, 1)

            def modes_of(b, u, j):
                if j == 0:
                    pe.wait_ge(a1_done, done(b * NJ + NJ - 1))
                    pe.wait_ge(xm_done, done(b - 2))
                for n in (2 * j, 2 * j + 1):
                    f, kg = n // 8, n % 8
                    for g in range(2):
                        last = pe.matmul(psX[u][:, n * M:(n + 1) * M],
                                         A1[u][:, g, f * M + 4 * kg:f * M + 4 * kg + 4, :],
                                         t["cas_n"][:, g, f * M:f * M + M], start=g == 0, stop=g == 1)
                if j == NJ - 1:
                    last.then_inc(modes_done, 1)

            def columns(b, u):
                for j in range(NJ):
                    columns_of(b, u, j)

            def both(b, u):
                for j in range(NJ):
                    columns_of(b, u, j)
                    modes_of(b - 1, 1 - u, j)

            def modes(b, u):
                for j in range(NJ):
                    modes_of(b, u, j)

            pe.wait_ge(k.cas_loaded, 16)
            images(pe, columns, both, modes)

        @block.scalar
        def _(act):
            def columns(b, u):
                act.wait_ge(modes_done, done(b - 2))
                for j in range(NJ):
                    act.wait_ge(cols_done, done(b * NJ + j))
                    for bank in range(2):
                        last = act.copy(A1[u][:, :, :, CH * j + 2 * bank:CH * j + 2 * bank + 2].rearrange("p g n c -> p c g n"),
                                        psA[j % 2][:, bank, 0:4 * KEEP].rearrange("p (c g n) -> p c g n", c=2, g=2)[:, :, :, 0:2 * M])
                    last.then_inc(a1_done, 1)

            def modes(b, u):
                act.wait_ge(modes_done, done(b))
                act.copy(XM[:, 0:2 * 8 * M, bass.ds(b, 1)], psX[u][:, :].rearrange("p (n a) -> p n a", a=1)).then_inc(xm_done, 1)

            def both(b, u):
                columns(b, u)
                modes(b - 1, 1 - u)

            for name in TABLES:
                if name != "cas_n":
                    load_table(k, act, name, k.tables_loaded)
            images(act, columns, both, modes)

        @block.vector
        def _(v):
            with v.Fori(0, B) as b:
                for j in range(NJ):
                    v.wait_ge(loaded[j % 4], (b * 2 + j // 4 + 1) * 16)
                    if j == 0:
                        v.wait_ge(rows_agg, done(b - 1))
                    for c in range(CH):
                        last = v.bn_stats(ST[:, CH * j + c, :], xa[j % 4][:, c, :, :].rearrange("p g w -> p (g w)"))
                    last.then_inc(stats_done, 1)
                v.wait_ge(stats_done, done(b * NJ + NJ - 1))
                v.wait_ge(rows_kept, done(b - 1))
                v.memset(pad[:, :], 0.0)
                for g in range(16):
                    last = v.bn_aggr(AG[:, g, :], ST[:, 2 * g:2 * g + 2, :].rearrange("p a s -> p (a s)"))
                last.then_inc(rows_agg, 1)
                v.wait_ge(rows_agg, done(b))
                v.tensor_copy(MV[:, bass.ds(b, 1), :, :], AG[:, :, :].rearrange("p (a g) s -> p a g s", a=1)).then_inc(rows_kept, 1)


def select_channels(v, link, dst, src, t, tmp, B):
    link(v.tensor_tensor(tmp, src, t["chan_mask"][:, :].unsqueeze(1).broadcast_to([P, B, 16]), ALU.mult))
    link(v.reduce_sum(dst, tmp, axis=AX.X))


def mix0(k):
    nc, t, B = k.nc, k.t, k.B
    XM, MV = t["XM"], t["MV"]
    chain, st_mm, w_loaded, w_ready, w_used = (k.sem(n) for n in
                                               ("mix0_chain", "mix0_stat_mm", "mix0_w_loaded", "mix0_w_ready", "mix0_w_used"))
    zs, z_done, xn_ready, z_ready, z_stored = (k.sem(n) for n in
                                               ("mix0_z_mm", "mix0_z_copied", "mix0_xm_ready", "mix0_z_ready", "mix0_z_stored"))
    st_in = k.sem("mix0_stat_in")
    NB = B * 16
    groups = [(kg, q) for kg in range(8) for q in range(3) if q == 1 or kg < 4 or (kg == 4 and q == 0)]
    before = [sum(g[0] < kg for g in groups) for kg in range(9)]
    with ExitStack() as ctx:
        Z = k.sb("Z", [P, 8, M, B], F32, ctx)
        ZB = k.sb("ZB", [P, B, 8, M], F32, ctx)
        tmp = k.sb("mix0_tmp", [P, 8, M, B], F32, ctx)
        w = [k.sb(f"mix0_w{i}", [P, 2, M, C], F32, ctx) for i in range(2)]
        wy = [k.sb(f"mix0_wy{i}", [P, 2, M, C], F32, ctx) for i in range(2)]
        sq = k.sb("mix0_sq", [P, B, 16], F32, ctx)
        mb = k.sb("mix0_mb", [P, B, 16], F32, ctx)
        s = {n: k.sb("mix0_" + n, [P, B], F32, ctx) for n in
             ("mean", "var", "r", "u", "v", "z00", "my", "cov", "vy", "p1", "p2")}
        ps = k.ps("mix0_ps", ctx)
        psZ = [ctx.enter_context(nc.psum_tensor(f"mix0_psZ{q}", [P, 2, 512], F32)) for q in range(3)]
        block = ctx.enter_context(nc.Block())
        mean1, invs, s1 = t["mean1"], t["invs"], t["s1"]

        @block.sync
        def _(sp):
            for kg in range(8):
                if kg >= 2:
                    sp.wait_ge(w_ready, kg - 1)
                sp.dma_start(w[kg % 2][:, :, :, :], k.a["l0_w"][kg]).then_inc(w_loaded, 16)
                sp.wait_ge(w_loaded, 16 * (kg + 1))
            sp.wait_ge(z_ready, 1)
            for q in range(4):
                for oj in range(4):
                    sp.dma_start(k.zd[oj, q].rearrange("b g o w -> o (b g) w"),
                                 ZB[32 * q + oj:32 * q + 32:4, :, :, :].rearrange("o b g w -> o (b g) w")).then_inc(z_stored, 16)
            sp.wait_ge(z_stored, 256)

        @block.tensor
        def _(pe):
            def avg(n, weights, src, width):
                pe.wait_ge(st_in, n)
                pe.matmul(ps[:, 0:width], weights, src, start=True, stop=True).then_inc(st_mm, 1)
            avg(1, t["ones_avg"][:, :], mb[:, :, :].rearrange("p b g -> p (b g)"), NB)
            avg(2, t["ones_avg"][:, :], sq[:, :, :].rearrange("p b g -> p (b g)"), NB)
            pe.wait_ge(xn_ready, 1)
            for n, (kg, q) in enumerate(groups):
                pe.wait_ge(w_ready, kg + 1)
                if kg >= 1:
                    pe.wait_ge(z_done, groups.index((kg - 1, q)) + 1)
                r = slice(32 * q, 32 * q + 32)
                for kw in range(M):
                    out = psZ[q][r, kw // 16, :].rearrange("p (n b) -> p n b", b=B)
                    unit = kw % 16
                    flipped = 31 if kw == 0 else 16 + (M - kw) - (17, 1)[kw // 16]
                    mode = kg * M + kw
                    for f in range(2):
                        first = f * 8 * M + mode
                        last = pe.matmul(out[:, unit:flipped + 1:flipped - unit, :], wy[kg % 2][r, f, kw, :],
                                         XM[r, first:first + 8 * M + 1:8 * M, :], start=f == 0, stop=f == 1)
                last.then_inc(zs, 1)
            avg(3, t["group_avg"][:, :], s["z00"][:, :], B)
            avg(4, t["group_avg"][:, :], s["p1"][:, :], B)
            avg(5, t["group_avg"][:, :], s["p2"][:, :], B)

        @block.scalar
        def _(act):
            def copy_own(q, kg):
                return act.mul(Z[32 * q:32 * q + 32, kg, :, :].rearrange("p (k w) b -> p k (w b)", k=2),
                               psZ[q][32 * q:32 * q + 32, :, 0:16 * B], 0.5 / NPX)

            def copy_flipped(q_to, kg_to, q):
                for bank, unit, w0, w1 in ((0, 31, 0, 0), (0, 16, 17, 31), (1, 16, 1, 16)):
                    last = act.mul(Z[32 * q_to:32 * q_to + 32, kg_to, w0:w1 + 1, :].rearrange("p w b -> p (w b)"),
                                   psZ[q][32 * q:32 * q + 32, bank, unit * B:(unit + w1 - w0 + 1) * B], 0.5 / NPX)
                return last
            for n, (kg, q) in enumerate(groups):
                act.wait_ge(zs, n + 1)
                last = copy_own(q, kg)
                if q == 0 and 1 <= kg <= 3:
                    last = copy_flipped(0, 8 - kg, q)
                if q >= 1:
                    last = copy_flipped(4 - q, 7 - kg, q)
                last.then_inc(z_done, 1)

        @block.vector
        def _(v):
            link = Chain(v, chain)
            v.tensor_copy(mb[:, :, :], MV[:, :, :, 0]).then_inc(st_in, 1)
            v.wait_ge(st_mm, 1)
            link(v.tensor_copy(mb[:, :, :], ps[:, 0:NB].rearrange("p (b g) -> p b g", g=16)))
            select_channels(v, link, s["mean"][:, :], mb[:, :, :], t, sq[:, :, :], B)
            link(v.tensor_tensor(sq[:, :, :], MV[:, :, :, 0], mb[:, :, :], ALU.subtract))
            link(v.tensor_tensor(sq[:, :, :], sq[:, :, :], sq[:, :, :], ALU.mult))
            v.tensor_tensor(sq[:, :, :], sq[:, :, :], MV[:, :, :, 1], ALU.add).then_inc(st_in, 1)
            v.wait_ge(st_mm, 2)
            link(v.tensor_copy(mb[:, :, :], ps[:, 0:NB].rearrange("p (b g) -> p b g", g=16)))
            select_channels(v, link, s["var"][:, :], mb[:, :, :], t, sq[:, :, :], B)
            link(v.tensor_scalar(s["u"][:, :], s["var"][:, :], 1e-5, None, ALU.add))
            rsqrt_chain(v, link, s["r"][:, :], s["u"][:, :], s["v"][:, :])
            link(v.tensor_scalar(s["v"][:, :], s["mean"][:, :], float(NPX), None, ALU.mult))
            for f in range(2):
                link(v.tensor_tensor(XM[0:32, f * 8 * M, :], XM[0:32, f * 8 * M, :], s["v"][0:32, :], ALU.subtract))
            link(v.tensor_tensor(XM[:, 0:2 * 8 * M, :], XM[:, 0:2 * 8 * M, :],
                                 s["r"][:, :].unsqueeze(1).broadcast_to([P, 2 * 8 * M, B]), ALU.mult))
            v.tensor_scalar(XM[:, 2 * 8 * M:3 * 8 * M, :], XM[:, 0:8 * M, :], -1.0, None, ALU.mult).then_inc(xn_ready, 1)
            for kg in range(8):
                v.wait_ge(w_loaded, 16 * (kg + 1))
                if kg >= 2:
                    v.wait_ge(zs, before[kg - 1])
                v.tensor_tensor(wy[kg % 2][:, 0, :, :], w[kg % 2][:, 0, :, :], w[kg % 2][:, 1, :, :], ALU.add)
                v.tensor_tensor(wy[kg % 2][:, 1, :, :], w[kg % 2][:, 0, :, :], w[kg % 2][:, 1, :, :], ALU.subtract)\
                 .then_inc(w_ready, 1)
            v.wait_ge(z_done, len(groups))
            v.wait_ge(xn_ready, 1)
            link(v.memset(s["z00"][:, :], 0.0))
            v.tensor_scalar(s["z00"][0:32, :], Z[0:32, 0, 0, :], 4.0, None, ALU.mult).then_inc(st_in, 1)
            v.wait_ge(st_mm, 3)
            link(v.tensor_copy(s["my"][:, :], ps[:, 0:B]))
            link(v.tensor_tensor(tmp[:, :, :, :].rearrange("p g w b -> p (g w) b"), XM[:, 0:8 * M, :],
                                 Z[:, :, :, :].rearrange("p g w b -> p (g w) b"), ALU.mult))
            link(v.reduce_sum(s["u"][:, :], tmp[:, :, :, :].rearrange("p g w b -> p b (g w)"), axis=AX.X))
            v.tensor_scalar(s["p1"][:, :], s["u"][:, :], 4.0 / NPX, None, ALU.mult).then_inc(st_in, 1)
            v.wait_ge(st_mm, 4)
            link(v.tensor_copy(s["cov"][:, :], ps[:, 0:B]))
            link(v.tensor_copy(tmp[:, :, :, :], Z[:, :, :, :]))
            link(v.tensor_tensor(tmp[0:32, 0, 0, :], tmp[0:32, 0, 0, :], s["my"][0:32, :], ALU.subtract))
            link(v.tensor_tensor(tmp[:, :, :, :], tmp[:, :, :, :], tmp[:, :, :, :], ALU.mult))
            link(v.reduce_sum(s["u"][:, :], tmp[:, :, :, :].rearrange("p g w b -> p b (g w)"), axis=AX.X))
            v.tensor_scalar(s["p2"][:, :], s["u"][:, :], 4.0, None, ALU.mult).then_inc(st_in, 1)
            v.wait_ge(st_mm, 5)
            link(v.tensor_copy(s["vy"][:, :], ps[:, 0:B]))
            link(v.tensor_scalar(s["u"][:, :], s["var"][:, :], 1e-5, None, ALU.add))
            link(v.tensor_tensor(s["u"][:, :], s["u"][:, :], s["r"][:, :], ALU.mult))
            link(v.tensor_tensor(s["cov"][:, :], s["cov"][:, :], s["u"][:, :], ALU.mult))
            link(v.tensor_scalar(s["cov"][:, :], s["cov"][:, :], 2.0, 1e-5, ALU.mult, ALU.add))
            link(v.tensor_tensor(s["cov"][:, :], s["cov"][:, :], s["var"][:, :], ALU.add))
            link(v.tensor_tensor(s["u"][:, :], s["cov"][:, :], s["vy"][:, :], ALU.add))
            rsqrt_chain(v, link, s1[:, :], s["u"][:, :], s["v"][:, :])
            link(v.tensor_tensor(invs[:, :], s["u"][:, :], s1[:, :], ALU.mult))
            link(v.tensor_tensor(mean1[:, :], s["mean"][:, :], s["my"][:, :], ALU.add))
            link(v.tensor_tensor(s["v"][:, :], mean1[:, :], s1[:, :], ALU.mult))
            link(v.tensor_tensor(ZB[:, :, :, :].rearrange("p b g w -> p b (g w)"),
                                 Z[:, :, :, :].rearrange("p g w b -> p b (g w)"),
                                 s1[:, :].unsqueeze(2).broadcast_to([P, B, 8 * M]), ALU.mult))
            v.tensor_tensor(ZB[0:32, :, 0, 0], ZB[0:32, :, 0, 0], s["v"][0:32, :], ALU.subtract).then_inc(z_ready, 1)


def rows0(k):
    nc, t, B = k.nc, k.t, k.B
    z_loaded = [k.sem(f"rows0_z_loaded{i}") for i in range(2)]
    v_stored = [k.sem(f"rows0_v_stored{i}") for i in range(2)]
    mm_done = k.sem("rows0_mm_done")
    copied = [k.sem(f"rows0_copied_{n}") for n in ("act", "dve")]
    GR = 4
    with ExitStack() as ctx:
        ZT = [k.sb(f"ZT{i}", [P, 8, M], F32, ctx) for i in range(2)]
        V = [k.sb(f"V{i}", [M, HP, P], F32, ctx) for i in range(2)]
        ps = [k.ps(f"rows0_ps{i}", ctx) for i in range(GR)]
        block = ctx.enter_context(nc.Block())

        def image(b, u):
            return b * 2 + u

        def copies(eng, copy, bh, u, half):
            eng.wait_ge(v_stored[u], bh * 16 + 16)
            for n in range(half, GR, 2):
                eng.wait_ge(mm_done, image(bh, u) * GR + n + 1 + PRIME)
                for g in range(4):
                    c0 = (4 * (n // 2) + g) * 4 + 2 * (n % 2)
                    dst = V[u][:, :, :].rearrange("k h (p j c) -> k c j p h", p=2, j=2)
                    src = ps[n][M * g:M * g + M, :].rearrange("k (c j p h) -> k c j p h", c=2, j=2, p=2)
                    for hj in range(2):
                        last = copy(dst[:, c0:c0 + 2, hj, :, :], src[:, :, hj, :, :])
                last.then_inc(copied[half], 1)

        @block.sync
        def _(sp):
            prime(sp, mm_done, *copied)
            for u in range(2):
                sp.sem_inc(v_stored[u], 16)
            with sp.Fori(0, B // 2) as bh:
                for u in range(2):
                    if u == 0:
                        sp.wait_ge(mm_done, bh * (2 * GR) + PRIME)
                    sp.dma_start(ZT[u][:, :, :],
                                 k.zd[:, :, bass.ds(bh * 2 + u, 1)].rearrange("j q a g o w -> (j q a) g (o w)"))\
                      .then_inc(z_loaded[u], 16)
                for u in range(2):
                    for done_copies in copied:
                        sp.wait_ge(done_copies, image(bh, u) * (GR // 2) + GR // 2 + PRIME)
                    sp.dma_start(k.vd[bass.ds(bh * 2 + u, 1)].rearrange("a k h q -> (a k) h q"), V[u][:, :, :])\
                      .then_inc(v_stored[u], 16)
            for u in range(2):
                sp.wait_ge(v_stored[u], 16 * (B // 2) + 16)

        @block.tensor
        def _(pe):
            with pe.Fori(0, B // 2) as bh:
                for u in range(2):
                    pe.wait_ge(z_loaded[u], bh * 16 + 16)
                    for n in range(GR):
                        pe.wait_ge(copied[n % 2], image(bh, u) * (GR // 2) + n // 2 + 1 - GR // 2 + PRIME)
                        pe.matmul(ps[n][:, :], ZT[u][:, 4 * (n // 2):4 * (n // 2) + 4, :].rearrange("q g w -> q (g w)"),
                                  t["cas_bd"][:, 512 * (n % 2):512 * (n % 2) + 512],
                                  start=True, stop=True).then_inc(mm_done, 1)

        @block.scalar
        def _(act):
            with act.Fori(0, B // 2) as bh:
                for u in range(2):
                    copies(act, act.copy, bh, u, 0)

        @block.vector
        def _(v):
            with v.Fori(0, B // 2) as bh:
                for u in range(2):
                    copies(v, v.tensor_copy, bh, u, 1)


NSTEP = ITERS * STEPS


class Step:

    def __init__(self, b, i, s, edge=None):
        self.b, self.i, self.s, self.edge = b, i, s, edge

    def n(self, lag):
        return self.b * NSTEP + self.i * STEPS + (self.s - lag)

    def it(self, lag):
        return self.b * ITERS + self.i + (self.s - lag) // STEPS

    def pair(self, lag):
        return self.b * (NSTEP // 2) + self.i * (STEPS // 2) + (self.s - lag) // 2

    def row(self, lag):
        h0 = self.i * (ROWS * STEPS) + ROWS * (self.s - lag)
        return h0 % HP if isinstance(h0, int) else h0

    def slot(self, lag, of):
        return (self.s - lag) % of

    def live(self, lag):
        m = self.i * STEPS + self.s - lag if self.edge else None
        return m >= 0 if self.edge == "first" else m < 0 if self.edge == "last" else True

    def opens_image(self, lag):
        return isinstance(self.i, int) and self.edge != "last" and self.i * STEPS + self.s == lag


def turns_and_ends(eng, B, step, end):
    def first_turns(b, edge):
        for s in range(STEPS):
            step(Step(b, 0, s, edge))

    def other_turns(b):
        with eng.Fori(1, ITERS) as i:
            for s in range(STEPS):
                step(Step(b, i, s))
    first_turns(0, "first")
    with eng.Fori(1, B) as b:
        other_turns(b - 1)
        first_turns(b, None)
        end(b - 1, False)
    other_turns(B - 1)
    first_turns(B, "last")
    end(B - 1, True)


def forward(k):
    nc, t, x, B = k.nc, k.t, k.a["x"], k.B
    XH, s1 = t["XH"], t["s1"]
    x_loaded = [k.sem(f"fw_x_loaded{u}") for u in range(2)]
    v_loaded = [k.sem(f"fw_v_loaded{u}") for u in range(2)]
    xn_stored = [k.sem(f"fw_xn_stored{u}") for u in range(2)]
    names = ("y_done", "xn_done", "xt_done", "xt_copied", "l0_done", "p0_done", "g0_done", "l1_done", "p1_done", "g1_done", "gm_done",
             "gm_copied", "xw_done", "xwa_done", "xs_done", "xb_done",
             "bt_done", "bt_copied", "bt_half_copied", "b0_done", "b0_added", "b0_gelu", "b1_done", "b1_added", "b1_gelu", "e_done", "e_copied", "xh_done", "xh_copied")
    S = {n: k.sem("fw_" + n) for n in names}
    zeroed = k.sem("fw_zeroed")
    N = ROWS * W
    with ExitStack() as ctx:
        sb = lambda name, shape: k.sb("fw_" + name, shape, F32, ctx)
        xin = [sb(f"x{u}", [P, CHUNK * W]) for u in range(2)]
        vch = [sb(f"v{u}", [M, CHUNK, P]) for u in range(2)]
        xn = [sb(f"xn{u}", [P, CHUNK * W]) for u in range(2)]
        h1 = [sb(f"h1{u}", [P, 2, ROWS, W]) for u in range(2)]
        h2 = [sb(f"h2{u}", [P, 2, ROWS, 2, P]) for u in range(2)]
        xT = [sb(f"xT{u}", [P, ROWS, 2, P]) for u in range(4)]
        coord_w = sb("coord_w", [P, W])
        coord_h = sb("coord_h", [P, 2, HP])
        gt = sb("gt", [P, ROWS, 2, 2, C])
        xs = sb("xs", [P, 8])
        xb = sb("xb", [P, 8, HID])
        xwa = sb("xwa", [P, 2 * M, HP])
        xwT = sb("xwT", [P, M, 2, HID])
        hb1 = sb("hb1", [P, M, 2, HP])
        hb2 = sb("hb2", [P, M, 2, HID + 1])
        et = sb("et", [HID + 1, 2, 8, 4, C])
        psY, psT, psG, psW = (k.ps("fw_ps" + n, ctx) for n in "YTGW")
        psL0 = [k.ps(f"fw_psL0{p}", ctx) for p in range(2)]
        psL1 = [k.ps(f"fw_psL1{p}", ctx) for p in range(2)]
        block = ctx.enter_context(nc.Block())
        x_v = x.rearrange("b c (j p i u r) w -> b j p u i c (r w)", j=2, p=2, i=ITERS, u=2)
        v_v = k.vd.rearrange("b k (i u r) q -> b u i k (r q)", i=ITERS, u=2)

        def copy_xwT(copy, i, m2):
            src = (psT, psY)[i % 2][HID * m2:HID * m2 + HID, :].rearrange("q (a r p c) -> q a r p c", a=2, r=2, p=2)
            for p in range(2):
                last = copy(xwT[HP * p:HP * p + HP, 4 * i + m2:4 * i + m2 + 3:2, :, :], src[:, :, :, p, :])
            return last

        @block.sync
        def _(sp):
            prime(sp, *S.values())
            for u in range(2):
                sp.sem_inc(xn_stored[u], 16)
            with sp.Fori(0, B) as b:
                with sp.Fori(0, ITERS) as i:
                    for u in range(2):
                        sp.wait_ge(S["xn_done"], done((b * ITERS + i) * STEPS + 2 * u - 3))
                        sp.dma_start(vch[u][:, :, :], v_v[bass.ds(b, 1), u, bass.ds(i, 1)]
                                     .rearrange("a e k (r q) -> (a e k) r q", r=CHUNK)).then_inc(v_loaded[u], 16)
                        for q in range(4):
                            sp.dma_start(xin[u][32 * q:32 * q + 32, :],
                                         x_v[bass.ds(b, 1), q % 2, q // 2, u, bass.ds(i, 1)]
                                         .rearrange("a e c n -> (a e c) n")).then_inc(x_loaded[u], 16)
            for u in range(2):
                sp.wait_ge(xn_stored[u], B * ITERS * 16 + 16)

        @block.tensor
        def _(pe):
            def step(st):
                s = st.s
                if st.live(0):
                    n = st.n(0)
                    if s % 2 == 0:
                        pe.wait_ge(v_loaded[s // 2], (st.it(0) + 1) * 16)
                    pe.wait_ge(S["xn_done"], done(n - 1))
                    for r in range(ROWS):
                        last = pe.matmul(psY[:, r * W:r * W + W], vch[s // 2][:, (s % 2) * ROWS + r, :], t["cas_k"][:, :],
                                         start=True, stop=True)
                    last.then_inc(S["y_done"], 1)
                if st.live(1):
                    n, c = st.n(1), st.slot(1, 4)
                    pe.wait_ge(S["xn_done"], done(n))
                    pe.wait_ge(S["xt_copied"], done(n - 1))
                    for r in range(ROWS):
                        for g in range(2):
                            o = (c % 2) * N + r * W + g * P
                            last = pe.transpose(psT[:, (2 * r + g) * P:(2 * r + g) * P + P],
                                                xn[c // 2][:, o:o + P], t["ident"][:, :])
                    last.then_inc(S["xt_done"], 1)
                    for p in range(2):
                        pe.wait_ge(S["p0_done"], done(2 * (n - 1) + p))
                        pe.matmul(psL0[p][:, :], t["bw0"][:, p, :], xn[c // 2][:, (c % 2) * N:(c % 2) * N + N],
                                  start=True, stop=True).then_inc(S["l0_done"], 1)
                if st.live(4):
                    n, c = st.n(4), st.slot(4, 4)
                    pe.wait_ge(S["gm_copied"], done(n))
                    if c == 0:
                        pe.wait_ge(S["xwa_done"], done(st.it(4) - 1))
                    for r in range(ROWS):
                        for p in range(2):
                            last = pe.matmul(psW[p * HID:p * HID + HID, (ROWS * c + r) * HID:(ROWS * c + r + 1) * HID],
                                             gt[:, r, p, :, :], t["bw2"][:, :], start=True, stop=True)
                    last.then_inc(S["xw_done"], 1)
                if st.live(3):
                    n, c = st.n(3), st.slot(3, 4)
                    pe.wait_ge(S["g1_done"], done(2 * n + 1))
                    pe.wait_ge(S["xt_copied"], done(n))
                    pe.wait_ge(S["gm_copied"], done(n - 1))
                    for r in range(ROWS):
                        for p in range(2):
                            for g in range(2):
                                last = pe.matmul(psG[:, (2 * r + p) * HID:(2 * r + p) * HID + HID], h2[c % 2][:, p, r, g, :],
                                                 xT[c][:, r, g, p * HID:p * HID + HID], start=g == 0, stop=g == 1)
                    last.then_inc(S["gm_done"], 1)
                if st.live(2):
                    n, u = st.n(2), st.slot(2, 2)
                    for p in range(2):
                        pe.wait_ge(S["g0_done"], done(2 * n + p))
                        pe.wait_ge(S["p1_done"], done(2 * (n - 1) + p))
                        for r in range(ROWS):
                            for g in range(2):
                                last = pe.matmul(psL1[p][:, (2 * r + g) * P:(2 * r + g) * P + P],
                                                 h1[u][:, p, r, g * P:g * P + P], t["bw1"][:, :], start=True, stop=True)
                        last.then_inc(S["l1_done"], 1)

            def basis_h(b, last_image):
                end = (b + 1) * NSTEP - 1
                ahead = 0 if last_image else STEPS
                pe.wait_ge(S["xn_done"], done(end + ahead))
                pe.wait_ge(S["xt_copied"], done(end + max(ahead - 1, 0)))
                pe.wait_ge(S["p0_done"], done(2 * (end + max(ahead - 1, 0)) + 1))
                pe.wait_ge(S["gm_copied"], done(end + max(ahead - 3, 0)))
                pe.wait_ge(S["xwa_done"], done(b * ITERS + ITERS - 1))
                for i in range(8):
                    pe.wait_ge(S["bt_copied"], done(8 * b + i - 2))
                    pe.wait_ge(S["bt_half_copied"], done(8 * b + i - 2))
                    for j in range(4):
                        mp, ri = 2 * i + j // 2, j % 2
                        last = pe.transpose((psT, psY)[i % 2][:, j * P:j * P + P],
                                            xwa[:, ri * M + 2 * mp:ri * M + 2 * mp + 2, :].rearrange("p m h -> p (m h)"),
                                            t["ident"][:, :])
                    last.then_inc(S["bt_done"], 1)
                for i in range(8):
                    mg, p = i // 2, i % 2
                    pe.wait_ge(S["b0_added"], done(8 * b + i - 2))
                    pe.matmul(psL0[p][:, :], t["bh0"][:, p, :], xwa[:, 8 * mg:8 * mg + 8, :].rearrange("p m h -> p (m h)"),
                              start=True, stop=True).then_inc(S["b0_done"], 1)
                for i in range(8):
                    pe.wait_ge(S["b0_gelu"], done(8 * b + 2 * (i // 2) + 1))
                    pe.wait_ge(S["b1_added"], done(8 * b + i - 2))
                    ps = (psG, psW)[i % 2]
                    for j in range(4):
                        last = pe.matmul(ps[:, j * P:j * P + P], hb1[:, 4 * i + j, :, :].rearrange("q p h -> q (p h)"),
                                         t["bh1"][:, :], start=True, stop=True)
                    last.then_inc(S["b1_done"], 1)
                pe.wait_ge(S["bt_copied"], done(8 * b + 7))
                pe.wait_ge(S["bt_half_copied"], done(8 * b + 7))
                for i in range(4):
                    pe.wait_ge(S["b1_gelu"], done(8 * b + 2 * i + 1))
                    for j in range(8):
                        for hj in range(2):
                            last = pe.matmul((psT, psY, psL0[0], psL0[1])[i][0:HID + 1, j * HID:j * HID + HID],
                                             hb2[:, 8 * i + j, hj, :], xwT[:, 8 * i + j, :, hj * C:hj * C + C],
                                             start=hj == 0, stop=hj == 1)
                    last.then_inc(S["e_done"], 1)
                pe.wait_ge(S["e_copied"], done(4 * b + 3))
                for m8 in range(8):
                    for ri in range(2):
                        last = pe.matmul(psG[:, m8 * HID:m8 * HID + HID], et[:, ri, m8, :, :].rearrange("f g c -> f (g c)"), t["bh2"][:, ri, :],
                                         start=ri == 0, stop=ri == 1)
                last.then_inc(S["xh_done"], 1)
                pe.wait_ge(S["xh_copied"], done(b))

            turns_and_ends(pe, B, step, basis_h)

        @block.scalar
        def _(act):
            def step(st):
                if st.live(3):
                    n, u = st.n(3), st.slot(3, 2)
                    for p in range(2):
                        act.wait_ge(S["p1_done"], done(2 * n + p))
                        y = h2[u][:, p, :, :, :].rearrange("q r g f -> q (r g f)")
                        act.activation(y, y, ACT.Gelu).then_inc(S["g1_done"], 1)
                if st.live(1):
                    n, u = st.n(1), st.slot(1, 2)
                    for p in range(2):
                        act.wait_ge(S["p0_done"], done(2 * n + p))
                        y = h1[u][:, p, :, :].rearrange("q r w -> q (r w)")
                        act.activation(y, y, ACT.Gelu, bias=t["bw0_b"][:, :]).then_inc(S["g0_done"], 1)
                if st.s % 2 == 1 and st.live(0):
                    u = st.s // 2
                    act.wait_ge(S["xn_done"], done(st.n(0)))
                    act.dma_start(k.xnd[bass.ds(st.b * (2 * ITERS) + 2 * st.i + u, 1)].rearrange("a p n -> (a p) n"),
                                  xn[u][:, :]).then_inc(xn_stored[u], 16)

            def basis_h(b, last_image):
                for i in range(8):
                    act.wait_ge(S["bt_done"], done(8 * b + i))
                    act.wait_ge(S["e_done"], done(4 * b - 1))
                    copy_xwT(act.copy, i, 1).then_inc(S["bt_half_copied"], 1)
                for i in range(8):
                    mg, p = i // 2, i % 2
                    act.wait_ge(S["b0_added"], done(8 * b + i))
                    y = hb1[:, 8 * mg:8 * mg + 8, p, :]
                    act.activation(y, y, ACT.Gelu, bias=t["bh0_b"][:, :]).then_inc(S["b0_gelu"], 1)
                for i in range(8):
                    act.wait_ge(S["b1_added"], done(8 * b + i))
                    y = hb2[:, 4 * i:4 * i + 4, :, 0:HID].rearrange("q m j f -> q (m j) f")
                    act.activation(y, y, ACT.Gelu).then_inc(S["b1_gelu"], 1)

            turns_and_ends(act, B, step, basis_h)

        @block.vector
        def _(v):
            def step(st):
                s = st.s
                if st.live(3):
                    n, u = st.n(3), st.slot(3, 2)
                    for p in range(2):
                        v.wait_ge(S["l1_done"], done(2 * n + p))
                        v.wait_ge(S["gm_done"], done(n - 2))
                        v.tensor_tensor(h2[u][:, p, :, :, :].rearrange("q r g (j f) -> q (r g j) f", j=2),
                                        psL1[p][:, :].rearrange("q (a f) -> q a f", f=HID),
                                        t["bw1_row"][:, :].unsqueeze(1).broadcast_to([P, 8, HID]), ALU.add).then_inc(S["p1_done"], 1)
                if st.live(0):
                    n = st.n(0)
                    u, cols = s // 2, slice((s % 2) * N, (s % 2) * N + N)
                    if s % 2 == 0:
                        v.wait_ge(x_loaded[u], (st.it(0) + 1) * 64)
                        v.wait_ge(xn_stored[u], (st.it(0) + 1) * 16)
                        v.wait_ge(S["l0_done"], done(2 * (n - 3) + 1))
                        v.wait_ge(S["xs_done"], done(n - 3))
                    v.wait_ge(S["y_done"], done(n))
                    v.scalar_tensor_tensor(xn[u][:, cols], xin[u][:, cols], s1[:, bass.ds(st.b, 1)], psY[:, :],
                                           ALU.mult, ALU.add).then_inc(S["xn_done"], 1)
                if st.live(1):
                    n, u, c = st.n(1), st.slot(1, 2), st.slot(1, 4)
                    v.wait_ge(S["xt_done"], done(n))
                    v.wait_ge(S["gm_done"], done(n - 4))
                    v.tensor_copy(xT[c][:, :, :, :].rearrange("q r g c -> q (r g c)"), psT[:, :]).then_inc(S["xt_copied"], 1)
                    for p in range(2):
                        v.wait_ge(S["l0_done"], done(2 * n + p))
                        v.wait_ge(S["l1_done"], done(2 * (n - 2) + p))
                        v.tensor_tensor(h1[u][:, p, :, :], psL0[p][:, :].rearrange("q (r w) -> q r w", r=ROWS),
                                        coord_w[:, :].unsqueeze(1).broadcast_to([P, ROWS, W]), ALU.add).then_inc(S["p0_done"], 1)
                    if c == 0:
                        v.wait_ge(S["xb_done"], done(st.it(1) - 1))
                    v.wait_ge(S["xn_done"], done(n))
                    v.reduce_sum(xs[:, ROWS * c:ROWS * c + ROWS],
                                 xn[c // 2][:, (c % 2) * N:(c % 2) * N + N].rearrange("q (r w) -> q r w", r=ROWS),
                                 axis=AX.X).then_inc(S["xs_done"], 1)
                if s == 3 and st.live(4):
                    it, i = st.it(4), st.i - 1
                    v.wait_ge(S["xw_done"], done(st.n(4)))
                    v.wait_ge(S["xb_done"], done(it))
                    own = st.b - 1 if isinstance(st.i, int) else st.b
                    v.wait_ge(S["b0_done"], done(8 * own - 1))
                    v.wait_ge(S["bt_done"], done(8 * own - 1))
                    at = slice(HP - 8, HP) if isinstance(i, int) else bass.ds(i * 8, 8)
                    v.tensor_tensor(xwa[:, :, at], psW[:, :].rearrange("q (h m) -> q m h", h=8),
                                    xb[:, :, :].rearrange("q h m -> q m h"), ALU.add).then_inc(S["xwa_done"], 1)
                if st.live(3):
                    n = st.n(3)
                    v.wait_ge(S["gm_done"], done(n))
                    v.wait_ge(S["xw_done"], done(n - 1))
                    for hj in range(2):
                        r = slice(HID * hj, HID * hj + HID)
                        last = v.tensor_copy(gt[r, :, :, hj, :].rearrange("q r p c -> q (r p) c"),
                                             psG[r, 0:4 * HID].rearrange("q (a c) -> q a c", c=HID)[:, :, hj * C:hj * C + C])
                    last.then_inc(S["gm_copied"], 1)

            def basis_h(b, last_image):
                for i in range(8):
                    v.wait_ge(S["bt_done"], done(8 * b + i))
                    v.wait_ge(S["e_done"], done(4 * b - 1))
                    copy_xwT(v.tensor_copy, i, 0).then_inc(S["bt_copied"], 1)
                for i in range(8):
                    mg, p = i // 2, i % 2
                    v.wait_ge(S["b0_done"], done(8 * b + i))
                    v.wait_ge(S["b1_done"], done(8 * b - 1))
                    v.tensor_tensor(hb1[:, 8 * mg:8 * mg + 8, p, :], psL0[p][:, :].rearrange("q (m h) -> q m h", m=8),
                                    coord_h[:, p, :].unsqueeze(1).broadcast_to([P, 8, HP]), ALU.add).then_inc(S["b0_added"], 1)
                for i in range(8):
                    v.wait_ge(S["b1_done"], done(8 * b + i))
                    v.wait_ge(S["e_done"], done(4 * b - 1))
                    v.tensor_tensor(hb2[:, 4 * i:4 * i + 4, :, 0:HID].rearrange("q m j f -> q (m j) f"),
                                    (psG, psW)[i % 2][:, :].rearrange("q (a f) -> q a f", f=HID),
                                    t["bh1_row"][:, :].unsqueeze(1).broadcast_to([P, 8, HID]), ALU.add).then_inc(S["b1_added"], 1)
                for i in range(4):
                    v.wait_ge(S["e_done"], done(4 * b + i))
                    v.wait_ge(S["xh_done"], done(b - 1))
                    last = v.tensor_copy(et[:, :, :, i, :].rearrange("q r m c -> q m r c"),
                                         (psT, psY, psL0[0], psL0[1])[i][0:HID + 1, :].rearrange("q (m r c) -> q m r c", m=8, r=2))
                    last.then_inc(S["e_copied"], 1)
                v.wait_ge(S["xh_done"], done(b))
                v.tensor_copy(XH[:, :, bass.ds(b, 1)], psG[:, :].rearrange("q (n a) -> q n a", a=1)).then_inc(S["xh_copied"], 1)

            v.memset(hb2[:, :, :, HID:HID + 1], 1.0)
            v.tensor_scalar(coord_w[:, :], t["wc_row"][:, :], t["bw0_c"][:, :], None, ALU.mult)
            v.tensor_scalar(coord_h[:, :, :], t["hc_rows"][:, :, :], t["bh0_c"][:, :], None, ALU.mult)
            v.memset(gt[:, :, :, :, :], 0.0).then_inc(zeroed, 1)
            v.wait_ge(zeroed, 1)
            turns_and_ends(v, B, step, basis_h)

        @block.gpsimd
        def _(g):
            with g.Fori(0, B * ITERS) as it:
                g.wait_ge(S["xs_done"], done(it * STEPS + STEPS - 1))
                g.wait_ge(S["xwa_done"], done(it - 1))
                g.tensor_tensor(xb[:, :, :], t["bw2_b"][:, :].unsqueeze(1).broadcast_to([P, 8, HID]),
                                xs[:, :].unsqueeze(2).broadcast_to([P, 8, HID]), ALU.mult).then_inc(S["xb_done"], 1)


def mix1(k):
    nc, t, B = k.nc, k.t, k.B
    XH = t["XH"]
    stacked = [k.sem(f"mix1_stacked{part}") for part in range(4)]
    w_loaded = [k.sem(f"mix1_w_loaded{u}") for u in range(2)]
    stored = [k.sem(f"mix1_stored{u}") for u in range(2)]
    zeroed, w_ready, mm_done, copied = (k.sem(n) for n in ("mix1_zeroed", "mix1_w_ready", "mix1_mm_done", "mix1_copied"))
    with ExitStack() as ctx:
        XS = [k.sb(f"mix1_x{gh}", [P, 8, M, B], F32, ctx) for gh in range(2)]
        wb = [k.sb(f"mix1_w{u}", [P, 2, M, 2, C], F32, ctx) for u in range(2)]
        xf = [k.sb(f"mix1_xf{u}", [B, 2, M, 2, C], F32, ctx) for u in range(2)]
        ps = [k.ps(f"mix1_ps{i}", ctx) for i in range(4)]
        block = ctx.enter_context(nc.Block())
        units = [(gh, m8) for gh in range(2) for m8 in range(8)]
        BANKS = M // 4
        rows = lambda gl, ri: slice((2 * gl + ri) * C, (2 * gl + ri) * C + C)

        @block.sync
        def _(sp):
            def store(n):
                gh, m8 = units[n]
                sp.wait_ge(copied, BANKS * (n + 1))
                for ri in range(2):
                    sp.dma_start(k.xfd[m8, :, ri, :, 2 * gh:2 * gh + 2].rearrange("b k g o -> b k (g o)"),
                                 xf[n % 2][:, ri, :, :, :].rearrange("b k g o -> b k (g o)")).then_inc(stored[n % 2], 16)

            def load(n):
                gh, m8 = units[n]
                for gl in range(2):
                    g = 2 * gh + gl
                    sp.dma_start(wb[n % 2][rows(gl, 0), gl, :, :, :].rearrange("c k r o -> c (k r o)"),
                                 k.a["l1_w"][m8, C * g:C * g + C].rearrange("c k r o -> c (k r o)")).then_inc(w_loaded[n % 2], 16)
            for n in range(len(units)):
                if n >= 2:
                    sp.wait_ge(mm_done, BANKS * (n - 1))
                load(n)
                if n >= 1:
                    store(n - 1)
            store(len(units) - 1)
            for u in range(2):
                sp.wait_ge(stored[u], 32 * len(units) // 2)

        @block.gpsimd
        def _(g):
            for u in range(2):
                g.memset(wb[u][0:2 * C, 1, :, :, :], 0.0)
                g.memset(wb[u][2 * C:P, 0, :, :, :], 0.0).then_inc(zeroed, 1)

        @block.vector
        def _(v):
            for n in range(len(units)):
                v.wait_ge(w_loaded[n % 2], 32 * (n // 2 + 1))
                if n >= 2:
                    v.wait_ge(mm_done, BANKS * (n - 1))
                for gl in range(2):
                    w = wb[n % 2]
                    v.tensor_scalar(w[rows(gl, 1), gl, :, 0, :], w[rows(gl, 0), gl, :, 1, :], -1.0, None, ALU.mult)
                    last = v.tensor_copy(w[rows(gl, 1), gl, :, 1, :], w[rows(gl, 0), gl, :, 0, :])
                last.then_inc(w_ready, 1)

        @block.tensor
        def _(pe):
            for n, (gh, m8) in enumerate(units):
                pe.wait_ge(w_ready, n + 1)
                if n < 2:
                    pe.wait_ge(zeroed, n + 1)
                if m8 % 4 == 0:
                    pe.wait_ge(stacked[2 * gh + m8 // 4], 64)
                for j in range(BANKS):
                    g = BANKS * n + j
                    if g >= 4:
                        pe.wait_ge(copied, g - 3)
                    for i in range(4):
                        kk = 4 * j + i
                        last = pe.matmul(ps[g % 4][0:B, P * i:P * i + P], XS[gh][:, m8, kk, :], wb[n % 2][:, :, kk, :, :],
                                         start=True, stop=True)
                    last.then_inc(mm_done, 1)

        @block.scalar
        def _(act):
            for part in range(4):
                gh, m = part // 2, slice(4 * (part % 2), 4 * (part % 2) + 4)
                for gl in range(2):
                    for ri in range(2):
                        g = 2 * gh + gl
                        act.dma_start(XS[gh][rows(gl, ri), m, :, :].rearrange("c m k b -> c m (k b)"),
                                      XH[C * g:C * g + C, :, :].rearrange("c (m r k) b -> c m r (k b)", m=8, r=2)[:, m, ri, :])\
                           .then_inc(stacked[part], 16)
            for n in range(len(units)):
                if n >= 2:
                    act.wait_ge(stored[n % 2], 32 * (n // 2))
                for j in range(BANKS):
                    g = BANKS * n + j
                    act.wait_ge(mm_done, g + 1)
                    act.copy(xf[n % 2][:, :, 4 * j:4 * j + 4, :, :].rearrange("b r k g o -> b (k g) r o"),
                             ps[g % 4][0:B, :].rearrange("b (k r o) -> b k r o", k=8, r=2)).then_inc(copied, 1)


HEAD = 3


def all_steps(eng, B, image, step, last_lag):
    def head(b, edge):
        image(b)
        for s in range(HEAD * STEPS):
            step(Step(b, s // STEPS, s % STEPS, edge))

    def body(b):
        with eng.Fori(HEAD, ITERS) as i:
            for s in range(STEPS):
                step(Step(b, i, s))
    head(0, "first")
    with eng.Fori(1, B) as b:
        body(b - 1)
        head(b, None)
    body(B - 1)
    for s in range(last_lag):
        step(Step(B, s // STEPS, s % STEPS, "last"))


def inverse(k):
    nc, t, B = k.nc, k.t, k.B
    XF_LOADED, OUT = k.sem("iv_xf_loaded"), k.out
    xn_loaded = [k.sem(f"iv_xn_loaded{u}") for u in range(2)]
    out_stored = [k.sem(f"iv_out_stored{u}") for u in range(2)]
    yb_stored = k.sem("iv_yb_stored")
    yb_loaded = [k.sem(f"iv_yb_loaded{u}") for u in range(2)]
    zeroed = k.sem("iv_zeroed")
    names = ("pre_done", "g1_done", "l1_done", "g2_done", "tp_done", "tp_copied", "y_done", "yc_done", "sq_done",
             "sum_done", "rs_done", "yn_done", "tr_done", "gy_done", "sc_done", "t_done", "gs_done",
             "res_done", "out_done", "yt_done", "yt_copied", "ivm_set", "cw0_sum", "cw1_sum", "cw_term", "by_sum",
             "cond_done", "cond_copied", "td_done", "td_copied", "ah_done", "ah_copied", "hg0_done", "hl1_done",
             "hg1_done", "r_done", "r_copied", "aw_done", "rh_done", "rh_copied", "rt_done", "rt_copied", "rt_half_copied", "aw_copied", "newton", "held")
    S = {n: k.sem("iv_" + n) for n in names}
    N = ROWS * W
    with ExitStack() as ctx:
        sb = lambda name, shape: k.sb("iv_" + name, shape, F32, ctx)
        two = lambda name, shape: [sb(f"{name}{u}", shape) for u in range(2)]
        xfk = sb("xfk", [2 * M, 2, 16, C])
        ch = sb("ch", [C, 2, 2, 16])
        tb_row = sb("tb_row", [P, 16])
        td = sb("td", [P, 16, 2, 2, C])
        ah = sb("ah", [P, 16])
        ha = sb("ha", [P, 16, H])
        hb = sb("hb", [P, 16, H])
        R = sb("R", [P, 16, H])
        rh = ha[:, :, :].rearrange("q a (u n) -> q (a u n)", u=2).rearrange("q (j o c) -> q j o c", j=2, o=C)
        rt = sb("rt", [P, C, P])
        aw = sb("aw", [P, P])
        yb = sb("yb", [P, HP])
        ybt = sb("ybt", [HP, P])
        ybb = [sb(f"ybb{u}", [P, CHUNK, P]) for u in range(2)]
        cw = two("cw", [P, H])
        cw_term = sb("cw_term", [P, H])
        by = sb("by", [P, H])
        wc_w = sb("wc_w", [P, W])
        ivm = sb("ivm", [P, 2])
        pre, wg1, wg2 = two("pre", [P, 2, ROWS, W]), two("wg1", [P, 2, ROWS, W]), two("wg2", [P, 2, ROWS, W])
        tp = sb("tp", [P, 8, 2, 2, C])
        yc = [sb(f"yc{i}", [P, N]) for i in range(4)]
        sq, yn, gy, tt, gs = (two(n, [P, N]) for n in ("sq", "yn", "gy", "tt", "gs"))
        res = [sb(f"res{i}", [P, N]) for i in range(4)]
        vs, xv, xh, nt = (sb(n, [P, 32]) for n in ("vs", "xv", "xh", "nt"))
        rs = two("rs", [P, 32])
        xn, osb = two("xn", [P, CHUNK * W]), two("osb", [P, CHUNK * W])
        psL = ctx.enter_context(nc.psum_tensor("iv_psL", [P, 2, 512], F32))
        psY, psR, psP, psX = (k.ps("iv_ps" + n, ctx) for n in "YRPX")
        psS = [k.ps(f"iv_psS{u}", ctx) for u in range(2)]
        block = ctx.enter_context(nc.Block())
        out_v = OUT.rearrange("b c (j p i r) w -> b j p i c (r w)", j=2, p=2, i=2 * ITERS)

        def rt_bank(j):
            return (psP[:, :], psX[:, :], psL[:, 0, :], psL[:, 1, :])[j % 4]

        def copy_rt(copy, j, u):
            hj, og = j // 4, j % 4
            return copy(rt[HID * hj:HID * hj + HID, 8 * og + u:8 * og + u + 7:2, :],
                        rt_bank(j)[HID * u:HID * u + HID, :].rearrange("q (o h) -> q o h", h=P))

        @block.sync
        def _(sp):
            prime(sp, *S.values())
            for u in range(2):
                sp.sem_inc(out_stored[u], 64)

            def load_modes(b):
                sp.wait_ge(S["cond_done"], done(b - 1))
                sp.wait_ge(S["td_done"], done(2 * b - 1))
                sp.dma_start(xfk[:, :, :, :].rearrange("q a m o -> q (a m o)").rearrange("q (m n) -> q m n", m=8),
                             k.xfd[:, bass.ds(b, 1)].rearrange("m a r k g o -> (a r k) m (g o)")).then_inc(XF_LOADED, 16)

            def store(b):
                with sp.Fori(0, ITERS) as i:
                    for u in range(2):
                        sp.wait_ge(S["out_done"], done(b * NSTEP + i * STEPS + 2 * u + 1))
                        for q in range(4):
                            sp.dma_start(out_v[bass.ds(b, 1), q % 2, q // 2, bass.ds(i * 2 + u, 1)]
                                         .rearrange("a e c n -> (a e c) n"), osb[u][32 * q:32 * q + 32, :])\
                              .then_inc(out_stored[u], 16)
            load_modes(0)
            with sp.Fori(0, B - 1) as b:
                load_modes(b + 1)
                store(b)
            store(B - 1)
            for u in range(2):
                sp.wait_ge(out_stored[u], B * ITERS * 64 + 64)

        @block.tensor
        def _(pe):
            def wcond(b):
                pe.wait_ge(S["cw0_sum"], done(7 * b + 6))
                pe.matmul(psY[0:HID, 0:H], t["wi0"][:, :], cw[0][:, :], start=True, stop=False)
                pe.wait_ge(S["cw1_sum"], done(8 * b + 7))
                pe.matmul(psY[0:HID, 0:H], t["wi0"][:, :], cw[1][:, :], start=False, stop=True)
                pe.wait_ge(S["by_sum"], done(16 * b + 15))
                pe.sem_inc(S["held"], 1)
                pe.matmul(psY[HID:HID + C, 0:H], t["mix_c"][:, :], by[:, :], start=True, stop=True).then_inc(S["aw_done"], 1)

            def image(b):
                for name, lag in (("g2_done", 2), ("yc_done", 3)):
                    pe.wait_ge(S[name], done(b * NSTEP - 1 - lag))
                pe.wait_ge(S["tp_copied"], done(b * ITERS - 1))
                pe.wait_ge(S["aw_copied"], done(b - 1))
                pe.wait_ge(XF_LOADED, (b + 1) * 16)
                pe.sem_inc(S["held"], 1)
                for m in range(M):
                    last = pe.matmul(psX[0:C, 4 * m:4 * m + 4], xfk[:, m // 16, m % 16, :], t["cond_h"][:, :],
                                     start=True, stop=True)
                last.then_inc(S["cond_done"], 1)
                for mj in range(2):
                    pe.matmul(psL[:, mj, :], t["hi2"][:, :, :].rearrange("q r f -> q (r f)"),
                              xfk[:, mj, :, :].rearrange("q m o -> q (m o)"), start=True, stop=True).then_inc(S["td_done"], 1)
                pe.wait_ge(S["cond_copied"], done(b))
                for mj in range(2):
                    for ri in range(2):
                        last = pe.matmul(psY[HID * mj:HID * mj + HID, 0:16], t["hi0"][:, ri, :], ch[:, ri, mj, :],
                                         start=ri == 0, stop=ri == 1)
                last.then_inc(S["ah_done"], 1)
                pe.wait_ge(S["td_copied"], done(2 * b + 1))

                def hidden(j):
                    pe.wait_ge(S["hg0_done"], done(8 * b + j))
                    pe.wait_ge(S["hg1_done"], done(8 * b + j - 2))
                    pe.matmul(psL[:, j % 2, :], t["hi1"][:, :], ha[:, 2 * j:2 * j + 2, :].rearrange("q a h -> q (a h)"),
                              start=True, stop=True).then_inc(S["hl1_done"], 1)
                hidden(0)
                hidden(1)
                for j in range(8):
                    if j + 2 < 8:
                        hidden(j + 2)
                    pe.wait_ge(S["hg1_done"], done(8 * b + j))
                    pe.wait_ge(S["r_copied"], done(8 * b + j - 2))
                    for u in range(2):
                        last = pe.matmul((psP, psX)[j % 2][:, u * H:u * H + H], td[:, 2 * j + u, :, :, :].rearrange("q a r o -> q (a r o)"),
                                         hb[:, 2 * j + u, :], start=True, stop=True)
                    last.then_inc(S["r_done"], 1)
                for j in range(8):
                    if j == 7:
                        wcond(b)
                    hj, mg = j // 4, j % 4
                    pe.wait_ge(S["r_copied"], done(8 * b + 2 * mg + 1))
                    pe.wait_ge(S["rh_copied"], done(8 * b + j - 2))
                    for a in range(4):
                        mp = 4 * mg + a
                        last = pe.matmul(psL[:, j % 2, a * P:a * P + P], R[:, mp, hj * P:hj * P + P], t["mix_bd"][:, :],
                                         start=True, stop=True)
                    last.then_inc(S["rh_done"], 1)
                pe.wait_ge(S["aw_copied"], done(b))
                pe.sem_inc(S["held"], 1)
                pe.transpose(psY[0:HP, 0:P], yb[:, :], t["ident"][:, :]).then_inc(S["yt_done"], 1)
                for j in range(8):
                    hj, og = j // 4, j % 4
                    pe.wait_ge(S["rh_copied"], done(8 * b + 7))
                    pe.wait_ge(S["rt_copied"], done(8 * b + j - 4))
                    pe.wait_ge(S["rt_half_copied"], done(8 * b + j - 4))
                    for a in range(4):
                        o = 8 * og + 2 * a
                        last = pe.transpose(rt_bank(j)[:, a * P:a * P + P],
                                            rh[:, hj, o:o + 2, :].rearrange("q o j -> q (o j)"), t["ident"][:, :])
                    last.then_inc(S["rt_done"], 1)
                pe.wait_ge(S["rt_copied"], done(8 * b + 7))
                pe.wait_ge(S["rt_half_copied"], done(8 * b + 7))
                pe.wait_ge(S["yt_copied"], done(b))

            def step(st):
                if st.live(7):
                    n, u = st.n(7), st.slot(7, 2)
                    pe.wait_ge(S["yn_done"], done(n))
                    pe.wait_ge(S["gy_done"], done(n - 1))
                    for g in range(2):
                        for r in range(ROWS):
                            o = (g * ROWS + r) * P
                            last = pe.transpose(psR[:, r * W + g * P:r * W + g * P + P], yn[u][:, o:o + P], t["ident"][:, :])
                    last.then_inc(S["tr_done"], 1)
                if st.live(2):
                    n, u = st.n(2), st.slot(2, 2)
                    pe.wait_ge(S["g1_done"], done(n))
                    pe.wait_ge(S["g2_done"], done(n - 1))
                    for p in range(2):
                        last = pe.matmul(psL[:, p, :], t["wi1"][:, :], wg1[u][:, p, :, :].rearrange("q r w -> q (r w)"),
                                         start=True, stop=True)
                    last.then_inc(S["l1_done"], 1)
                if st.live(3):
                    n, u, c = st.n(3), st.slot(3, 2), st.slot(3, 4)
                    pe.wait_ge(S["g2_done"], done(n))
                    pe.wait_ge(S["yc_done"], done(n - 1))
                    pe.wait_ge(S["tp_copied"], done(st.it(3)))
                    for g in range(2):
                        for r in range(ROWS):
                            for p in range(2):
                                o = (2 * (g * ROWS + r) + p) * HID
                                last = pe.matmul(psY[:, o:o + HID], wg2[u][:, p, r, g * P:g * P + P],
                                                 tp[:, ROWS * c + r, p, :, :].rearrange("q j o -> q (j o)"), start=True, stop=True)
                    last.then_inc(S["y_done"], 1)
                if st.s == 2 and st.live(2):
                    pe.wait_ge(S["tp_copied"], done(st.it(2) - 1))
                    h0 = st.row(2)
                    w = rt[:, :, :].rearrange("q o (p h) -> q h p o", p=2)
                    w = w[:, bass.ds(h0, 8)] if not isinstance(h0, int) else w[:, h0:h0 + 8]
                    pe.matmul(psP[:, :].rearrange("q (h p o) -> q h p o", h=8, p=2), t["wi2"][:, :], w,
                              start=True, stop=True).then_inc(S["tp_done"], 1)
                if st.live(7):
                    n, c = st.n(7), st.slot(7, 4)
                    if c % 2 == 0:
                        pe.wait_ge(xn_loaded[c // 2], (st.it(7) + 1) * 16)
                    pe.wait_ge(S["t_done"], done(n - 2))
                    pe.matmul(psS[c % 2][:, :], t["sc"][:, :], xn[c // 2][:, (c % 2) * N:(c % 2) * N + N],
                              start=True, stop=True).then_inc(S["sc_done"], 1)

            all_steps(pe, B, image, step, 8)

        @block.scalar
        def _(act):
            def image(b):
                act.wait_ge(S["ah_copied"], done(b))
                act.wait_ge(S["rt_done"], done(8 * b - 1))
                act.wait_ge(S["r_done"], done(8 * b - 1))

                def first(j):
                    for mp in (2 * j, 2 * j + 1):
                        last = act.activation(ha[:, mp, :], t["hc_row"][:, :], ACT.Gelu, scale=t["hi0_c"][:, :], bias=ah[:, mp:mp + 1])
                    last.then_inc(S["hg0_done"], 1)
                first(0)
                first(1)
                for j in range(8):
                    if j + 2 < 8:
                        first(j + 2)
                    act.wait_ge(S["hl1_done"], done(8 * b + j))
                    act.activation(hb[:, 2 * j:2 * j + 2, :].rearrange("q a h -> q (a h)"), psL[:, j % 2, :],
                                   ACT.Gelu, bias=t["hi1_b"][:, :]).then_inc(S["hg1_done"], 1)
                for j in range(8):
                    hj, mg = j // 4, j % 4
                    act.wait_ge(S["rh_done"], done(8 * b + j))
                    act.wait_ge(S["hl1_done"], done(8 * b + 7))
                    act.copy(rh[:, hj, :, 16 * mg:16 * mg + 16].rearrange("q o c -> q c o"),
                             psL[:, j % 2, :].rearrange("q (c o) -> q c o", o=C)).then_inc(S["rh_copied"], 1)
                act.wait_ge(S["yt_copied"], done(b))
                act.dma_start(k.ybd[bass.ds(b * (2 * ITERS), 2 * ITERS)].rearrange("a (h c) -> (a h) c", h=CHUNK), ybt[:, :])\
                   .then_inc(yb_stored, 16)
                act.wait_ge(S["tp_done"], done(b * ITERS - 1))
                for j in range(8):
                    act.wait_ge(S["rt_done"], done(8 * b + j))
                    copy_rt(act.copy, j, 1).then_inc(S["rt_half_copied"], 1)

            def step(st):
                if st.live(1):
                    n, u = st.n(1), st.slot(1, 2)
                    act.wait_ge(S["pre_done"], done(n))
                    act.wait_ge(S["l1_done"], done(n - 2))
                    act.activation(wg1[u][:, :, :, :].rearrange("q p r w -> q (p r w)"),
                                   pre[u][:, :, :, :].rearrange("q p r w -> q (p r w)"), ACT.Gelu).then_inc(S["g1_done"], 1)
                if st.live(7):
                    n, u = st.n(7), st.slot(7, 2)
                    act.wait_ge(S["tr_done"], done(n))
                    act.wait_ge(S["t_done"], done(n - 2))
                    act.activation(gy[u][:, :], psR[:, :], ACT.Gelu, scale=t["ln_g"][:, :], bias=t["ln_b"][:, :])\
                       .then_inc(S["gy_done"], 1)
                if st.live(9):
                    n, u = st.n(9), st.slot(9, 2)
                    act.wait_ge(S["t_done"], done(n))
                    act.wait_ge(S["out_done"], done(n - 2))
                    act.activation(gs[u][:, :], tt[u][:, :], ACT.Gelu, bias=t["sc_b"][:, :]).then_inc(S["gs_done"], 1)
                if st.live(2):
                    n, u = st.n(2), st.slot(2, 2)
                    act.wait_ge(S["l1_done"], done(n))
                    act.wait_ge(S["y_done"], done(n - 2))
                    act.activation(wg2[u][:, :, :, :].rearrange("q p r w -> q (p r w)"),
                                   psL[:, :, :].rearrange("q p n -> q (p n)"), ACT.Gelu, bias=t["wi1_b"][:, :]).then_inc(S["g2_done"], 1)
                if st.s % 2 == 1 and st.live(5):
                    u = st.slot(5, 4) // 2
                    act.wait_ge(S["sc_done"], done(st.n(8)))
                    act.wait_ge(S["res_done"], done(st.n(8)))
                    act.dma_start(xn[u][:, :], k.xnd[bass.ds(st.b * (2 * ITERS) + 2 * st.i + (st.s - 5) // 2, 1)]
                                  .rearrange("a p n -> (a p) n")).then_inc(xn_loaded[u], 16)
                if st.s % 2 == 1 and st.live(1):
                    u = st.slot(1, 4) // 2
                    if st.opens_image(1):
                        act.wait_ge(yb_stored, (st.b + 1) * 16)
                    act.wait_ge(S["yc_done"], done(st.n(4)))
                    act.dma_start(ybb[u][:, :, :].rearrange("q h c -> q (h c)"),
                                  k.ybd[bass.ds(st.b * (2 * ITERS) + 2 * st.i + st.s // 2, 1)].broadcast_to([P, CHUNK * P]))\
                       .then_inc(yb_loaded[u], 16)

            all_steps(act, B, image, step, 10)

        @block.vector
        def _(v):
            def add_mode(b, total, mp, first, weights, summed, count):
                if mp != first:
                    v.wait_ge(summed, count + PRIME)
                w = weights[:, mp:mp + 1]
                if mp == first:
                    v.sem_inc(S["held"], 1)
                    ins = v.tensor_scalar(total[:, :], R[:, mp, :], w, None, ALU.mult)
                else:
                    ins = v.scalar_tensor_tensor(total[:, :], R[:, mp, :], w, total[:, :], ALU.mult, ALU.add)
                ins.then_inc(summed, 1)

            def add_pair(b, j):
                v.wait_ge(S["aw_done"], done(b - 1))
                v.wait_ge(S["r_copied"], done(8 * b + j))
                for mp in (2 * j, 2 * j + 1):
                    add_mode(b, by, mp, 0, t["wi2_b"], S["by_sum"], 16 * b + mp)

            def image(b):
                v.wait_ge(S["cond_done"], done(b))
                c_ps = psX[0:C, 0:P].rearrange("q (a m f) -> q f a m", a=2, f=4)
                v.wait_ge(S["ah_done"], done(b - 1))
                v.tensor_scalar(ch[:, :, :, :].rearrange("q r a m -> q r (a m)"),
                                psX[0:C, 0:P].rearrange("q (m f) -> q f m", f=4)[:, 0:2, :], t["comp_h_b"][:, :], None, ALU.add)
                v.wait_ge(S["r_copied"], done(8 * b - 1))
                for mj in range(2):
                    for ri in range(2):
                        q = 2 * mj + ri
                        last = v.tensor_copy(tb_row[C * q:C * q + C, :], c_ps[:, 2 + ri, mj, :])
                last.then_inc(S["cond_copied"], 1)
                v.wait_ge(S["r_done"], done(8 * b - 1))
                for mj in range(2):
                    v.wait_ge(S["td_done"], done(2 * b + mj))
                    for ri in range(2):
                        last = v.tensor_copy(td[HID * mj:HID * mj + HID, :, mj, ri, :],
                                             psL[HID * ri:HID * ri + HID, mj, :].rearrange("q (m o) -> q m o", o=C))
                    last.then_inc(S["td_copied"], 1)
                v.wait_ge(S["ah_done"], done(b))
                v.wait_ge(S["hg0_done"], done(8 * b - 1))
                v.tensor_scalar(ah[:, :], psY[:, 0:16], t["hi0_b"][:, :], None, ALU.add).then_inc(S["ah_copied"], 1)
                v.wait_ge(S["rh_done"], done(8 * b - 1))
                v.wait_ge(S["cond_copied"], done(b))
                for j in range(8):
                    v.wait_ge(S["r_done"], done(8 * b + j))
                    for u in range(2):
                        last = v.tensor_scalar(R[:, 2 * j + u, :], (psP, psX)[j % 2][:, u * H:u * H + H],
                                               tb_row[:, 2 * j + u:2 * j + u + 1], None, ALU.add)
                    last.then_inc(S["r_copied"], 1)
                    if j >= 1:
                        add_pair(b, j - 1)
                add_pair(b, 7)
                for mp in range(8, 16):
                    add_mode(b, cw[1], mp, 8, t["comp_w"], S["cw1_sum"], 8 * b + mp - 8)
                v.wait_ge(S["aw_done"], done(b))
                v.wait_ge(S["pre_done"], done(b * NSTEP - 1))
                v.wait_ge(S["yt_done"], done(b - 1))
                for hj in range(2):
                    v.tensor_scalar(aw[HID * hj:HID * hj + HID, :], psY[0:HID, hj * P:hj * P + P], wi0_const, None, ALU.add)
                for q in range(4):
                    h0 = (q % 2) * P + (q // 2) * HP
                    last = v.tensor_scalar(yb[C * q:C * q + C, :], psY[HID:HID + C, h0:h0 + HP], y_const, None, ALU.add)
                last.then_inc(S["aw_copied"], 1)
                v.wait_ge(yb_stored, b * 16)
                v.wait_ge(S["yt_done"], done(b))
                v.tensor_copy(ybt[:, :], psY[0:HP, 0:P]).then_inc(S["yt_copied"], 1)
                v.wait_ge(S["tp_done"], done(b * ITERS - 1))
                for j in range(8):
                    v.wait_ge(S["rt_done"], done(8 * b + j))
                    copy_rt(v.tensor_copy, j, 0).then_inc(S["rt_copied"], 1)

            wi0_const, y_const = t["wi0_const"][0:HID, :], t["y_const"][HID:HID + C, :]

            def newton(y):
                ops = [lambda: v.tensor_scalar(xv[:, :], vs[:, :], 1.0 / C, 1e-5, ALU.mult, ALU.add),
                       lambda: v.tensor_scalar(y.bitcast(I32), xv[:, :].bitcast(I32), -0.5, MAGIC, ALU.mult, ALU.add),
                       lambda: v.tensor_scalar(xh[:, :], xv[:, :], -0.5, None, ALU.mult)]
                for _ in range(3):
                    ops += [lambda: v.tensor_tensor(nt[:, :], y, y, ALU.mult),
                            lambda: v.tensor_tensor(nt[:, :], nt[:, :], xh[:, :], ALU.mult),
                            lambda: v.scalar_tensor_tensor(y, nt[:, :], 1.5, y, ALU.add, ALU.mult)]
                return ops

            NEWTON, HALF = 12, 6

            def newton_part(pair, y, first, end):
                for j, op in enumerate(newton(y)[first:end], first):
                    if j:
                        v.wait_ge(S["newton"], pair * (NEWTON - 1) + j + PRIME)
                    op().then_inc(S["newton"] if j < NEWTON - 1 else S["rs_done"], 1)

            def step(st):
                if st.opens_image(7):
                    v.wait_ge(S["res_done"], done(st.n(8)))
                    v.tensor_copy(ivm[:, 0:1], t["invs"][:, bass.ds(st.b, 1)])
                    v.tensor_copy(ivm[:, 1:2], t["mean1"][:, bass.ds(st.b, 1)]).then_inc(S["ivm_set"], 1)
                if st.s == 3 and st.live(3):
                    v.wait_ge(S["tp_done"], done(st.it(3)))
                    v.wait_ge(S["y_done"], done(st.n(4)))
                    for hj in range(2):
                        r = slice(HID * hj, HID * hj + HID)
                        last = v.tensor_copy(tp[r, :, :, hj, :].rearrange("q h p o -> q (h p) o"),
                                             psP[r, :].rearrange("q (a o) -> q a o", o=C))
                    last.then_inc(S["tp_copied"], 1)
                if st.s % 2 == 0 and st.live(6):
                    newton_part(st.pair(6), rs[st.slot(6, 4) // 2][:, :], HALF, NEWTON)
                if st.live(6):
                    n, c, u = st.n(6), st.slot(6, 4), st.slot(6, 2)
                    v.wait_ge(S["rs_done"], done(st.pair(6)))
                    v.wait_ge(S["tr_done"], done(n - 2))
                    v.wait_ge(S["yc_done"], done(n))
                    v.tensor_tensor(yn[u][:, :].rearrange("q (a o) -> q a o", o=C), yc[c][:, :].rearrange("q (a o) -> q a o", o=C),
                                    rs[c // 2][:, 16 * u:16 * u + 16].unsqueeze(2).broadcast_to([P, 16, C]), ALU.mult)\
                     .then_inc(S["yn_done"], 1)
                if st.live(8):
                    n, u = st.n(8), st.slot(8, 2)
                    v.wait_ge(S["gy_done"], done(n))
                    v.wait_ge(S["sc_done"], done(n))
                    v.wait_ge(S["gs_done"], done(n - 2))
                    v.tensor_tensor(tt[u][:, :], gy[u][:, :], psS[u][:, :], ALU.add).then_inc(S["t_done"], 1)
                if st.live(4):
                    n, u = st.n(4), st.slot(4, 2)
                    v.wait_ge(S["sq_done"], done(n))
                    if u == 0:
                        v.wait_ge(S["rs_done"], done(st.pair(4) - 1))
                    v.reduce_sum(vs[:, 16 * u:16 * u + 16], sq[u][:, :].rearrange("q (a o) -> q a o", o=C), axis=AX.X)\
                     .then_inc(S["sum_done"], 1)
                if st.live(3):
                    n, c = st.n(3), st.slot(3, 4)
                    v.wait_ge(S["y_done"], done(n))
                    v.wait_ge(S["yn_done"], done(n - 4))
                    v.wait_ge(S["sq_done"], done(n - 4))
                    if c % 2 == 0:
                        v.wait_ge(yb_loaded[c // 2], (st.it(3) + 1) * 16)
                    bias = ybb[c // 2][:, (c % 2) * ROWS:(c % 2) * ROWS + ROWS, :].rearrange("q r c -> q (r c)")
                    v.tensor_tensor(yc[c][:, :].rearrange("q (g n) -> q g n", g=2), psY[:, :].rearrange("q (g n) -> q g n", g=2),
                                    bias.unsqueeze(1).broadcast_to([P, 2, ROWS * P]), ALU.add).then_inc(S["yc_done"], 1)
                if st.live(10):
                    n, c, u = st.n(10), st.slot(10, 4), st.slot(10, 2)
                    v.wait_ge(S["gs_done"], done(n))
                    v.wait_ge(S["res_done"], done(n))
                    if c % 2 == 0:
                        v.wait_ge(out_stored[c // 2], (st.it(10) + 1) * 64)
                    v.tensor_tensor(osb[c // 2][:, (c % 2) * N:(c % 2) * N + N], res[c][:, :], gs[u][:, :], ALU.add)\
                     .then_inc(S["out_done"], 1)
                if st.s % 2 == 1 and st.live(5):
                    v.wait_ge(S["sum_done"], done(st.n(4)))
                    v.wait_ge(S["yn_done"], done(st.n(8)))
                    v.wait_ge(S["rs_done"], done(st.pair(5) - 1))
                    newton_part(st.pair(5), rs[st.slot(5, 4) // 2][:, :], 0, HALF)

            v.memset(td[:, :, :, :, :], 0.0)
            v.memset(tp[:, :, :, :, :], 0.0)
            v.tensor_scalar(wc_w[:, :], t["wc_row"][:, :], t["wi0_c"][:, :], None, ALU.mult).then_inc(zeroed, 1)
            v.wait_ge(zeroed, 1)
            all_steps(v, B, image, step, 11)

        @block.gpsimd
        def _(g):
            def image(b):
                g.wait_ge(S["aw_done"], done(b - 1))
                for mp in range(8):
                    if mp % 2 == 0:
                        g.wait_ge(S["r_copied"], done(8 * b + mp // 2))
                    w, to = t["comp_w"][:, mp:mp + 1], (cw_term if mp else cw[0])
                    g.sem_inc(S["held"], 1)
                    g.tensor_scalar(to[:, :], R[:, mp, :], w, None, ALU.mult).then_inc(S["cw_term"], 1)
                    g.wait_ge(S["cw_term"], done(8 * b + mp))
                    if mp:
                        g.tensor_tensor(cw[0][:, :], cw[0][:, :], cw_term[:, :], ALU.add).then_inc(S["cw0_sum"], 1)
                        g.wait_ge(S["cw0_sum"], done(7 * b + mp - 1))
                g.wait_ge(S["aw_copied"], done(b))

            def step(st):
                if st.live(7):
                    n, c = st.n(7), st.slot(7, 4)
                    if st.opens_image(7):
                        g.wait_ge(S["ivm_set"], done(st.b))
                    if c % 2 == 0:
                        g.wait_ge(xn_loaded[c // 2], (st.it(7) + 1) * 16)
                    g.wait_ge(S["out_done"], done(n - 4))
                    g.sem_inc(S["held"], 1)
                    g.tensor_scalar(res[c][:, :], xn[c // 2][:, (c % 2) * N:(c % 2) * N + N], ivm[:, 0:1], ivm[:, 1:2],
                                    ALU.mult, ALU.add).then_inc(S["res_done"], 1)
                if st.live(0):
                    n, u = st.n(0), st.slot(0, 2)
                    g.wait_ge(S["g1_done"], done(n - 2))
                    h0 = st.row(0)
                    a = aw[:, :].rearrange("q (p h) -> q p h", p=2)
                    a = a[:, :, bass.ds(h0, ROWS)] if not isinstance(h0, int) else a[:, :, h0:h0 + ROWS]
                    g.tensor_tensor(pre[u][:, :, :, :], wc_w[:, :].unsqueeze(1).unsqueeze(1).broadcast_to([P, 2, ROWS, W]),
                                    a.unsqueeze(3).broadcast_to([P, 2, ROWS, W]), ALU.add).then_inc(S["pre_done"], 1)
                if st.live(3):
                    n, c, u = st.n(3), st.slot(3, 4), st.slot(3, 2)
                    g.wait_ge(S["yc_done"], done(n))
                    g.wait_ge(S["sum_done"], done(n - 2))
                    g.tensor_tensor(sq[u][:, :], yc[c][:, :], yc[c][:, :], ALU.mult).then_inc(S["sq_done"], 1)

            g.wait_ge(zeroed, 1)
            all_steps(g, B, image, step, 8)


def build(nc, a, out):
    with ExitStack() as ctx:
        k = Kit(nc, ctx, a, out)
        B = k.B
        k.zd = nc.dram_tensor("zd", (4, 4, B, 8, 8, M), F32).ap()
        k.vd = nc.dram_tensor("vd", (B, M, HP, P), F32).ap()
        k.xnd = nc.dram_tensor("xnd", (B * 2 * ITERS, P, CHUNK * W), F32).ap()
        k.xfd = nc.dram_tensor("xfd", (8, B, 2, M, 4, C), F32).ap()
        k.ybd = nc.dram_tensor("ybd", (B * 2 * ITERS, CHUNK * P), F32).ap()
        place_tables(k)
        for n in ("mean1", "invs", "s1"):
            k.sb(n, [P, B])
        with ExitStack() as c0:
            k.sb("XM", [P, 3 * 8 * M, B], F32, c0)
            k.sb("MV", [P, B, 16, 2], F32, c0)
            dht(k)
            setup(k)
            mix0(k)
        rows0(k)
        with ExitStack() as c1:
            k.sb("XH", [P, 8 * 2 * M, B], F32, c1)
            forward(k)
            mix1(k)
        inverse(k)


def weight_layouts(w):
    f = np.float32
    t = {n: np.zeros(s, f) for n, s in TABLES.items()}
    n, kk = np.arange(W), np.arange(M)
    ang = 2 * np.pi * ((n[:, None] * kk[None, :]) % W) / W
    cas = (np.cos(ang) + np.sin(ang)).astype(f)
    flip = (-kk) % M
    t["cas_n"][:, :, :M] = cas.reshape(2, P, M).transpose(1, 0, 2)
    t["cas_n"][:, :, 2 * M:] = t["cas_n"][:, :, :M]
    t["cas_n"][:, :, M:2 * M] = cas[:, flip].reshape(2, P, M).transpose(1, 0, 2)
    t["cas_k"][:] = cas.T
    for j in range(4):
        t["cas_bd"][32 * j:32 * j + 32, H * j:H * j + H] = cas.T.reshape(8, 4, H).transpose(1, 0, 2).reshape(M, H)
    t["ident"][:] = np.eye(P, dtype=f)
    c = np.arange(P) % C
    t["chan_mask"][:] = c[:, None] // 2 == np.arange(16)[None, :]
    t["group_avg"][:] = (c[:, None] // 2 == c[None, :] // 2) * f(1 / 8)
    t["ones_avg"][:] = f(1 / P)

    def two(m):
        r, q = m.shape
        z = np.zeros((2 * r, 2 * q), f)
        z[:r, :q] = m
        z[r:, q:] = m
        return z

    for name in ("bw", "bh"):
        for p in range(2):
            for hj in range(2):
                q = 2 * p + hj
                t[name + "0"][32 * q:32 * q + 32, p, HID * hj:HID * hj + HID] = w[name + "0_w"][:C]
    for name in ("bw", "bh", "hi", "wi"):
        t[name + "1"][:] = two(w[name + "1_w"])
        t[name + "0_b"][:, 0] = np.tile(w[name + "0_b"], 2)
    for name in ("bw", "bh"):
        t[name + "0_c"][:, 0] = np.tile(w[name + "0_w"][C], 2)
        t[name + "1_row"][:] = w[name + "1_b"][None, :]
    for name in ("hi", "wi"):
        t[name + "1_b"][:, 0] = np.tile(w[name + "1_b"], 2)
        t[name + "0_c"][:, 0] = np.tile(w[name + "0_w"][0], 2)
    t["bw2"][:] = np.tile(w["bw2_w"], (2, 1))
    t["bw2_b"][:] = w["bw2_b"][None, :]
    bh2 = np.concatenate([w["bh2_w"], w["bh2_b"][None, :]], 0)
    t["bh2"][:, 0] = bh2
    t["bh2"][:, 1] = np.concatenate([bh2[:, M:], bh2[:, :M]], 1)
    ch, b2 = w["comp_h_w"], w["hi2_b"]
    t["cond_h"][:M, 0] = ch
    t["cond_h"][M:, 1] = ch
    t["cond_h"][:, 2] = b2
    t["cond_h"][:M, 3] = b2[M:]
    t["cond_h"][M:, 3] = b2[:M]
    t["comp_h_b"][:] = w["comp_h_b"][None, :]
    t["hi0"][:] = w["hi0_w"][1:].reshape(2, C, HID).transpose(1, 0, 2)
    hc = np.linspace(-1.0, 1.0, H, dtype=f)
    t["hc_row"][:] = hc[None, :]
    t["hc_rows"][:] = np.repeat(hc.reshape(2, 2, HP), HID, 0)
    t["wc_row"][:] = hc[None, :]
    t["hi2"][:, 0] = w["hi2_w"].T
    t["hi2"][:M, 1] = w["hi2_w"].T[M:]
    t["hi2"][M:, 1] = w["hi2_w"].T[:M]
    t["wi0"][:] = np.tile(w["wi0_w"][1:], (2, 1))
    t["wi0_sum"][:] = np.tile(w["wi0_w"][1:], (1, 2))
    t["comp_w_b"][:] = w["comp_w_b"][None, :]
    place = np.array([[(mp % 4) * 8 + mj * 4 + mp // 4 for mp in range(16)] for mj in range(2)])
    t["comp_w"][:] = np.repeat(w["comp_w_w"][place], HID, 0)
    t["mixer"][:] = np.tile(w["mixer_w"].T, (4, 1))
    t["mixer_b"][:] = w["mixer_b"][None, :]
    t["mixer_own"][:, 0] = np.tile(w["mixer_b"], 4)
    b2 = w["wi2_b"].reshape(2, M)[:, place]
    t["wi2_b"][:] = np.repeat(b2.transpose(1, 0, 2).reshape(4, 16), C, 0)
    w2 = w["wi2_w"].reshape(HID, 2, M)[:, :, place].transpose(3, 2, 1, 0).reshape(HID, HID)
    t["wi2"][:] = two(w2)
    t["sc"][:] = two(two(w["sc_w"].T))
    for name, src in (("sc_b", "sc_b"), ("ln_g", "ln_g"), ("ln_b", "ln_b")):
        t[name][:, 0] = np.tile(w[src], 4)
    w0 = w["l0"]
    both = np.stack([w0, w0[:, :, flip][:, :, :, flip]], 0)
    t["l0_w"] = both.reshape(2, C, C, 8, 4, M).transpose(3, 4, 1, 0, 5, 2).reshape(8, P, 2, M, C)
    wf = np.stack([w["wf_real"], w["wf_imag"]], 0).reshape(2, C, C, M, 4, 8)
    t["l1_w"] = wf.transpose(5, 4, 2, 3, 0, 1).reshape(8, P, M, 2, C)
    return {n: np.ascontiguousarray(v, dtype=f) for n, v in t.items()}


def kernel(**inputs):
    import concourse.bacc as bacc
    from concourse.bass_utils import run_bass_kernel_spmd as run

    w = {n[len("L1_conv_"):]: np.asarray(v) for n, v in inputs.items() if n.startswith("L1_conv_")}
    w["l0"] = np.asarray(inputs["L0_conv_weights1"])
    arrays = weight_layouts(w)
    arrays["x"] = np.asarray(inputs["x"])
    nc = bacc.Bacc("TRN2", target_bir_lowering=False, num_devices=1)
    a = {n: nc.dram_tensor("in_" + n, v.shape, mybir.dt.from_np(v.dtype), kind="ExternalInput").ap()
         for n, v in arrays.items()}
    out = nc.dram_tensor("out", arrays["x"].shape, F32, kind="ExternalOutput").ap()
    build(nc, a, out)
    r = run(nc, [{"in_" + n: v for n, v in arrays.items()}], core_ids=[0])
    return r.results[0]["out"]
```
